# Optimizing a Trainium2 kernel written in Bass

```python
import numpy as np
import jax
import jax.numpy as jnp

def _softmax(x, axis=-1):
    return jax.nn.softmax(x, axis=axis)

def _gelu(x):
    return jax.nn.gelu(x, approximate=True)

def _silu(x):
    return jax.nn.silu(x)

def _sigmoid(x):
    return jax.nn.sigmoid(x)

def _layernorm(x, axis=-1, eps=1e-05):
    m = jnp.mean(x, axis=axis, keepdims=True)
    v = jnp.var(x, axis=axis, keepdims=True)
    return (x - m) / jnp.sqrt(v + eps)

def _scatter_add(tgt, idx, src, axis=0):
    return tgt.at[idx].add(src)

def _segment_sum(src, seg, n):
    return jax.ops.segment_sum(src, seg, n)
kernel_name = 'mk_vit_tower_d2_tok_img768_r4_514183'

def setup_inputs(seed: int=0):
    np.random.seed(seed)
    _w = jnp.asarray

    def _rec_inputs():
        import jax
        import jax.numpy as jnp
        _rk = jax.random.key(seed)
        x = -0.00016672 + 0.999947 * jax.random.normal(jax.random.fold_in(_rk, 1), (16, 3, 96, 96), jnp.float32)
        return x
    x = _rec_inputs()

    def _L0_tok_setup():
        import jax, jax.numpy as jnp
        import numpy as np
        PH = PW = 16
        C, H, W = (3, 96, 96)
        EMBED = 192
        PATCH_DIM = C * PH * PW
        key = jax.random.key(seed)
        k1, k2, k3 = jax.random.split(key, 3)
        x = jax.random.normal(k1, (64, C, H, W), dtype=jnp.float32)
        bound = 1.0 / np.sqrt(PATCH_DIM)
        W_proj = jax.random.uniform(k2, (EMBED, PATCH_DIM), minval=-bound, maxval=bound, dtype=jnp.float32)
        b_proj = jax.random.uniform(k3, (EMBED,), minval=-bound, maxval=bound, dtype=jnp.float32)
        return {'x': x, 'W_proj': W_proj, 'b_projb'[:6]: b_proj}
    _L0_tok_all = _L0_tok_setup()
    _L0_tok_in = {k: v for k, v in _L0_tok_all.items() if k in ('W_proj', 'b_proj')}
    del _L0_tok_all

    def _L0_attn_setup():
        import jax, jax.numpy as jnp
        import numpy as np
        EMBED = 192
        HEADS = 12
        HEAD_DIM = EMBED // HEADS
        LN_EPS = 1e-05
        key = jax.random.key(seed)
        k1, k2, k3 = jax.random.split(key, 3)
        B, T = (2, 1024)
        x = jax.random.normal(k1, (B, T, EMBED), dtype=jnp.float32)
        w_qkv = jax.random.normal(k2, (EMBED, 3 * EMBED), dtype=jnp.float32) * EMBED ** (-0.5)
        w_out = jax.random.normal(k3, (EMBED, EMBED), dtype=jnp.float32) * EMBED ** (-0.5)
        b_out = jnp.zeros((EMBED,), dtype=jnp.float32)
        ln_g = jnp.ones((EMBED,), dtype=jnp.float32)
        ln_b = jnp.zeros((EMBED,), dtype=jnp.float32)
        return {'x': x, 'w_qkv': w_qkv, 'w_out': w_out, 'b_out': b_out, 'ln_g': ln_g, 'ln_b': ln_b}
    _L0_attn_all = _L0_attn_setup()
    _L0_attn_in = {k: v for k, v in _L0_attn_all.items() if k in ('w_qkv', 'w_out', 'b_out', 'ln_g', 'ln_b')}
    del _L0_attn_all

    def _L0_ffn_setup():
        import jax, jax.numpy as jnp
        import numpy as np
        B, M, D = (32, 196, 192)
        N, P, H = (64, 1, 768)
        EPS = 1e-12

        def _l2norm(v, axis):
            n = jnp.sqrt(jnp.sum(v * v, axis=axis, keepdims=True))
            return v / jnp.maximum(n, EPS)
        key = jax.random.key(seed)
        ks = jax.random.split(key, 7)
        x = jax.random.normal(ks[0], (B, M, D), dtype=jnp.float32)
        phi = jax.random.normal(ks[1], (D, N, P), dtype=jnp.float32) * (1.0 / D ** 0.5)
        scale = jnp.ones((1,), dtype=jnp.float32)
        w1 = jax.random.normal(ks[2], (N, D, H), dtype=jnp.float32) * (1.0 / D ** 0.5)
        b1 = jnp.zeros((N, H), dtype=jnp.float32)
        w2 = jax.random.normal(ks[3], (N, H, D), dtype=jnp.float32) * (1.0 / H ** 0.5)
        b2 = jnp.zeros((N, D), dtype=jnp.float32)
        return {'x': x, 'phi': phi, 'scale': scale, 'w1': w1, 'b1': b1, 'w2': w2, 'b2': b2}
    _L0_ffn_all = _L0_ffn_setup()
    _L0_ffn_in = {k: v for k, v in _L0_ffn_all.items() if k in ('phi', 'scale', 'w1', 'b1', 'w2', 'b2')}
    del _L0_ffn_all

    def _L1_attn_setup():
        import jax, jax.numpy as jnp
        import numpy as np
        B_, L_, D_ = (4, 512, 192)
        EXP, NST, K = (2, 16, 4)
        DIN = EXP * D_
        D2 = DIN // 2
        DTR = int(np.ceil(D_ / 16))

        def dwconv_same(x, w):
            total = K - 1
            left = total // 2
            return jax.lax.conv_general_dilated(x, w, window_strides=(1,), padding=[(left, total - left)], feature_group_count=x.shape[1], dimension_numbers=('NCH', 'OIH', 'NCH'))
        key = jax.random.key(seed)
        ks = jax.random.split(key, 9)
        sc = lambda k, sh, s=0.02: jax.random.normal(k, sh, jnp.float32) * s
        hidden_states = jax.random.normal(ks[0], (B_, L_, D_), jnp.float32)
        in_proj_w = sc(ks[1], (DIN, D_))
        x_proj_w = sc(ks[2], (DTR + 2 * NST, D2))
        dt_proj_w = sc(ks[3], (D2, DTR), DTR ** (-0.5))
        dt_proj_b = jax.random.uniform(ks[4], (D2,), jnp.float32, -6.0, -2.0)
        A_log = jnp.log(jnp.broadcast_to(jnp.arange(1, NST + 1, dtype=jnp.float32), (D2, NST)))
        D_param = jnp.ones((D2,), jnp.float32)
        out_proj_w = sc(ks[5], (D_, DIN))
        conv_x_w = sc(ks[6], (D2, 1, K), 0.1)
        conv_z_w = sc(ks[7], (D2, 1, K), 0.1)
        return dict(hidden_states=hidden_states, in_proj_w=in_proj_w, x_proj_w=x_proj_w, dt_proj_w=dt_proj_w, dt_proj_b=dt_proj_b, A_log=A_log, D_param=D_param, out_proj_w=out_proj_w, conv_x_w=conv_x_w, conv_z_w=conv_z_w)
    _L1_attn_all = _L1_attn_setup()
    _L1_attn_in = {k: v for k, v in _L1_attn_all.items() if k in ('in_proj_w', 'x_proj_w', 'dt_proj_w', 'dt_proj_b', 'A_log', 'D_param', 'out_proj_w', 'conv_x_w', 'conv_z_w')}
    del _L1_attn_all

    def _L1_ffn_setup():
        import jax, jax.numpy as jnp
        import numpy as np
        D_MODEL, D_FF, N_EXPERTS, TOP_K = (192, 768, 8, 2)
        B, S = (2, 256)
        LN_EPS = 1e-05

        def _layernorm(x, gamma, beta):
            mu = jnp.mean(x, axis=-1, keepdims=True)
            var = jnp.mean(jnp.square(x - mu), axis=-1, keepdims=True)
            return (x - mu) * jax.lax.rsqrt(var + LN_EPS) * gamma + beta
        key = jax.random.key(seed)
        k1, k2, k3, k4 = jax.random.split(key, 4)
        return {'hidden_states': jax.random.normal(k1, (B, S, D_MODEL), dtype=jnp.float32), 'ln_gamma': jnp.ones((D_MODEL,), dtype=jnp.float32), 'ln_beta': jnp.zeros((D_MODEL,), dtype=jnp.float32), 'router_w': jax.random.normal(k2, (D_MODEL, N_EXPERTS), dtype=jnp.float32) * 0.02, 'w1': jax.random.normal(k3, (N_EXPERTS, D_MODEL, D_FF), dtype=jnp.float32) * 0.02, 'w2': jax.random.normal(k4, (N_EXPERTS, D_FF, D_MODEL), dtype=jnp.float32) * 0.02}
    _L1_ffn_all = _L1_ffn_setup()
    _L1_ffn_in = {k: v for k, v in _L1_ffn_all.items() if k in ('ln_gamma', 'ln_beta', 'router_w', 'w1', 'w2')}
    del _L1_ffn_all
    return {'x': x, 'L0_tok_W_proj': _L0_tok_in['W_proj'], 'L0_tok_b_proj': _L0_tok_in['b_proj'], 'L0_attn_w_qkv': _L0_attn_in['w_qkv'], 'L0_attn_w_out': _L0_attn_in['w_out'], 'L0_attn_b_out': _L0_attn_in['b_out'], 'L0_attn_ln_g': _L0_attn_in['ln_g'], 'L0_attn_ln_b': _L0_attn_in['ln_b'], 'L0_ffn_phi': _L0_ffn_in['phi'], 'L0_ffn_scale': _L0_ffn_in['scale'], 'L0_ffn_w1': _L0_ffn_in['w1'], 'L0_ffn_b1': _L0_ffn_in['b1'], 'L0_ffn_w2': _L0_ffn_in['w2'], 'L0_ffn_b2': _L0_ffn_in['b2'], 'L1_attn_in_proj_w': _L1_attn_in['in_proj_w'], 'L1_attn_x_proj_w': _L1_attn_in['x_proj_w'], 'L1_attn_dt_proj_w': _L1_attn_in['dt_proj_w'], 'L1_attn_dt_proj_b': _L1_attn_in['dt_proj_b'], 'L1_attn_A_log': _L1_attn_in['A_log'], 'L1_attn_D_param': _L1_attn_in['D_param'], 'L1_attn_out_proj_w': _L1_attn_in['out_proj_w'], 'L1_attn_conv_x_w': _L1_attn_in['conv_x_w'], 'L1_attn_conv_z_w': _L1_attn_in['conv_z_w'], 'L1_ffn_ln_gamma': _L1_ffn_in['ln_gamma'], 'L1_ffn_ln_beta': _L1_ffn_in['ln_beta'], 'L1_ffn_router_w': _L1_ffn_in['router_w'], 'L1_ffn_w1': _L1_ffn_in['w1'], 'L1_ffn_w2': _L1_ffn_in['w2']}

def reference(x, L0_tok_W_proj, L0_tok_b_proj, L0_attn_w_qkv, L0_attn_w_out, L0_attn_b_out, L0_attn_ln_g, L0_attn_ln_b, L0_ffn_phi, L0_ffn_scale, L0_ffn_w1, L0_ffn_b1, L0_ffn_w2, L0_ffn_b2, L1_attn_in_proj_w, L1_attn_x_proj_w, L1_attn_dt_proj_w, L1_attn_dt_proj_b, L1_attn_A_log, L1_attn_D_param, L1_attn_out_proj_w, L1_attn_conv_x_w, L1_attn_conv_z_w, L1_ffn_ln_gamma, L1_ffn_ln_beta, L1_ffn_router_w, L1_ffn_w1, L1_ffn_w2):
    import jax
    import jax.numpy as jnp

    def _L0_tok_ref(x, W_proj, b_proj):
        import jax, jax.numpy as jnp
        import numpy as np
        PH = PW = 16
        C, H, W = (3, 96, 96)
        EMBED = 192
        PATCH_DIM = C * PH * PW
        B = x.shape[0]
        Hn, Wn = (H // PH, W // PW)
        patches = x.reshape(B, C, Hn, PH, Wn, PW).transpose(0, 2, 4, 1, 3, 5)
        patches = patches.reshape(B, Hn * Wn, PATCH_DIM)
        return jnp.einsum('bnd,ed->bne', patches, W_proj) + b_proj

    def _L0_attn_ref(x, w_qkv, w_out, b_out, ln_g, ln_b):
        import jax, jax.numpy as jnp
        import numpy as np
        EMBED = 192
        HEADS = 12
        HEAD_DIM = EMBED // HEADS
        LN_EPS = 1e-05
        B, T, E = x.shape
        qkv = jnp.einsum('bte,ef->btf', x, w_qkv)
        q, k, v = jnp.split(qkv, 3, axis=-1)

        def split_heads(t):
            return t.reshape(B, T, HEADS, HEAD_DIM).transpose(0, 2, 1, 3)
        q, k, v = map(split_heads, (q, k, v))
        scores = jnp.einsum('bhtd,bhsd->bhts', q, k) / jnp.sqrt(jnp.float32(HEAD_DIM))
        attn = jax.nn.softmax(scores, axis=-1)
        out = jnp.einsum('bhts,bhsd->bhtd', attn, v)
        out = out.transpose(0, 2, 1, 3).reshape(B, T, E)
        y = jnp.einsum('bte,ef->btf', out, w_out) + b_out
        mu = jnp.mean(y, axis=-1, keepdims=True)
        var = jnp.var(y, axis=-1, keepdims=True)
        y = (y - mu) * jax.lax.rsqrt(var + LN_EPS) * ln_g + ln_b
        return y

    def _L0_ffn_ref(x, phi, scale, w1, b1, w2, b2):
        import jax, jax.numpy as jnp
        import numpy as np
        B, M, D = (32, 196, 192)
        N, P, H = (64, 1, 768)
        EPS = 1e-12

        def _l2norm(v, axis):
            n = jnp.sqrt(jnp.sum(v * v, axis=axis, keepdims=True))
            return v / jnp.maximum(n, EPS)
        xn = _l2norm(x, axis=2)
        phin = scale * _l2norm(phi, axis=0)
        logits = jnp.einsum('bmd,dnp->bmnp', xn, phin)
        d = jax.nn.softmax(logits, axis=1)
        b_, m_, n_, p_ = logits.shape
        c = jax.nn.softmax(logits.reshape(b_, m_, n_ * p_), axis=-1).reshape(b_, m_, n_, p_)
        xs = jnp.einsum('bmd,bmnp->bnpd', xn, d)
        h = jax.nn.gelu(jnp.einsum('bnpd,ndh->bnph', xs, w1) + b1[None, :, None, :], approximate=False)
        ys = jnp.einsum('bnph,nhd->bnpd', h, w2) + b2[None, :, None, :]
        y = jnp.einsum('bnpd,bmnp->bmd', ys, c)
        return y

    def _L1_attn_ref(hidden_states, in_proj_w, x_proj_w, dt_proj_w, dt_proj_b, A_log, D_param, out_proj_w, conv_x_w, conv_z_w):
        import jax, jax.numpy as jnp
        import numpy as np
        B_, L_, D_ = (4, 512, 192)
        EXP, NST, K = (2, 16, 4)
        DIN = EXP * D_
        D2 = DIN // 2
        DTR = int(np.ceil(D_ / 16))

        def dwconv_same(x, w):
            total = K - 1
            left = total // 2
            return jax.lax.conv_general_dilated(x, w, window_strides=(1,), padding=[(left, total - left)], feature_group_count=x.shape[1], dimension_numbers=('NCH', 'OIH', 'NCH'))
        B, L, Dm = hidden_states.shape
        xz = (hidden_states @ in_proj_w.T).transpose(0, 2, 1)
        x, z = jnp.split(xz, 2, axis=1)
        x = jax.nn.silu(dwconv_same(x, conv_x_w))
        z = jax.nn.silu(dwconv_same(z, conv_z_w))
        x_dbl = jnp.einsum('bdl,ed->ble', x, x_proj_w)
        dtr, Bm, Cm = jnp.split(x_dbl, [DTR, DTR + NST], axis=-1)
        dt = dtr @ dt_proj_w.T + dt_proj_b
        delta = jax.nn.softplus(dt + dt_proj_b)
        A = -jnp.exp(A_log)
        u = x.transpose(0, 2, 1)
        dA = jnp.exp(delta[..., None] * A)
        dBu = delta[..., None] * Bm[:, :, None, :] * u[..., None]

        def step(h, inp):
            dA_t, dBu_t, C_t = inp
            h = dA_t * h + dBu_t
            return (h, jnp.einsum('bdn,bn->bd', h, C_t))
        h0 = jnp.zeros((B, D2, NST), jnp.float32)
        _, ys = jax.lax.scan(step, h0, (dA.transpose(1, 0, 2, 3), dBu.transpose(1, 0, 2, 3), Cm.transpose(1, 0, 2)))
        y = ys.transpose(1, 0, 2) + u * D_param
        out = jnp.concatenate([y, z.transpose(0, 2, 1)], axis=-1) @ out_proj_w.T
        return out

    def _L1_ffn_ref(hidden_states, ln_gamma, ln_beta, router_w, w1, w2):
        import jax, jax.numpy as jnp
        import numpy as np
        D_MODEL, D_FF, N_EXPERTS, TOP_K = (192, 768, 8, 2)
        B, S = (2, 256)
        LN_EPS = 1e-05

        def _layernorm(x, gamma, beta):
            mu = jnp.mean(x, axis=-1, keepdims=True)
            var = jnp.mean(jnp.square(x - mu), axis=-1, keepdims=True)
            return (x - mu) * jax.lax.rsqrt(var + LN_EPS) * gamma + beta
        Bz, Sz, D = hidden_states.shape
        residual = hidden_states
        x = _layernorm(hidden_states, ln_gamma, ln_beta)
        tokens = x.reshape(-1, D)
        T = tokens.shape[0]
        logits = tokens @ router_w
        probs = jax.nn.softmax(logits, axis=-1)
        topw, topi = jax.lax.top_k(probs, TOP_K)
        topw = topw / jnp.sum(topw, axis=-1, keepdims=True)
        gates = jnp.zeros((T, N_EXPERTS), dtype=tokens.dtype)
        gates = gates.at[jnp.arange(T)[:, None], topi].set(topw)
        h = jnp.einsum('td,edf->etf', tokens, w1)
        h = jax.nn.silu(h)
        y = jnp.einsum('etf,efd->etd', h, w2)
        out = jnp.einsum('te,etd->td', gates, y)
        return residual + out.reshape(Bz, Sz, D)
    h = _L0_tok_ref(x, L0_tok_W_proj, L0_tok_b_proj)
    h = h + _L0_attn_ref(_layernorm(h, axis=-1), L0_attn_w_qkv, L0_attn_w_out, L0_attn_b_out, L0_attn_ln_g, L0_attn_ln_b)
    h = h + _L0_ffn_ref(_layernorm(h, axis=-1), L0_ffn_phi, L0_ffn_scale, L0_ffn_w1, L0_ffn_b1, L0_ffn_w2, L0_ffn_b2)
    h = h + _L1_attn_ref(_layernorm(h, axis=-1), L1_attn_in_proj_w, L1_attn_x_proj_w, L1_attn_dt_proj_w, L1_attn_dt_proj_b, L1_attn_A_log, L1_attn_D_param, L1_attn_out_proj_w, L1_attn_conv_x_w, L1_attn_conv_z_w)
    h = h + _L1_ffn_ref(_layernorm(h, axis=-1), L1_ffn_ln_gamma, L1_ffn_ln_beta, L1_ffn_router_w, L1_ffn_w1, L1_ffn_w2)
    return h

_drawn_inputs = setup_inputs


def setup_inputs(seed=0):
    import zlib

    import numpy as np

    out = dict(_drawn_inputs(seed))
    spreads = {'L0_attn_b_out': (0.0, 0.1),
     'L0_attn_ln_g': (1.0, 0.2),
     'L0_attn_ln_b': (0.0, 0.1),
     'L0_ffn_b1': (0.0, 0.8),
     'L0_ffn_b2': (0.0, 0.756),
     'L1_attn_D_param': (1.0, 0.6),
     'L1_ffn_ln_gamma': (1.0, 0.6),
     'L1_ffn_ln_beta': (0.0, 2.0)}
    factors = {'L0_ffn_phi': 8.0,
     'L0_ffn_w1': 8.0,
     'L0_ffn_w2': 8.0,
     'L1_attn_in_proj_w': 6.009,
     'L1_attn_x_proj_w': 8.0,
     'L1_attn_dt_proj_w': 8.0,
     'L1_attn_dt_proj_b': 8.0,
     'L1_attn_A_log': 8.0,
     'L1_attn_out_proj_w': 5.9,
     'L1_attn_conv_x_w': 7.886,
     'L1_attn_conv_z_w': 200.0,
     'L1_ffn_router_w': 40.794,
     'L1_ffn_w1': 45.889,
     'L1_ffn_w2': 38.325}
    for name, (base, spread) in spreads.items():
        noise = np.random.default_rng([zlib.crc32(name.encode()), seed]).standard_normal(out[name].shape)
        drawn = base * np.exp(spread * noise) if base else spread * noise
        out[name] = jnp.asarray(drawn.astype(out[name].dtype))
    for name, factor in factors.items():
        out[name] = (out[name] * factor).astype(out[name].dtype)
    return out
```

```python
import numpy as np
import concourse.bass as bass
from concourse import mybir
from contextlib import ExitStack

B, L, D = 16, 36, 192
T = B * L
PD = 768
H = D // 2
NH, HD = 12, 16
NE, FF = 64, 768
NS, DTR, TAPS = 16, 12, 4
NX, TOPK = 8, 2
LN_EPS = 1e-5

LOG1P_MAX = 0.125
LOG1P = (0.15590593948099316, -0.2454479896579373, 0.3331359025735257, -0.4999969678046037, 0.9999999925054689)

RSQRT_GUESS = float(0x5F3759DF)

PAIR = 2 * L
NT = T // PAIR
KP = PD // 128
QUAD = 4
NQ = NE // QUAD
RING = 4
ROUNDS = NQ // RING
NFT = 3
KF = FF // 128
HALF = B // 2
TH = HALF * L
CC = D // 64
XD = DTR + 2 * NS
NG = 4
TT = 5
TP = TT * 128
LAST = T - (TT - 1) * 128

C_ID, C_HEAD, C_VM, C_BM, C_IOTA = 0, 128, 134, 326, 328
C_W = 336
W_QKV, W_OUT, W_PHI, W_RT, W_PHIS = 0, 3 * D, 4 * D, 4 * D + NE, 4 * D + NE + NX
W_W = 4 * D + NE + NX
R_BP, R_LG, R_LB, R_FG, R_FB = range(5)
K_CX, K_CZ, K_D, K_DT, K_AL, K_SC = 0, 12, 24, 27, 30, 78
K_W = 79
S_IN, S_XP, S_DT, S_OUT = 0, 768, 1032, 1416
S_W = S_OUT + 2 * CC * D


def build_tower(nc, patches, w_patch, consts, half_w, rows, cols, b1t, b2n, scan_w, w1q, w2q, f1, f2, out):
    fp32 = mybir.dt.float32
    ALU = mybir.AluOpType
    ACT = mybir.ActivationFunctionType
    AX = mybir.AxisListType.X
    ds = bass.ds
    MULT, ADD, SUB, MAX = ALU.mult, ALU.add, ALU.subtract, ALU.max

    ctx = ExitStack()
    with ctx:
        def sb(name, shape, dt=fp32):
            return ctx.enter_context(nc.sbuf_tensor(name, shape, dt))

        def sem(name):
            return ctx.enter_context(nc.semaphore(name))

        ring = [sb(f"ring{s}", [128, 2 * QUAD * KF * D]) for s in range(RING)]
        W1N = QUAD * KF * D
        w1s = [r[:, 0:W1N].rearrange("p (a c f) -> p a c f", a=2, c=3) for r in ring]
        w2s = [r[:, W1N:2 * W1N].rearrange("p (q k d) -> p q k d", q=QUAD, k=KF) for r in ring]
        cst = sb("cst", [128, C_W])
        ident = cst[:, C_ID:C_ID + 128]
        hw = sb("hw", [128, 2, W_W])
        row = sb("row", [128, 5, D])
        col = sb("col", [128, K_W])
        b1 = sb("b1", [128, NQ, NFT, 8])
        b2 = sb("b2", [128, D])
        hA = sb("hA", [PAIR, NT, D])
        ones = sb("ones", [128, 128])
        phin = sb("phin", [128, 2, NE])
        bn = sb("bn", [128, NT, 6])
        mv = sb("mv", [128, NT, 2])
        rs = [sb(f"rs{k}", [128, 64]) for k in range(5)]
        mxs = sb("mxs", [128, 4, NH])
        ar = sb("ar", [128, 10264])

        pat = ring[3][:, 0:KP * T].rearrange("p (k t) -> p k t", k=KP)
        wpa = ring[3][:, KP * T:KP * (T + D)].rearrange("p (k d) -> p k d", k=KP)

        def view(first, end, pattern=None, rows_=128, **kw):
            v = ar[0:rows_, first:end]
            return v.rearrange(pattern, **kw) if pattern else v

        xn = view(0, 1536, "p (t d) -> p t d", rows_=PAIR, t=NT)
        ysn = view(0, 1536, "p (t d) -> p t d", t=NT)
        xT = view(1536, 2688, "p (k t) -> p k t", k=2)
        TQ = T + 28
        qT = view(2688, 2688 + 2 * TQ, "p (k t) -> p k t", k=2)
        kT = view(3896, 5048, "p (k t) -> p k t", rows_=H, k=2)
        kbd = view(5048, 5912, "p (g h t) -> p g h t", g=2, h=6)
        xR = [view(5912 + 432 * n, 6344 + 432 * n, "p (k b r l) -> p k b r l", k=2, b=2, r=3) for n in range(2)]
        prob = [view(6776 + 432 * n, 7208 + 432 * n, "p (h k) -> p h k", h=NH) for n in range(2)]
        pT = view(7640, 8152, "p (g t) -> p g t", g=4)
        vbd = [view(8152 + 384 * n, 8536 + 384 * n, "p (b d) -> p b d", b=2) for n in range(2)]
        osb = view(8920, 9112)
        oT = view(9112, 10264, "p (k t) -> p k t", k=2)
        XS = view(1536, 4608, "p (a c e b) -> p a c e b", a=NE // 2, c=3, e=2)
        Lc = view(4608, 5120, "p (t n) -> p t n", rows_=PAIR, t=NT)
        Ld = view(5120, 5696, "p (b m) -> p b m", rows_=NE, b=B)
        cbd = view(6464, 7488, "p (t b n) -> p t b n", rows_=PAIR, t=NT, b=2)
        dbd = view(8192, 9216, "p (t b n) -> p t b n", rows_=PAIR, t=NT, b=2)
        cT = view(9216, 9792, "p (t m) -> p t m", t=NT)
        XSq = [view(9792 + 192 * n, 9984 + 192 * n, "p (a c m) -> p a c m", a=2, c=3) for n in range(2)]
        hs = [view(7680 + 384 * n, 8064 + 384 * n) for n in range(2)]
        hb = view(8448, 8832, "p (t g b) -> p t g b", t=NFT, g=8)
        hg = view(8832, 9216, "p (t g b) -> p t g b", t=NFT, g=8)
        ysb = view(5696, 5696 + RING * D, "p (s d) -> p s d", s=RING)
        sw = ring[1][:, 0:S_W]
        w_in = sw[:, S_IN:S_IN + 768].rearrange("p (k c d) -> p k c d", k=2, c=2 * CC)
        w_xp = sw[:, S_XP:S_XP + 264].rearrange("p (c e) -> p c e", c=CC)
        w_dt = sw[0:2 * XD, S_DT:S_DT + 384].rearrange("p (c d) -> p c d", c=CC)
        w_so = sw[:, S_OUT:S_OUT + 2 * CC * D].rearrange("p (c d) -> p c d", c=2 * CC)
        o1 = [S_W]

        def slot1(n, p=128):
            o1[0] += n
            return ring[1][0:p, o1[0] - n:o1[0]]

        u = slot1(CC * TH).rearrange("p (c b l) -> p c b l", c=CC, b=HALF)
        du = slot1(CC * TH).rearrange("p (c t) -> p c t", c=CC)
        delta = slot1(CC * TH).rearrange("p (c t) -> p c t", c=CC)
        sp = [slot1(CC * TH).rearrange("p (c t) -> p c t", c=CC) for _ in range(3)]
        xd = slot1(TH, 2 * XD)
        negA = slot1(CC * NS)
        assert o1[0] <= 2 * W1N
        zr = view(9216, 9216 + CC * TH, "p (c b l) -> p c b l", c=CC, b=HALF)
        ybd = view(2688, 2688 + 2 * CC * TP, "p (c t) -> p c t", c=2 * CC)
        zc = view(6528, 6528 + CC * TH, "p (c b l) -> p c b l", c=CC, b=HALF)
        ztmp = view(7392, 7392 + CC * TH, "p (c b l) -> p c b l", c=CC, b=HALF)
        sel = [ring[s][0:2 * XD, a + 128 * n:a + 128 * (n + 1)] for s, a, m in ((0, 5376, 30), (1, o1[0], 2)) for n in range(m)]
        Bb = ring[2][:, 0:NS * TH].rearrange("p (n t) -> p n t", n=NS)
        Cb = ring[2][:, NS * TH:2 * NS * TH].rearrange("p (n t) -> p n t", n=NS)
        GW = NG * TH
        dA = [ring[3][:, n * GW:(n + 1) * GW] for n in range(2)]
        dBu = [ring[3][:, (2 + n) * GW:(3 + n) * GW] for n in range(2)]
        hst = [ring[3][:, (4 + n) * GW:(5 + n) * GW] for n in range(2)]
        hC = [ring[3][:, (6 + n) * GW:(7 + n) * GW] for n in range(2)]
        hB = view(8256, 8256 + TT * D, "p (t d) -> p t d", t=TT)
        f1s = [ring[0][:, 2688 * n:2688 * n + 1536].rearrange("p (k f) -> p k f", k=2) for n in range(2)]
        f2s = [ring[0][:, 2688 * n + 1536:2688 * (n + 1)].rearrange("p (k d) -> p k d", k=KF) for n in range(2)]
        tk = ring[2][:, 0:TT * D].rearrange("p (t d) -> p t d", t=TT)
        tkT = ring[2][:, 1000:1000 + 2 * TP].rearrange("p (k t) -> p k t", k=2)
        gT = [ring[3][:, n * KF * T:(n + 1) * KF * T].rearrange("p (f t) -> p f t", f=KF) for n in range(2)]
        rt = [ring[2][:, 2400 + 40 * n:2440 + 40 * n].rearrange("p (t e) -> p t e", t=TT) for n in range(8)]
        ridx = sb("ridx", [128, TT, 8], mybir.dt.uint32)

        ps = [ctx.enter_context(nc.psum_tensor(f"ps{k}", [128, 512], fp32)) for k in range(8)]

        patch_loaded = [sem(f"patch_loaded{k}") for k in range(3)]
        cst_loaded, hw_loaded, row_loaded, col_loaded = map(sem, ("cst_loaded", "hw_loaded", "row_loaded", "col_loaded"))
        padded, xT_padded, tkT_padded, sel_ready = map(sem, ("padded", "xT_padded", "tkT_padded", "sel_ready"))
        bias_loaded, scan_w_loaded = sem("bias_loaded"), sem("scan_w_loaded")
        w1_loaded = [sem(f"w1_loaded{s}") for s in range(RING)]
        w2_loaded = [sem(f"w2_loaded{s}") for s in range(RING)]
        ys_stored = [sem(f"ys_stored{s}") for s in range(RING)]
        f1_loaded = [sem(f"f1_loaded{s}") for s in range(2)]
        f2_loaded = [sem(f"f2_loaded{s}") for s in range(2)]
        ys_moved, resid_moved, out_stored = map(sem, ("ys_moved", "resid_moved", "out_stored"))
        (dve_step, act_step, pool_step, embedded, xn_ready, x_turned, xT_ready) = map(sem, (
            "dve_step", "act_step", "pool_step", "embedded", "xn_ready", "x_turned", "xT_ready"))
        (qk_done, qk_saved, xR_ready, kbd_ready, v_done, vbd_ready, scores_done, shifted, exp_done, p_turned, pT_ready,
         av_done, o_ready, o_turned, oT_ready, y_done, an_ready, h1_ready) = map(sem, (
            "qk_done", "qk_saved", "xR_ready", "kbd_ready", "v_done", "vbd_ready", "scores_done", "shifted", "exp_done",
            "p_turned", "pT_ready", "av_done", "o_ready", "o_turned", "oT_ready", "y_done", "an_ready", "h1_ready"))
        (phi_sq, phi_sum, phi_ready, ld_done, lc_done, sm_shift, sm_exp, d_ready, d_turned, dbd_ready, c_ready,
         c_turned, cT_ready, xs_done, xs_zero, xs_ready) = map(sem, (
            "phi_sq", "phi_sum", "phi_ready", "ld_done", "lc_done", "sm_shift", "sm_exp", "d_ready", "d_turned",
            "dbd_ready", "c_ready", "c_turned", "cT_ready", "xs_done", "xs_zero", "xs_ready"))
        (xsq_ready, h_done, h_saved, h_turned, b1_added, gelu_done, ys_done, ys_ready, comb_done, hA_ready) = map(sem, (
            "xsq_ready", "h_done", "h_saved", "h_turned", "b1_added", "gelu_done", "ys_done", "ys_ready",
            "comb_done", "hA_ready"))
        (in_done, z_saved, conv_ready, zconv_ready, u_ready, xd_done, xd_saved, dt_done, sp_t, sp_act, bc_done,
         bc_saved, dA_zeroed, negA_ready, delta_ready, dA_ready, scan_done, h_used, hC_ready, z_ready, ybd_zero, yb_ready,
         so_done) = map(sem, (
            "in_done", "z_saved", "conv_ready", "zconv_ready", "u_ready", "xd_done", "xd_saved", "dt_done", "sp_t",
            "sp_act", "bc_done", "bc_saved", "dA_zeroed", "negA_ready", "delta_ready", "dA_ready", "scan_done", "h_used", "hC_ready",
            "z_ready", "ybd_zero", "yb_ready", "so_done"))
        (hB_pad, tk_ready, tk_turned, tkT_ready, logit_done, rt_shift, rt_exp, up_done, silu_done, down_done,
         expert_added) = map(sem, (
            "hB_pad", "tk_ready", "tk_turned", "tkT_ready", "logit_done", "rt_shift", "rt_exp", "up_done", "silu_done",
            "down_done", "expert_added"))

        ys_dram = nc.dram_tensor("ys_dram", (NE, B, D), fp32, kind="Internal").ap()
        NUNIT = (NS // NG) * CC
        PADS = 8
        COMB = (0, 1, 4, 5)
        SO = (0, 1, 2, 6, 7)
        XS_BANKS = ((4, 5, 6), (7, 0, 1))
        XS_PARTS = ((0, 0, 128, 0, 0), (1, 0, 64, 128, 0), (1, 64, 64, 0, 1), (2, 0, 128, 64, 1))

        def slot_inputs(half, n):
            c, p0, m, _, e = XS_PARTS[n]
            bs = slice(half * HALF, (half + 1) * HALF)
            return (XS[p0:p0 + m, :, c, e, bs].rearrange("p a b -> p b a"), ps[XS_BANKS[half][c]][p0:p0 + m, half * 4 * NE:(half + 1) * 4 * NE].rearrange("p (b a) -> p b a", b=HALF))

        block = ctx.enter_context(nc.Block())

        @block.sync
        def _(sp_):
            for k in range(3):
                sp_.dma_start(wpa[:, 2 * k:2 * k + 2, :], w_patch[:, 2 * k:2 * k + 2, :]).then_inc(patch_loaded[k], 16)
                sp_.dma_start(pat[:, 2 * k:2 * k + 2, :], patches[:, 2 * k:2 * k + 2, :]).then_inc(patch_loaded[k], 16)
            sp_.dma_start(row[:, :, :], rows).then_inc(row_loaded, 16)
            sp_.dma_start(hw[:, :, :], half_w).then_inc(hw_loaded, 16)
            sp_.dma_start(col[:, :], cols).then_inc(col_loaded, 16)
            sp_.dma_start(b1[:, :, :, :], b1t).then_inc(bias_loaded, 16)
            sp_.dma_start(b2[:, :], b2n).then_inc(bias_loaded, 16)

            def load_quad(s, quad):
                sp_.dma_start(ring[s][:, 0:W1N], w1q[quad, :, :]).then_inc(w1_loaded[s], 16)
                sp_.dma_start(ring[s][:, W1N:2 * W1N], w2q[quad, :, :]).then_inc(w2_loaded[s], 16)

            def store_ys(s, quad):
                sp_.wait_ge(ys_ready, quad + 1)
                for q in range(QUAD):
                    p0 = 32 * q + B * (q % 2)
                    sp_.dma_start(ys_dram[ds(QUAD * quad + q, 1), :, :].rearrange("a b d -> (a b) d"), ysb[p0:p0 + B, s, :]).then_inc(ys_stored[s], 16)

            def load_ys(n0, n1):
                for s in range(RING):
                    sp_.wait_ge(ys_stored[s], 16 * n1 // RING)
                for odd in range(2):
                    sp_.dma_start(ysn[64 * odd + n0:64 * odd + n1, :, :], ys_dram[n0:n1, odd:B:2, :]).then_inc(ys_moved, 16)

            for s in range(RING):
                if s == RING - 1:
                    sp_.wait_ge(embedded, NT)
                load_quad(s, s)
            with sp_.Fori(0, ROUNDS - 1) as r:
                for s in range(RING):
                    sp_.wait_ge(h_done, RING * r + s + 1)
                    sp_.dma_start(ring[s][:, 0:W1N], w1q[ds(RING * r + (RING + s), 1), :, :].rearrange("a p n -> (a p) n")).then_inc(w1_loaded[s], 16)
                    sp_.wait_ge(ys_done, RING * r + s + 1)
                    sp_.dma_start(ring[s][:, W1N:2 * W1N], w2q[ds(RING * r + (RING + s), 1), :, :].rearrange("a p n -> (a p) n")).then_inc(w2_loaded[s], 16)
                    store_ys(s, RING * r + s)
            sp_.wait_ge(ys_done, NQ - 3)
            for s in range(2):
                sp_.dma_start(f1s[s], f1[s, :, :, :]).then_inc(f1_loaded[s], 16)
                sp_.dma_start(f2s[s], f2[s, :, :, :]).then_inc(f2_loaded[s], 16)
            sp_.wait_ge(ys_done, NQ - 2)
            sp_.dma_start(ring[1][:, 0:S_W], scan_w).then_inc(scan_w_loaded, 16)
            load_ys(0, NE - QUAD * RING)
            for s in range(RING):
                store_ys(s, NQ - RING + s)
            load_ys(NE - QUAD * RING, NE)
            sp_.wait_ge(hA_ready, 2)
            n = 0
            for t in range(NT):
                a, end = PAIR * t, PAIR * (t + 1)
                while a < end:
                    m = min(end, (a // 128 + 1) * 128) - a
                    sp_.dma_start(hB[a % 128:a % 128 + m, a // 128, :], hA[a - PAIR * t:a - PAIR * t + m, t, :]).then_inc(resid_moved, 16)
                    a += m
                    n += 1
            with sp_.Fori(0, NX // 2 - 1) as r:
                for s in range(2):
                    sp_.wait_ge(up_done, 12 * (2 * r + s + 1))
                    sp_.dma_start(f1s[s], f1[ds(2 * r + (2 + s), 1), :, :, :].rearrange("a p k n -> (a p) k n")).then_inc(f1_loaded[s], 16)
                    sp_.wait_ge(down_done, TT * (2 * r + s + 1))
                    sp_.dma_start(f2s[s], f2[ds(2 * r + (2 + s), 1), :, :, :].rearrange("a p k n -> (a p) k n")).then_inc(f2_loaded[s], 16)
            sp_.wait_ge(expert_added, TT * NX)
            sp_.dma_start(out[0:(TT - 1) * 128, :].rearrange("(t p) d -> p t d", p=128), hB[:, 0:TT - 1, :]).then_inc(out_stored, 16)
            sp_.dma_start(out[(TT - 1) * 128:T, :], hB[0:LAST, TT - 1, :]).then_inc(out_stored, 16)
            sp_.wait_ge(out_stored, 32)

        NMOVE = 0
        for t in range(NT):
            a, end = PAIR * t, PAIR * (t + 1)
            while a < end:
                a += min(end, (a // 128 + 1) * 128) - a
                NMOVE += 1
        YMOVE = 4

        @block.gpsimd
        def _(gp):
            gp.memset(ones[:, :], 1.0).then_inc(padded, 1)
            gp.wait_ge(padded, 1)
            for first, end, value in ((1536, 3896, 1.0), (9112, 10264, 1.0), (5048, 5912, 0.0), (5912, 6776, 1.0), (7640, 8152, 1.0), (8152, 8920, 0.0)):
                gp.memset(ar[96:128, first:end], value).then_inc(padded, 1)
            gp.wait_ge(padded, PADS - 1)
            gp.memset(qT[0:H, :, T:TQ], 0.0).then_inc(padded, 1)
            gp.wait_ge(padded, PADS)
            gp.wait_ge(cst_loaded, 16)
            steps = 0

            def pool_link(ins):
                nonlocal steps
                ins.then_inc(pool_step, 1)
                steps += 1
                gp.wait_ge(pool_step, steps)

            def add_attention(g):
                two = slice(2 * g, 2 * g + 2)
                gp.wait_ge(an_ready, g + 1)
                pool_link(nc.gpsimd.tensor_tensor(xn[:, two, :], xn[:, two, :], row[0:PAIR, R_LG:R_LG + 1, :].to_broadcast([PAIR, 2, D]), MULT))
                pool_link(nc.gpsimd.tensor_tensor(xn[:, two, :], xn[:, two, :], row[0:PAIR, R_LB:R_LB + 1, :].to_broadcast([PAIR, 2, D]), ADD))
                nc.gpsimd.tensor_tensor(hA[:, two, :], hA[:, two, :], xn[:, two, :], ADD).then_inc(h1_ready, 1)

            gp.wait_ge(qk_saved, 8)
            for t in range(NT):
                if t == 6:
                    add_attention(0)
                if t >= 1:
                    gp.wait_ge(scores_done, t)
                for g in range(2):
                    ins = nc.gpsimd.tensor_tensor(
                        kbd[0:H, g, :, :],
                        kT[:, g:g + 1, PAIR * t:PAIR * (t + 1)].to_broadcast([H, 6, PAIR]),
                        cst[0:H, C_HEAD:C_HEAD + 6].rearrange("p (h a) -> p h a", a=1).to_broadcast([H, 6, PAIR]), MULT)
                ins.then_inc(kbd_ready, 1)
            for g in range(1, NT // 2 - 1):
                add_attention(g)
            gp.wait_ge(scores_done, NT)
            gp.wait_ge(h1_ready, 3)
            gp.memset(ar[:, 2688:4608], 0.0).then_inc(xs_zero, 1)
            gp.wait_ge(lc_done, 2)
            gp.memset(ar[:, 1536:2688], 0.0).then_inc(xs_zero, 1)
            gp.wait_ge(xs_ready, 8)
            gp.tensor_copy(XSq[0], XS[:, 0:2, :, :, :].rearrange("p a c e b -> p a c (e b)")).then_inc(xsq_ready, 1)
            gp.tensor_copy(XSq[1], XS[:, 2:4, :, :, :].rearrange("p a c e b -> p a c (e b)")).then_inc(xsq_ready, 1)
            with gp.Fori(0, (NQ - 2) // 2) as r:
                for s in range(2):
                    gp.wait_ge(h_done, 2 * r + s + 1)
                    gp.tensor_copy(XSq[s], XS[:, ds(4 * r + (4 + 2 * s), 2), :, :, :].rearrange("p a c e b -> p a c (e b)")).then_inc(xsq_ready, 1)
            gp.wait_ge(xsq_ready, NQ)
            gp.memset(ar[96:128, 1536:2688], 1.0).then_inc(xT_padded, 1)
            for n in range(2 * NS):
                if n in (0, 30):
                    gp.wait_ge(ys_done, NQ - 3 if n == 0 else NQ - 2)
                e = DTR + (n % 2) * NS + n // 2
                ins = nc.gpsimd.tensor_copy(sel[n].rearrange("p (b d) -> p b d", b=2), ident[0:2 * XD, e:XD + e + 1:XD].rearrange("p (b a) -> p b a", a=1).to_broadcast([2 * XD, 2, 64]))
            ins.then_inc(sel_ready, 1)
            gp.wait_ge(sel_ready, 1)
            gp.wait_ge(comb_done, 4)
            gp.memset(hB[LAST:128, TT - 1, :], 0.0).then_inc(hB_pad, 1)
            gp.wait_ge(hB_pad, 1)
            gp.memset(ybd[:, :, :], 0.0).then_inc(ybd_zero, 1)
            gp.wait_ge(ybd_zero, 1)
            for n in range(2):
                gp.memset(dA[n].rearrange("p (g l) -> p g l", l=L)[:, :, 0:1], 0.0).then_inc(dA_zeroed, 1)
            gp.wait_ge(z_saved, CC)
            for k in (1, 0, 2, 3):
                o = k - 1
                a, e = max(0, -o), L - max(0, o)
                dst = zc if k == 1 else ztmp
                for c in range(CC):
                    ins = nc.gpsimd.tensor_scalar(dst[:, c, :, a:e], zr[:, c, :, a + o:e + o], col[:, K_CZ + TAPS * c + k:K_CZ + TAPS * c + k + 1], None, MULT)
                pool_link(ins)
                if k != 1:
                    pool_link(nc.gpsimd.tensor_tensor(zc[:, :, :, a:e].rearrange("p c b l -> p (c b) l"), zc[:, :, :, a:e].rearrange("p c b l -> p (c b) l"), ztmp[:, :, :, a:e].rearrange("p c b l -> p (c b) l"), ADD))
            gp.memset(ztmp[0:1, 0, 0, 0:1], 0.0).then_inc(zconv_ready, 1)
            gp.wait_ge(yb_ready, CC)
            gp.memset(tkT[96:128, :, :], 1.0).then_inc(tkT_padded, 1)

        @block.scalar
        def _(act):
            A = nc.scalar.activation
            act.dma_start(cst[:, :], consts).then_inc(cst_loaded, 16)
            def save_turned(n0, tiles):
                for t in tiles:
                    act.wait_ge(x_turned, n0 + t + 1)
                    A(xT[0:H, :, PAIR * t:PAIR * (t + 1)], ps[t][0:H, 0:2 * PAIR].rearrange("p (k t) -> p k t", k=2), ACT.Copy).then_inc(xT_ready, 1)

            def triple(t):
                if t >= 2:
                    act.wait_ge(v_done, t - 1)
                for k in range(2):
                    ins = A(xR[t % 2][0:H, k, :, :, :], xT[0:H, k, PAIR * t:PAIR * (t + 1)].rearrange("p (b a l) -> p b a l", b=2, a=1).to_broadcast([H, 2, 3, L]), ACT.Copy)
                ins.then_inc(xR_ready, 1)

            act.wait_ge(padded, PADS)
            for half in range(2):
                save_turned(0, range(4 * half, 4 * half + 4))
                for c in (0, 2):
                    n = 4 * half + c
                    act.wait_ge(qk_done, n + 1)
                    A((qT if c < 2 else kT)[0:H, c % 2, half * TH:(half + 1) * TH], ps[n][0:H, 0:TH], ACT.Copy).then_inc(qk_saved, 1)
            act.wait_ge(xT_ready, NT)
            triple(0)
            for i in range(NT + 2):
                if 1 <= i <= NT:
                    t = i - 1
                    act.wait_ge(p_turned, t + 1)
                    if t >= 1:
                        act.wait_ge(av_done, t)
                    A(pT[0:3 * L], ps[2][0:3 * L, :].rearrange("p (g t) -> p g t", g=4), ACT.Copy).then_inc(pT_ready, 1)
                if i + 1 < NT:
                    triple(i + 1)
                if i < NT:
                    act.wait_ge(shifted, i + 1)
                    A(prob[i % 2], prob[i % 2], ACT.Exp, scale=HD ** -0.5).then_inc(exp_done, 1)
                if 2 <= i < NT + 2:
                    t = i - 2
                    act.wait_ge(o_turned, t + 1)
                    A(oT[0:H, :, PAIR * t:PAIR * (t + 1)].rearrange("p k (b l) -> p k b l", b=2),
                      ps[5][0:H, 0:256].rearrange("p (k b l) -> p k b l", k=2, b=2)[:, :, :, 0:L], ACT.Copy).then_inc(oT_ready, 1)
            save_turned(NT, range(NT))
            for half in range(2):
                act.wait_ge(sm_shift, half + 1)
                bs = slice(half * HALF, (half + 1) * HALF)
                A(Ld[:, bs, :], Ld[:, bs, :], ACT.Exp).then_inc(sm_exp, 1)
            act.wait_ge(xs_zero, 2)
            for half in range(2):
                for n in (0, 1):
                    act.wait_ge(xs_done, 4 * half + n + 1)
                    dst, src = slot_inputs(half, n)
                    A(dst, src, ACT.Copy).then_inc(xs_ready, 1)
            act.wait_ge(sm_shift, 3)
            A(Lc, Lc, ACT.Exp).then_inc(sm_exp, 1)

            def hidden(r):
                for s in range(RING):
                    act.wait_ge(h_done, RING * r + s + 1)
                    A(hs[s % 2], ps[s % 2][:, 0:NFT * 128], ACT.Copy).then_inc(h_saved, 1)
                    act.wait_ge(b1_added, RING * r + s + 1)
                    A(hg, hb, ACT.Gelu).then_inc(gelu_done, 1)

            hidden(0)
            for n in range(2):
                act.wait_ge(c_turned, n + 1)
                A(cT[:, 4 * n:4 * n + 4, :], ps[6 + n][:, 0:4 * PAIR].rearrange("p (t m) -> p t m", t=4), ACT.Copy).then_inc(cT_ready, 1)
            with act.Fori(1, ROUNDS) as r:
                hidden(r)
            save_turned(2 * NT, range(NT))
            A(negA, col[:, K_AL:K_AL + CC * NS], ACT.Exp).then_inc(act_step, 1)
            for c in range(CC):
                act.wait_ge(in_done, CC + c + 1)
                A(zr[:, c, :, :], ps[CC + c][:, 0:TH].rearrange("p (b l) -> p b l", b=HALF), ACT.Copy).then_inc(z_saved, 1)
            for c in range(CC):
                act.wait_ge(conv_ready, c + 1)
                A(u[:, c, :, :], u[:, c, :, :], ACT.Silu).then_inc(u_ready, 1)
            act.wait_ge(xd_done, 1)
            A(xd, ps[6][0:2 * XD, 0:TH], ACT.Copy).then_inc(xd_saved, 1)
            act.wait_ge(sp_t, 1)
            A(sp[1], sp[0], ACT.Abs).then_inc(sp_act, 1)
            act.wait_ge(sp_act, 1)
            A(sp[1], sp[1], ACT.Exp, scale=-1.0).then_inc(sp_act, 1)
            act.wait_ge(sp_act, 2)
            A(delta, sp[1], ACT.Ln, bias=1.0).then_inc(sp_act, 1)
            bc = [0]

            def save_bc(upto):
                while bc[0] < upto:
                    n = bc[0]
                    act.wait_ge(bc_done, n + 1)
                    A((Bb if n % 2 == 0 else Cb)[:, n // 2, :], ps[6 + n % 2][:, 0:TH], ACT.Copy).then_inc(bc_saved, 1)
                    bc[0] += 1

            act.wait_ge(dA_zeroed, 2)
            act.wait_ge(negA_ready, 1)
            save_bc(2 * NG)
            act.wait_ge(delta_ready, 1)
            for k in range(NUNIT):
                g, c = k // CC, k % CC
                if k >= 2:
                    act.wait_ge(scan_done, k - 1)
                for j in range(NG):
                    n = NG * g + j
                    dst = dA[k % 2][:, j * TH:(j + 1) * TH].rearrange("p (b l) -> p b l", b=HALF)[:, :, 1:L]
                    ins = A(dst, delta[:, c, :].rearrange("p (b l) -> p b l", b=HALF)[:, :, 1:L], ACT.Exp, scale=negA[:, CC * 0 + NS * c + n:NS * c + n + 1])
                ins.then_inc(dA_ready, 1)
                if g + 1 < NS // NG:
                    save_bc(min(2 * NG * (g + 2), 2 * NG * (g + 1) + (c + 1) * 3))
            act.wait_ge(zconv_ready, 1)
            act.wait_ge(ybd_zero, 1)
            for half in range(2):
                p0 = 64 * half
                A(ybd[p0:p0 + 64, CC:2 * CC, half * TH:(half + 1) * TH], zc[p0:p0 + 64, :, :, :].rearrange("p c b l -> p c (b l)"), ACT.Silu).then_inc(z_ready, 1)
            for t in range(TT):
                act.wait_ge(tk_turned, t + 1)
                A(tkT[0:H, :, 128 * t:128 * (t + 1)], ps[t][0:H, 0:256].rearrange("p (k t) -> p k t", k=2), ACT.Copy).then_inc(tkT_ready, 1)
            act.wait_ge(rt_shift, 1)
            A(rt[1], rt[0], ACT.Exp).then_inc(rt_exp, 1)
            with act.Fori(0, NX // 2) as r:
                for s in range(2):
                    for n in range(12):
                        act.wait_ge(up_done, 24 * r + (12 * s + n + 1))
                        f, half = n // 2, n % 2
                        A(gT[s][:, f, half * TH:(half + 1) * TH], ps[n % 3][:, 0:TH], ACT.Silu).then_inc(silu_done, 1)

        @block.vector
        def _(dve):
            V = nc.vector
            chain = [0]

            def link(ins):
                ins.then_inc(dve_step, 1)
                chain[0] += 1
                dve.wait_ge(dve_step, chain[0])

            def rsqrt(p, n, first=0):
                z, t, y = (rs[k][0:p, first:first + n] for k in (0, 4, 3))
                link(V.tensor_scalar(y.bitcast(mybir.dt.int32), z.bitcast(mybir.dt.int32), -0.5, RSQRT_GUESS, MULT, ADD))
                for _ in range(3):
                    link(V.tensor_tensor(t, y, y, MULT))
                    link(V.scalar_tensor_tensor(out=t, in0=t, scalar=-0.5, in1=z, op0=MULT, op1=MULT))
                    link(V.scalar_tensor_tensor(out=y, in0=t, scalar=1.5, in1=y, op0=ADD, op1=MULT))

            def statistics(x, p, t0, n):
                for t in range(n):
                    ins = V.bn_stats(bn[0:p, t0 + t, :], x[:, t, :])
                link(ins)
                for t in range(n):
                    ins = V.bn_aggr(mv[0:p, t0 + t, :], bn[0:p, t0 + t, :])
                link(ins)

            def deviations(x, p, t0, n):
                statistics(x, p, t0, n)
                link(V.tensor_scalar(rs[0][0:p, t0:t0 + n], mv[0:p, t0:t0 + n, 1], LN_EPS, None, ADD))
                rsqrt(p, n, t0)

            def normalise(dst, x, p, t0, n):
                for t in range(n):
                    yield V.tensor_scalar(dst[:, t, :], x[:, t, :], mv[0:p, t0 + t, 0:1], rs[3][0:p, t0 + t:t0 + t + 1], SUB, MULT)

            def norm_in_halves(produce):
                n = NT // 2
                for half in range(2):
                    four = slice(half * n, (half + 1) * n)
                    produce(half)
                    deviations(hA[:, four, :], PAIR, half * n, n)
                    for ins in normalise(xn[:, four, :], hA[:, four, :], PAIR, half * n, n):
                        ins.then_inc(xn_ready, 1)

            def rowof(k, p, n):
                return row[0:p, k:k + 1, :].to_broadcast([p, n, D])

            dve.wait_ge(row_loaded, 16)

            def embedding(half):
                for t in range(4 * half, 4 * half + 4):
                    dve.wait_ge(embedded, t + 1)
                    ins = V.tensor_tensor(hA[:, t, :], ps[t][0:PAIR, 0:D], row[0:PAIR, R_BP, :], ADD)
                link(ins)

            norm_in_halves(embedding)
            dve.wait_ge(hw_loaded, 16)
            phi = hw[:, :, W_PHI:W_PHI + NE]
            V.tensor_tensor(phin[:, :, :], phi, phi, MULT).then_inc(phi_sq, 1)

            def unit_rows(t0, n):
                dve.wait_ge(h1_ready, min((t0 + n) // 2, 3))
                x = hA[:, t0:t0 + n, :]
                statistics(x, PAIR, t0, n)
                var, z = mv[0:PAIR, t0:t0 + n, 1], rs[0][0:PAIR, t0:t0 + n]
                link(V.tensor_scalar(z, var, LN_EPS, 1e-24, ADD, MULT))
                link(V.scalar_tensor_tensor(out=z, in0=var, scalar=float(D), in1=z, op0=MULT, op1=MAX))
                rsqrt(PAIR, n, t0)
                for ins in normalise(xn[:, t0:t0 + n, :], x, PAIR, t0, n):
                    ins.then_inc(xn_ready, 1)

            dve.wait_ge(padded, PADS)
            for half in range(2):
                for c in (1, 3):
                    n = 4 * half + c
                    dve.wait_ge(qk_done, n + 1)
                    V.tensor_copy((qT if c < 2 else kT)[0:H, c % 2, half * TH:(half + 1) * TH], ps[n][0:H, 0:TH]).then_inc(qk_saved, 1)
            for i in range(NT + 3):
                if i < NT:
                    dve.wait_ge(v_done, i + 1)
                    if i >= 2:
                        dve.wait_ge(av_done, i - 1)
                    V.tensor_tensor(vbd[i % 2][0:3 * L], ps[3][0:3 * L, 0:2 * D].rearrange("p (b d) -> p b d", b=2),
                                    cst[0:3 * L, C_VM:C_VM + D].rearrange("p (a d) -> p a d", a=1).to_broadcast([3 * L, 2, D]), MULT).then_inc(vbd_ready, 1)
                    dve.wait_ge(scores_done, i + 1)
                    s3 = ps[i % 2][:, 0:NH * L].rearrange("p (h k) -> p h k", h=NH)
                    link(V.tensor_reduce(mxs[:, 0, :], s3, AX, MAX))
                    if i >= 2:
                        dve.wait_ge(p_turned, i - 1)
                    V.tensor_tensor(prob[i % 2], s3, mxs[:, 0, :].rearrange("p (h a) -> p h a", a=1).to_broadcast([128, NH, L]), SUB).then_inc(shifted, 1)
                if i == 1:
                    dve.wait_ge(phi_sum, 1)
                    link(V.tensor_scalar(rs[0][:, 0:NE], ps[7][:, 0:NE], 1e-24, None, MAX))
                    rsqrt(128, NE)
                    dve.wait_ge(col_loaded, 16)
                    link(V.tensor_scalar(rs[3][:, 0:NE], rs[3][:, 0:NE], col[:, K_SC:K_SC + 1], None, MULT))
                    V.tensor_tensor(phin[:, :, :], phi, rs[3][:, 0:NE].rearrange("p (a n) -> p a n", a=1).to_broadcast([128, 2, NE]), MULT).then_inc(phi_ready, 1)
                g = (i - 4) // 2
                if 1 <= i <= NT:
                    t = i - 1
                    dve.wait_ge(av_done, t + 1)
                    if t >= 1:
                        dve.wait_ge(o_turned, t)
                    V.tensor_tensor(osb.rearrange("p (h d) -> p h d", h=NH), ps[4][:, 0:D].rearrange("p (h d) -> p h d", h=NH),
                                    mxs[:, 2 + t % 2, :].rearrange("p (h a) -> p h a", a=1).to_broadcast([128, NH, HD]), MULT).then_inc(o_ready, 1)
                if i >= 4 and i % 2 == 0:
                    dve.wait_ge(y_done, 2 * g + 2)
                    y2 = ps[6 + g % 2][0:PAIR, 0:2 * D].rearrange("p (t d) -> p t d", t=2)
                    deviations(y2, PAIR, 2 * g, 2)
                    for ins in normalise(xn[:, 2 * g:2 * g + 2, :], y2, PAIR, 2 * g, 2):
                        pass
                    ins.then_inc(an_ready, 1)
                if i < NT:
                    dve.wait_ge(exp_done, i + 1)
                    link(V.tensor_reduce(mxs[:, 1, :], prob[i % 2], AX, ADD))
                    link(V.reciprocal(mxs[:, 2 + i % 2, :], mxs[:, 1, :]))
                if i >= 7 and i % 2 == 1:
                    unit_rows(i - 7, 2)
            two = slice(NT - 2, NT)
            dve.wait_ge(an_ready, NT // 2)
            link(V.tensor_tensor(xn[:, two, :], xn[:, two, :], rowof(R_LG, PAIR, 2), MULT))
            link(V.tensor_tensor(xn[:, two, :], xn[:, two, :], rowof(R_LB, PAIR, 2), ADD))
            link(V.tensor_tensor(hA[:, two, :], hA[:, two, :], xn[:, two, :], ADD))
            unit_rows(NT // 2, NT // 2)
            mxd, smd = rs[0][0:NE, 0:B], rs[1][0:NE, 0:B]

            def dispatch_shift(half):
                dve.wait_ge(ld_done, half + 1)
                bs = slice(half * HALF, (half + 1) * HALF)
                l3 = ps[half][0:NE, 0:TH].rearrange("p (b m) -> p b m", b=HALF)
                link(V.tensor_reduce(mxd[:, bs], l3, AX, MAX))
                V.tensor_tensor(Ld[:, bs, :], l3, mxd[:, bs].rearrange("p (b a) -> p b a", a=1).to_broadcast([NE, HALF, L]), SUB).then_inc(sm_shift, 1)

            def dispatch_divide(half):
                dve.wait_ge(sm_exp, half + 1)
                bs = slice(half * HALF, (half + 1) * HALF)
                link(V.tensor_reduce(smd[:, bs], Ld[:, bs, :], AX, ADD))
                link(V.reciprocal(smd[:, bs], smd[:, bs]))
                V.tensor_tensor(Ld[:, bs, :], Ld[:, bs, :], smd[:, bs].rearrange("p (b a) -> p b a", a=1).to_broadcast([NE, HALF, L]), MULT).then_inc(d_ready, 1)

            def dispatch_save(half):
                dve.wait_ge(d_turned, half + 1)
                ts = slice(4 * half, 4 * half + 4)
                for b in range(2):
                    ins = V.tensor_scalar(dbd[:, ts, b, :], ps[3][0:PAIR, 4 * half * NE:4 * (half + 1) * NE].rearrange("p (t n) -> p t n", t=4), cst[0:PAIR, C_BM + b:C_BM + b + 1], None, MULT)
                ins.then_inc(dbd_ready, 1)

            dispatch_shift(0)
            dispatch_divide(0)
            dispatch_shift(1)
            dispatch_save(0)
            dispatch_divide(1)
            dispatch_save(1)
            mxc, smc = rs[2][0:PAIR, 0:NT], rs[3][0:PAIR, 0:NT]
            l3 = ps[2][0:PAIR, :].rearrange("p (t n) -> p t n", t=NT)
            dve.wait_ge(lc_done, 2)
            link(V.tensor_reduce(mxc, l3, AX, MAX))
            V.tensor_tensor(Lc, l3, mxc.rearrange("p (t a) -> p t a", a=1).to_broadcast([PAIR, NT, NE]), SUB).then_inc(sm_shift, 1)
            dve.wait_ge(xs_zero, 2)
            for half in range(2):
                for n in (2, 3):
                    dve.wait_ge(xs_done, 4 * half + n + 1)
                    dst, src = slot_inputs(half, n)
                    V.tensor_copy(dst, src).then_inc(xs_ready, 1)
            dve.wait_ge(sm_exp, 3)
            link(V.tensor_reduce(smc, Lc, AX, ADD))
            link(V.reciprocal(smc, smc))
            link(V.tensor_tensor(Lc, Lc, smc.rearrange("p (t a) -> p t a", a=1).to_broadcast([PAIR, NT, NE]), MULT))
            for b in range(2):
                ins = V.tensor_scalar(cbd[:, :, b, :], Lc, cst[0:PAIR, C_BM + b:C_BM + b + 1], None, MULT)
            ins.then_inc(c_ready, 1)
            dve.wait_ge(bias_loaded, 32)

            def quad_steps(r):
                for s in range(RING):
                    dve.wait_ge(h_turned, RING * r + s + 1)
                    V.tensor_tensor(hb.rearrange("p t g b -> p (t g) b"), ps[2 + s % 2][:, 0:NFT * 128].rearrange("p (g b) -> p g b", b=B),
                                    b1[:, ds(RING * r + s, 1), :, :].rearrange("p a t g -> p (a t g)").rearrange("p (g a) -> p g a", a=1).to_broadcast([128, NFT * 8, B]), ADD).then_inc(b1_added, 1)
                    dve.wait_ge(ys_done, RING * r + s + 1)
                    if not (isinstance(r, int) and r == 0):
                        dve.wait_ge(ys_stored[s], 16 * QUAD * r)
                    V.tensor_copy(ysb[:, s, :], ps[4 + s % 2][:, 0:D]).then_inc(ys_ready, 1)

            quad_steps(0)
            with dve.Fori(1, ROUNDS) as r:
                quad_steps(r)
            def combined(half):
                for k in range(2 * half, 2 * half + 2):
                    dve.wait_ge(comb_done, k + 1)
                    ins = V.tensor_tensor(hA[:, 2 * k:2 * k + 2, :], ps[COMB[k]][0:PAIR, 0:2 * D].rearrange("p (t d) -> p t d", t=2), hA[:, 2 * k:2 * k + 2, :], ADD)
                ins.then_inc(hA_ready, 1)
                dve.wait_ge(hA_ready, half + 1)

            norm_in_halves(combined)
            dve.wait_ge(act_step, 1)
            V.tensor_scalar(negA, negA, -1.0, None, MULT).then_inc(negA_ready, 1)
            for c in range(CC):
                dve.wait_ge(in_done, c + 1)
                src = ps[c][:, 0:TH].rearrange("p (b l) -> p b l", b=HALF)
                w = [col[:, K_CX + TAPS * c + k:K_CX + TAPS * c + k + 1] for k in range(TAPS)]
                link(V.tensor_scalar(u[:, c, :, :], src, w[1], None, MULT))
                link(V.scalar_tensor_tensor(out=u[:, c, :, 1:L], in0=src[:, :, 0:L - 1], scalar=w[0], in1=u[:, c, :, 1:L], op0=MULT, op1=ADD))
                link(V.scalar_tensor_tensor(out=u[:, c, :, 0:L - 1], in0=src[:, :, 1:L], scalar=w[2], in1=u[:, c, :, 0:L - 1], op0=MULT, op1=ADD))
                V.scalar_tensor_tensor(out=u[:, c, :, 0:L - 2], in0=src[:, :, 2:L], scalar=w[3], in1=u[:, c, :, 0:L - 2], op0=MULT, op1=ADD).then_inc(conv_ready, 1)
            for c in range(CC):
                dve.wait_ge(dt_done, c + 1)
                bias = col[:, K_DT + c:K_DT + c + 1]
                ins = V.tensor_scalar(sp[0][:, c, :], ps[c][:, 0:TH], bias, bias, ADD, ADD)
            ins.then_inc(sp_t, 1)
            dve.wait_ge(sp_act, 2)
            link(V.tensor_scalar(sp[2], sp[1], LOG1P[0], None, MULT))
            for k in LOG1P[1:]:
                link(V.scalar_tensor_tensor(out=sp[2], in0=sp[2], scalar=k, in1=sp[1], op0=ADD, op1=MULT))
            link(V.tensor_scalar(du, sp[1], LOG1P_MAX, None, ALU.is_lt))
            dve.wait_ge(sp_act, 3)
            link(V.copy_predicated(delta, du.bitcast(mybir.dt.uint32), sp[2]))
            V.scalar_tensor_tensor(out=delta, in0=sp[0], scalar=0.0, in1=delta, op0=MAX, op1=ADD).then_inc(delta_ready, 1)
            dve.wait_ge(delta_ready, 1)
            dve.wait_ge(u_ready, CC)
            link(V.tensor_tensor(du, delta, u.rearrange("p c b l -> p c (b l)"), MULT))
            for k in range(NUNIT):
                g, c = k // CC, k % CC
                dve.wait_ge(bc_saved, 2 * NG * (g + 1))
                link(V.tensor_tensor(dBu[k % 2].rearrange("p (n t) -> p n t", n=NG), Bb[:, NG * g:NG * (g + 1), :], du[:, c:c + 1, :].to_broadcast([128, NG, TH]), MULT))
                dve.wait_ge(dA_ready, k + 1)
                V.tensor_tensor_scan(hst[k % 2], dA[k % 2], dBu[k % 2], 0.0, MULT, ADD).then_inc(scan_done, 1)
                dve.wait_ge(scan_done, k + 1)
                if k >= 2:
                    dve.wait_ge(h_used, k - 1)
                V.tensor_tensor(hC[k % 2], hst[k % 2], Cb[:, NG * g:NG * (g + 1), :].rearrange("p n t -> p (n t)"), MULT).then_inc(hC_ready, 1)
            dve.wait_ge(ybd_zero, 1)
            for c in range(CC):
                dve.wait_ge(h_used, NUNIT - CC + c + 1)
                for half in range(2):
                    p0 = 64 * half
                    ins = V.scalar_tensor_tensor(out=ybd[p0:p0 + 64, c, half * TH:(half + 1) * TH], in0=u[p0:p0 + 64, c, :, :].rearrange("p b l -> p (b l)"),
                                                 scalar=col[p0:p0 + 64, K_D + c:K_D + c + 1], in1=ps[3 + c][p0:p0 + 64, 0:TH], op0=MULT, op1=ADD)
                ins.then_inc(yb_ready, 1)
            dve.wait_ge(resid_moved, 16 * NMOVE)
            dve.wait_ge(hB_pad, 1)
            for t in range(TT):
                dve.wait_ge(so_done, t + 1)
                ins = V.tensor_tensor(hB[:, t, :], ps[SO[t]][:, 0:D], hB[:, t, :], ADD)
            link(ins)

            statistics(hB, 128, 0, TT)
            var, z, r = mv[:, 0:TT, 1], rs[0][:, 0:TT], rs[4][:, 0:TT]
            link(V.tensor_scalar(z, var, LN_EPS, None, ADD))
            link(V.reciprocal(r, z))
            link(V.tensor_tensor(r, r, var, MULT))
            link(V.tensor_scalar(rs[0][:, TT:2 * TT], r, LN_EPS, None, ADD))
            rsqrt(128, 2 * TT)
            for ins in normalise(tk, hB, 128, 0, TT):
                pass
            link(ins)
            link(V.tensor_tensor(hB, hB, tk, ADD))
            for t in range(TT):
                ins = V.tensor_scalar(tk[:, t, :], tk[:, t, :], rs[3][:, TT + t:TT + t + 1], None, MULT)
            link(ins)
            link(V.tensor_tensor(tk, tk, rowof(R_FG, 128, TT), MULT))
            V.tensor_tensor(tk, tk, rowof(R_FB, 128, TT), ADD).then_inc(tk_ready, 1)
            dve.wait_ge(logit_done, 1)
            lg = ps[5][:, 0:TT * NX].rearrange("p (t e) -> p t e", t=TT)
            m5, s5 = mxs[:, 0, 0:TT], mxs[:, 1, 0:TT]

            def wide(x, n=NX):
                return x.rearrange("p (t a) -> p t a", a=1).to_broadcast([128, TT, n])

            link(V.tensor_reduce(m5, lg, AX, MAX))
            V.tensor_tensor(rt[0], lg, wide(m5), SUB).then_inc(rt_shift, 1)
            dve.wait_ge(rt_exp, 1)
            link(V.tensor_reduce(s5, rt[1], AX, ADD))
            link(V.reciprocal(s5, s5))
            link(V.tensor_tensor(rt[1], rt[1], wide(s5), MULT))
            for t in range(TT):
                ins = V.max(rt[2][:, t, :], rt[1][:, t, :])
            link(ins)
            for t in range(TT):
                ins = V.max_index(ridx[:, t, :], rt[2][:, t, :], rt[1][:, t, :])
            link(ins)
            link(V.tensor_copy(rt[3], ridx[:, :, :]))
            top = rt[2][:, :, 0:TOPK]
            link(V.tensor_reduce(s5, top, AX, ADD))
            link(V.reciprocal(s5, s5))
            link(V.tensor_tensor(top, top, wide(s5, TOPK), MULT))
            iota = cst[:, C_IOTA:C_IOTA + NX].rearrange("p (a e) -> p a e", a=1).to_broadcast([128, TT, NX])
            for k in range(TOPK):
                link(V.tensor_tensor(rt[4 + k], iota, rt[3][:, :, k:k + 1].to_broadcast([128, TT, NX]), ALU.is_equal))
                link(V.tensor_tensor(rt[4 + k], rt[4 + k], rt[2][:, :, k:k + 1].to_broadcast([128, TT, NX]), MULT))
            link(V.tensor_tensor(rt[6], rt[4], rt[5], ADD))
            gates = rt[6]
            with dve.Fori(0, NX // 2) as r:
                for s in range(2):
                    for t in range(TT):
                        p = 128 if t < TT - 1 else LAST
                        dve.wait_ge(down_done, 2 * TT * r + (TT * s + t + 1))
                        V.scalar_tensor_tensor(out=hB[0:p, t, :], in0=ps[3 + t][0:p, 0:D], scalar=gates[0:p, t, ds(2 * r + s, 1)], in1=hB[0:p, t, :],
                                               op0=MULT, op1=ADD).then_inc(expert_added, 1)

        
        @block.tensor
        def _(pe):
            mm, tr = nc.tensor.matmul, nc.tensor.transpose

            for k in range(KP):
                if k % 2 == 0:
                    pe.wait_ge(patch_loaded[k // 2], 32)
                for t in range(NT):
                    ins = mm(ps[t][0:PAIR, 0:D], pat[:, k, PAIR * t:PAIR * (t + 1)], wpa[:, k, :], start=(k == 0), stop=(k == KP - 1))
                    if k == KP - 1:
                        ins.then_inc(embedded, 1)

            def turn_tokens(n0, tiles=range(NT)):
                for t in tiles:
                    pe.wait_ge(xn_ready, n0 + t + 1)
                    for k in range(2):
                        ins = tr(ps[t][0:H, k * PAIR:(k + 1) * PAIR], xn[:, t, k * H:(k + 1) * H], ident[0:PAIR, 0:PAIR])
                    ins.then_inc(x_turned, 1)

            pe.wait_ge(cst_loaded, 16)
            pe.wait_ge(hw_loaded, 16)
            pe.wait_ge(padded, PADS)
            for half in range(2):
                turn_tokens(0, range(4 * half, 4 * half + 4))
                pe.wait_ge(xT_ready, 4 * half + 4)
                for c in range(4):
                    for k in range(2):
                        ins = mm(ps[4 * half + c][0:H, 0:TH], hw[:, k, W_QKV + c * H:W_QKV + (c + 1) * H], xT[:, k, half * TH:(half + 1) * TH], start=(k == 0), stop=(k == 1))
                    ins.then_inc(qk_done, 1)
            pe.wait_ge(qk_saved, 8)
            pe.wait_ge(phi_sq, 1)
            for k in range(2):
                ins = mm(ps[7][:, 0:NE], ones[:, :], phin[:, k, :], start=(k == 0), stop=(k == 1))
            ins.then_inc(phi_sum, 1)
            for i in range(NT + 3):
                if i >= 3:
                    t = i - 3
                    pe.wait_ge(oT_ready, t + 1)
                    if t == 2:
                        pe.wait_ge(phi_ready, 1)
                    if t >= 4 and t % 2 == 0:
                        pe.wait_ge(an_ready, t // 2 - 1)
                    for k in range(2):
                        ins = mm(ps[6 + t // 2 % 2][0:PAIR, t % 2 * D:(t % 2 + 1) * D], oT[:, k, PAIR * t:PAIR * (t + 1)], hw[:, k, W_OUT:W_OUT + D], start=(k == 0), stop=(k == 1))
                    ins.then_inc(y_done, 1)
                if i < NT:
                    if i >= 1:
                        pe.wait_ge(vbd_ready, i)
                    pe.wait_ge(xR_ready, i + 1)
                    for b in range(2):
                        for k in range(2):
                            ins = mm(ps[3][0:3 * L, b * D:(b + 1) * D], xR[i % 2][:, k, b, :, :].rearrange("p r l -> p (r l)"), hw[:, k, W_QKV + 2 * D:W_QKV + 3 * D], start=(k == 0), stop=(k == 1))
                    ins.then_inc(v_done, 1)
                if 1 <= i <= NT:
                    t = i - 1
                    pe.wait_ge(exp_done, t + 1)
                    if t >= 1:
                        pe.wait_ge(pT_ready, t)
                    for g in range(4):
                        ins = tr(ps[2][0:3 * L, g * 128:(g + 1) * 128], prob[t % 2][:, 3 * g:3 * g + 3, :].rearrange("p h k -> p (h k)"), ident)
                    ins.then_inc(p_turned, 1)
                if i < NT:
                    pe.wait_ge(kbd_ready, i + 1)
                    if i >= 2:
                        pe.wait_ge(shifted, i - 1)
                    for b in range(2):
                        t0 = PAIR * i + L * b
                        for g in range(2):
                            ins = mm(ps[i % 2][64 * b:64 * b + 64, g * 6 * L:(g + 1) * 6 * L], qT[:, g, t0:t0 + 64], kbd[:, g, :, b * L:(b + 1) * L], start=True, stop=True)
                    ins.then_inc(scores_done, 1)
                if 1 <= i <= NT:
                    t = i - 1
                    pe.wait_ge(pT_ready, t + 1)
                    pe.wait_ge(vbd_ready, t + 1)
                    if t >= 1:
                        pe.wait_ge(o_ready, t)
                    for b in range(2):
                        for g in range(4):
                            ins = mm(ps[4][64 * b:64 * b + 64, g * 3 * HD:(g + 1) * 3 * HD], pT[:, g, 64 * b:64 * b + 64], vbd[t % 2][:, b, g * 3 * HD:(g + 1) * 3 * HD], start=True, stop=True)
                    ins.then_inc(av_done, 1)
                if 2 <= i < NT + 2:
                    t = i - 2
                    pe.wait_ge(o_ready, t + 1)
                    if t >= 1:
                        pe.wait_ge(oT_ready, t)
                    for k in range(2):
                        ins = tr(ps[5][0:H, k * 128:(k + 1) * 128], osb[:, k * H:(k + 1) * H], ident)
                    ins.then_inc(o_turned, 1)

            def slot_logits(half):
                turn_tokens(NT, range(4 * half, 4 * half + 4))
                pe.wait_ge(xT_ready, NT + 4 * half + 4)
                for k in range(2):
                    ins = mm(ps[half][0:NE, 0:TH], phin[:, k, :], xT[:, k, half * TH:(half + 1) * TH], start=(k == 0), stop=(k == 1))
                ins.then_inc(ld_done, 1)

            def token_logits(half):
                for t in range(4 * half, 4 * half + 4):
                    for k in range(2):
                        ins = mm(ps[2][0:PAIR, t * NE:(t + 1) * NE], xT[:, k, PAIR * t:PAIR * (t + 1)], phin[:, k, :], start=(k == 0), stop=(k == 1))
                ins.then_inc(lc_done, 1)

            def turn_dispatch(half):
                pe.wait_ge(d_ready, half + 1)
                for t in range(4 * half, 4 * half + 4):
                    ins = tr(ps[3][0:PAIR, t * NE:(t + 1) * NE], Ld[:, 2 * t:2 * t + 2, :].rearrange("p b m -> p (b m)"), ident[0:NE, 0:NE])
                ins.then_inc(d_turned, 1)

            def dispatch(half):
                pe.wait_ge(dbd_ready, half + 1)
                for c, p0, m, d0, e in XS_PARTS:
                    for t in range(4 * half, 4 * half + 4):
                        ins = mm(ps[XS_BANKS[half][c]][p0:p0 + m, t * NE:(t + 1) * NE], xn[:, t, d0:d0 + m], dbd[:, t, :, e:NE:2], start=True, stop=True)
                    ins.then_inc(xs_done, 1)

            slot_logits(0)
            token_logits(0)
            slot_logits(1)
            turn_dispatch(0)
            token_logits(1)
            dispatch(0)
            turn_dispatch(1)
            dispatch(1)
            pe.wait_ge(sm_shift, 3)
            pe.wait_ge(xs_ready, 8)

            def experts(r):
                for s in range(RING):
                    pe.wait_ge(w1_loaded[s], 16 * r + 16)
                    pe.wait_ge(xsq_ready, RING * r + s + 1)
                    for c in range(3):
                        for j in range(4):
                            a, fh = j // 2, j % 2
                            ins = mm(ps[s % 2][32 * j:32 * j + 32, 0:NFT * 128], XSq[s % 2][:, a, c, :], w1s[s][:, a, c, fh * NFT * 128:(fh + 1) * NFT * 128], start=(c == 0), stop=(c == 2))
                    ins.then_inc(h_done, 1)
                    pe.wait_ge(h_saved, RING * r + s + 1)
                    for t in range(NFT):
                        ins = tr(ps[2 + s % 2][:, t * 128:(t + 1) * 128], hs[s % 2][:, t * 128:(t + 1) * 128], ident)
                    ins.then_inc(h_turned, 1)
                    pe.wait_ge(w2_loaded[s], 16 * r + 16)
                    pe.wait_ge(gelu_done, RING * r + s + 1)
                    for fh in range(2):
                        for t in range(NFT):
                            for q in range(QUAD):
                                a = q // 2
                                g0 = 4 * a + 2 * fh
                                ins = mm(ps[4 + s % 2][32 * q:32 * q + 32, 0:D], hg[:, t, g0:g0 + 2, :].rearrange("p g b -> p (g b)"), w2s[s][:, q, fh * NFT + t, :],
                                         start=(fh == 0 and t == 0), stop=(fh == 1 and t == NFT - 1))
                    ins.then_inc(ys_done, 1)

            experts(0)
            pe.wait_ge(c_ready, 1)
            for t in range(NT):
                ins = tr(ps[6 + t // 4][:, (t % 4) * PAIR:(t % 4 + 1) * PAIR], cbd[:, t, :, :].rearrange("p b n -> p (b n)"), ident[0:PAIR, 0:PAIR])
                if t % 4 == 3:
                    ins.then_inc(c_turned, 1)
            with pe.Fori(1, ROUNDS) as r:
                experts(r)
            pe.wait_ge(cT_ready, 2)
            pe.wait_ge(ys_moved, 16 * YMOVE)
            for t in range(NT):
                dst = ps[COMB[t // 2]][0:PAIR, (t % 2) * D:(t % 2 + 1) * D]
                mm(dst, cT[:, t, :], b2[:, :], start=True, stop=False)
                ins = mm(dst, cT[:, t, :], ysn[:, t, :], start=False, stop=True)
                if t % 2:
                    ins.then_inc(comb_done, 1)

            turn_tokens(2 * NT)
            pe.wait_ge(xT_padded, 1)
            pe.wait_ge(xT_ready, 3 * NT)
            pe.wait_ge(scan_w_loaded, 16)
            for c in range(2 * CC):
                for half in range(2):
                    for k in range(2):
                        ins = mm(ps[c][64 * half:64 * half + 64, 0:TH], w_in[:, k, c, :], xT[:, k, half * TH:(half + 1) * TH], start=(k == 0), stop=(k == 1))
                ins.then_inc(in_done, 1)
            for c in range(CC):
                pe.wait_ge(u_ready, c + 1)
                ins = mm(ps[6][0:2 * XD, 0:TH], w_xp[:, c, :], u[:, c, :, :].rearrange("p b l -> p (b l)"), start=(c == 0), stop=(c == CC - 1))
            ins.then_inc(xd_done, 1)
            pe.wait_ge(xd_saved, 1)
            for c in range(CC):
                mm(ps[c][:, 0:TH], w_dt[:, c, :], xd, start=True, stop=True).then_inc(dt_done, 1)

            def spread(n):
                if n == 0:
                    pe.wait_ge(sel_ready, 1)
                if n >= 2:
                    pe.wait_ge(bc_saved, n - 1)
                mm(ps[6 + n % 2][:, 0:TH], sel[n], xd, start=True, stop=True).then_inc(bc_done, 1)

            sent = 0
            for k in range(NUNIT + 1):
                if k < NUNIT:
                    g, c = k // CC, k % CC
                    upto = 2 * NG * (g + 1) if c == 0 else sent
                    if g + 1 < NS // NG:
                        upto = min(2 * NG * (g + 2), 2 * NG * (g + 1) + (c + 1) * 3)
                    while sent < upto:
                        spread(sent)
                        sent += 1
                if k >= 1:
                    g, c = (k - 1) // CC, (k - 1) % CC
                    pe.wait_ge(hC_ready, k)
                    for j in range(NG):
                        ins = mm(ps[3 + c][:, 0:TH], ident, hC[(k - 1) % 2][:, j * TH:(j + 1) * TH],
                                 start=(g == 0 and j == 0), stop=(g == NS // NG - 1 and j == NG - 1))
                    ins.then_inc(h_used, 1)
            pe.wait_ge(z_ready, 2)
            for half in range(2):
                for t in range(TT):
                    if half == 0 and t == 3:
                        pe.wait_ge(bc_saved, 2 * NS)
                    if half == 1:
                        pe.wait_ge(yb_ready, CC)
                    chunks = range(CC, 2 * CC) if half == 0 else range(CC)
                    for c in chunks:
                        ins = mm(ps[SO[t]][:, 0:D], ybd[:, c, 128 * t:128 * (t + 1)], w_so[:, c, :], start=(c == CC), stop=(c == CC - 1))
                    if half == 1:
                        ins.then_inc(so_done, 1)

            pe.wait_ge(tk_ready, 1)
            for t in range(TT):
                for k in range(2):
                    ins = tr(ps[t][0:H, k * 128:(k + 1) * 128], tk[:, t, k * H:(k + 1) * H], ident)
                ins.then_inc(tk_turned, 1)
            pe.wait_ge(tkT_ready, TT)
            pe.wait_ge(tkT_padded, 1)
            for t in range(TT):
                for k in range(2):
                    ins = mm(ps[5][:, t * NX:(t + 1) * NX], tkT[:, k, 128 * t:128 * (t + 1)], hw[:, k, W_RT:W_RT + NX], start=(k == 0), stop=(k == 1))
            ins.then_inc(logit_done, 1)

            def up(s, rnd, e):
                pe.wait_ge(f1_loaded[s], 16 * rnd + 16)
                for n in range(12):
                    f, half = n // 2, n % 2
                    if not (isinstance(e, int) and e == 0 and n < 3):
                        pe.wait_ge(silu_done, 12 * e + (n - 2))
                    for k in range(2):
                        ins = mm(ps[n % 3][:, 0:TH], f1s[s][:, k, f * 128:(f + 1) * 128], tkT[:, k, half * TH:(half + 1) * TH], start=(k == 0), stop=(k == 1))
                    ins.then_inc(up_done, 1)

            def down(s, rnd, e):
                pe.wait_ge(f2_loaded[s], 16 * rnd + 16)
                pe.wait_ge(silu_done, 12 * e + 12)
                for t in range(TT):
                    m = 128 if t < TT - 1 else LAST
                    if isinstance(e, int) and e == 0:
                        if t == 2:
                            pe.wait_ge(rt_shift, 1)
                    else:
                        pe.wait_ge(expert_added, TT * e + (t - TT + 1))
                    for f in range(KF):
                        ins = mm(ps[3 + t][0:m, 0:D], gT[s][:, f, 128 * t:128 * t + m], f2s[s][:, f, :], start=(f == 0), stop=(f == KF - 1))
                    ins.then_inc(down_done, 1)

            up(0, 0, 0)
            up(1, 0, 1)
            down(0, 0, 0)
            with pe.Fori(0, NX // 2 - 1) as r:
                up(0, r + 1, 2 * r + 2)
                down(1, r, 2 * r + 1)
                up(1, r + 1, 2 * r + 3)
                down(0, r + 1, 2 * r + 2)
            down(1, NX // 2 - 1, NX - 1)


def layouts(x, L0_tok_W_proj, L0_tok_b_proj, L0_attn_w_qkv, L0_attn_w_out, L0_attn_b_out, L0_attn_ln_g, L0_attn_ln_b,
            L0_ffn_phi, L0_ffn_scale, L0_ffn_w1, L0_ffn_b1, L0_ffn_w2, L0_ffn_b2, L1_attn_in_proj_w, L1_attn_x_proj_w,
            L1_attn_dt_proj_w, L1_attn_dt_proj_b, L1_attn_A_log, L1_attn_D_param, L1_attn_out_proj_w, L1_attn_conv_x_w,
            L1_attn_conv_z_w, L1_ffn_ln_gamma, L1_ffn_ln_beta, L1_ffn_router_w, L1_ffn_w1, L1_ffn_w2):
    f4 = np.float32
    C = np.ascontiguousarray

    def halves(w, row=None):
        out = np.zeros((128, 2, w.shape[1]), f4)
        out[0:H] = w.reshape(2, H, -1).transpose(1, 0, 2)
        if row is not None:
            out[H, 1] = row
        return out

    patches = x.reshape(B, 3, 6, 16, 6, 16).transpose(1, 3, 5, 0, 2, 4).reshape(KP, 128, T).transpose(1, 0, 2)
    w_patch = L0_tok_W_proj.T.reshape(KP, 128, D).transpose(1, 0, 2)
    consts = np.zeros((128, C_W), f4)
    p = np.arange(128)
    consts[:, C_ID:C_ID + 128] = np.eye(128)
    consts[:, C_HEAD:C_HEAD + 6] = p[:, None] // HD == np.arange(6)
    consts[:, C_VM:C_VM + D] = p[:, None] // L == np.arange(D) // HD % 3
    consts[:, C_BM:C_BM + 2] = p[:, None] // L == np.arange(2)
    consts[:, C_IOTA:C_IOTA + NX] = np.arange(NX)
    half_w = np.concatenate([halves(L0_attn_w_qkv), halves(L0_attn_w_out, L0_attn_b_out), halves(L0_ffn_phi.reshape(D, NE)), halves(L1_ffn_router_w)], 2)
    rows = np.broadcast_to(np.stack([L0_tok_b_proj, L0_attn_ln_g, L0_attn_ln_b, L1_ffn_ln_gamma, L1_ffn_ln_beta]), (128, 5, D))

    def by_channel(w):
        w = w.reshape(CC, 64, -1).transpose(1, 0, 2).reshape(64, -1)
        return np.concatenate([w, w])

    cols = np.concatenate([by_channel(L1_attn_conv_x_w), by_channel(L1_attn_conv_z_w), by_channel(L1_attn_D_param), by_channel(L1_attn_dt_proj_b),
                           by_channel(L1_attn_A_log), np.broadcast_to(L0_ffn_scale, (128, 1))], 1)
    b1t = L0_ffn_b1.reshape(NQ, 2, 2, 2, NFT, 128).transpose(5, 0, 4, 1, 3, 2).reshape(128, NQ, NFT, 8)
    b2n = np.concatenate([L0_ffn_b2, L0_ffn_b2])
    scan_w = np.zeros((128, S_W), f4)
    scan_w[:, S_IN:S_IN + 768] = halves(L1_attn_in_proj_w.T).reshape(128, -1)
    xp = np.zeros((2, 64, CC, 2, XD), f4)
    dt = np.zeros((2, XD, CC, 2, 64), f4)
    for half in range(2):
        xp[half, :, :, half, :] = L1_attn_x_proj_w.reshape(XD, CC, 64).transpose(2, 1, 0)
        dt[half, 0:DTR, :, half, :] = L1_attn_dt_proj_w.reshape(CC, 64, DTR).transpose(2, 0, 1)
    scan_w[:, S_XP:S_XP + 264] = xp.reshape(128, -1)
    scan_w[0:2 * XD, S_DT:S_DT + 384] = dt.reshape(2 * XD, -1)
    scan_w[:, S_OUT:] = np.concatenate(
        [by_channel(L1_attn_out_proj_w.T[0:D]), by_channel(L1_attn_out_proj_w.T[D:2 * D])], 1)
    w1q = L0_ffn_w1.reshape(NQ, 2, 3, 128, FF).transpose(0, 3, 1, 2, 4).reshape(NQ, 128, -1)
    w2q = L0_ffn_w2.reshape(NQ, QUAD, KF, 128, D).transpose(0, 3, 1, 2, 4).reshape(NQ, 128, -1)
    f1 = np.stack([halves(w) for w in L1_ffn_w1])
    f2 = L1_ffn_w2.reshape(NX, KF, 128, D).transpose(0, 2, 1, 3)
    return dict(patches=C(patches), w_patch=C(w_patch), consts=consts, half_w=C(half_w), rows=C(rows), cols=C(cols), b1t=C(b1t), b2n=C(b2n),
                scan_w=scan_w, w1q=C(w1q), w2q=C(w2q), f1=C(f1), f2=C(f2))


def kernel(**inputs):
    import concourse.bacc as bacc
    from concourse.bass_utils import run_bass_kernel_spmd

    nc = bacc.Bacc("TRN2", target_bir_lowering=False, num_devices=1)
    arrays = layouts(**{k: np.asarray(v) for k, v in inputs.items()})
    names = {k: f"in_{k}_dram" for k in arrays}
    args = {k: nc.dram_tensor(names[k], a.shape, mybir.dt.from_np(a.dtype), kind="ExternalInput").ap() for k, a in arrays.items()}
    out = nc.dram_tensor("out_dram", (T, D), mybir.dt.float32, kind="ExternalOutput").ap()
    build_tower(nc, out=out, **args)
    r = run_bass_kernel_spmd(nc, [{names[k]: a for k, a in arrays.items()}], core_ids=[0])
    return r.results[0]["out_dram"].reshape(B, L, D)
```

```python
import numpy as np
import concourse.bass as bass
from concourse import mybir
from contextlib import ExitStack

B, L, D = 16, 36, 192
T = B * L
PD = 768
H = D // 2
NH, HD = 12, 16
NE, FF = 64, 768
NS, DTR, TAPS = 16, 12, 4
NX, TOPK = 8, 2
LN_EPS = 1e-5

LOG1P_MAX = 0.125
LOG1P = (0.15590593948099316, -0.2454479896579373, 0.3331359025735257, -0.4999969678046037, 0.9999999925054689)

RSQRT_GUESS = float(0x5F3759DF)

PAIR = 2 * L
NT = T // PAIR
KP = PD // 128
QUAD = 4
NQ = NE // QUAD
RING = 4
ROUNDS = NQ // RING
NFT = 3
KF = FF // 128
HALF = B // 2
TH = HALF * L
CC = D // 64
XD = DTR + 2 * NS
NG = 4
TT = 5
NSLOT = (T * TOPK + NX * 127) // 128
NB = 4
TP = TT * 128
LAST = T - (TT - 1) * 128

C_ID, C_HEAD, C_VM, C_BM, C_IOTA = 0, 128, 134, 326, 328
C_W = 336
W_QKV, W_OUT, W_PHI, W_RT, W_PHIS = 0, 3 * D, 4 * D, 4 * D + NE, 4 * D + NE + NX
W_W = 4 * D + NE + NX
R_BP, R_LG, R_LB, R_FG, R_FB = range(5)
K_CX, K_CZ, K_D, K_DT, K_AL, K_SC = 0, 12, 24, 27, 30, 78
K_W = 79
S_IN, S_XP, S_DT, S_OUT = 0, 768, 1032, 1416
S_TRI = S_OUT + 2 * CC * D
S_SLOT, S_THR = S_TRI + 128, S_TRI + 128 + NSLOT
S_W = S_THR + TT


def build_tower(nc, patches, w_patch, consts, half_w, rows, cols, b1t, b2n, scan_w, w1q, w2q, f1, f2, out):
    fp32 = mybir.dt.float32
    ALU = mybir.AluOpType
    ACT = mybir.ActivationFunctionType
    AX = mybir.AxisListType.X
    ds = bass.ds
    MULT, ADD, SUB, MAX = ALU.mult, ALU.add, ALU.subtract, ALU.max

    ctx = ExitStack()
    with ctx:
        def sb(name, shape, dt=fp32):
            return ctx.enter_context(nc.sbuf_tensor(name, shape, dt))

        def sem(name):
            return ctx.enter_context(nc.semaphore(name))

        ring = [sb(f"ring{s}", [128, 2 * QUAD * KF * D]) for s in range(RING)]
        W1N = QUAD * KF * D
        w1s = [r[:, 0:W1N].rearrange("p (a c f) -> p a c f", a=2, c=3) for r in ring]
        w2s = [r[:, W1N:2 * W1N].rearrange("p (q k d) -> p q k d", q=QUAD, k=KF) for r in ring]
        cst = sb("cst", [128, C_W])
        ident = cst[:, C_ID:C_ID + 128]
        hw = sb("hw", [128, 2, W_W])
        row = sb("row", [128, 5, D])
        col = sb("col", [128, K_W])
        b1 = sb("b1", [128, NQ, NFT, 8])
        b2 = sb("b2", [128, D])
        hA = sb("hA", [PAIR, NT, D])
        ones = sb("ones", [128, 128])
        phin = sb("phin", [128, 2, NE])
        bn = sb("bn", [128, NT, 6])
        mv = sb("mv", [128, NT, 2])
        rs = [sb(f"rs{k}", [128, 64]) for k in range(5)]
        mxs = sb("mxs", [128, 4, NH])
        ar = sb("ar", [128, 10264])

        pat = ring[3][:, 0:KP * T].rearrange("p (k t) -> p k t", k=KP)
        wpa = ring[3][:, KP * T:KP * (T + D)].rearrange("p (k d) -> p k d", k=KP)

        def view(first, end, pattern=None, rows_=128, **kw):
            v = ar[0:rows_, first:end]
            return v.rearrange(pattern, **kw) if pattern else v

        xn = view(0, 1536, "p (t d) -> p t d", rows_=PAIR, t=NT)
        ysn = view(0, 1536, "p (t d) -> p t d", t=NT)
        xT = view(1536, 2688, "p (k t) -> p k t", k=2)
        TQ = T + 28
        qT = view(2688, 2688 + 2 * TQ, "p (k t) -> p k t", k=2)
        kT = view(3896, 5048, "p (k t) -> p k t", rows_=H, k=2)
        kbd = view(5048, 5912, "p (g h t) -> p g h t", g=2, h=6)
        xR = [view(5912 + 432 * n, 6344 + 432 * n, "p (k b r l) -> p k b r l", k=2, b=2, r=3) for n in range(2)]
        prob = [view(6776 + 432 * n, 7208 + 432 * n, "p (h k) -> p h k", h=NH) for n in range(2)]
        pT = view(7640, 8152, "p (g t) -> p g t", g=4)
        vbd = [view(8152 + 384 * n, 8536 + 384 * n, "p (b d) -> p b d", b=2) for n in range(2)]
        osb = view(8920, 9112)
        oT = view(9112, 10264, "p (k t) -> p k t", k=2)
        XS = view(1536, 4608, "p (a c e b) -> p a c e b", a=NE // 2, c=3, e=2)
        Lc = view(4608, 5120, "p (t n) -> p t n", rows_=PAIR, t=NT)
        Ld = view(5120, 5696, "p (b m) -> p b m", rows_=NE, b=B)
        cbd = view(6464, 7488, "p (t b n) -> p t b n", rows_=PAIR, t=NT, b=2)
        dbd = view(8192, 9216, "p (t b n) -> p t b n", rows_=PAIR, t=NT, b=2)
        cT = view(9216, 9792, "p (t m) -> p t m", t=NT)
        XSq = [view(9792 + 192 * n, 9984 + 192 * n, "p (a c m) -> p a c m", a=2, c=3) for n in range(2)]
        hs = [view(7680 + 384 * n, 8064 + 384 * n) for n in range(2)]
        hb = view(8448, 8832, "p (t g b) -> p t g b", t=NFT, g=8)
        hg = view(8832, 9216, "p (t g b) -> p t g b", t=NFT, g=8)
        ysb = view(5696, 5696 + RING * D, "p (s d) -> p s d", s=RING)
        sw = ring[1][:, 0:S_W]
        w_in = sw[:, S_IN:S_IN + 768].rearrange("p (k c d) -> p k c d", k=2, c=2 * CC)
        w_xp = sw[:, S_XP:S_XP + 264].rearrange("p (c e) -> p c e", c=CC)
        w_dt = sw[0:2 * XD, S_DT:S_DT + 384].rearrange("p (c d) -> p c d", c=CC)
        w_so = sw[:, S_OUT:S_OUT + 2 * CC * D].rearrange("p (c d) -> p c d", c=2 * CC)
        o1 = [S_W]

        def slot1(n, p=128):
            o1[0] += n
            return ring[1][0:p, o1[0] - n:o1[0]]

        u = slot1(CC * TH).rearrange("p (c b l) -> p c b l", c=CC, b=HALF)
        du = slot1(CC * TH).rearrange("p (c t) -> p c t", c=CC)
        delta = slot1(CC * TH).rearrange("p (c t) -> p c t", c=CC)
        sp = [slot1(CC * TH).rearrange("p (c t) -> p c t", c=CC) for _ in range(3)]
        xd = slot1(TH, 2 * XD)
        negA = slot1(CC * NS)
        assert o1[0] <= 2 * W1N
        zr = view(9216, 9216 + CC * TH, "p (c b l) -> p c b l", c=CC, b=HALF)
        ybd = view(2688, 2688 + 2 * CC * TP, "p (c t) -> p c t", c=2 * CC)
        zc = view(6528, 6528 + CC * TH, "p (c b l) -> p c b l", c=CC, b=HALF)
        ztmp = view(7392, 7392 + CC * TH, "p (c b l) -> p c b l", c=CC, b=HALF)
        sel = [ring[s][0:2 * XD, a + 128 * n:a + 128 * (n + 1)] for s, a, m in ((0, 5376, 30), (1, o1[0], 2)) for n in range(m)]
        Bb = ring[2][:, 0:NS * TH].rearrange("p (n t) -> p n t", n=NS)
        Cb = ring[2][:, NS * TH:2 * NS * TH].rearrange("p (n t) -> p n t", n=NS)
        GW = NG * TH
        dA = [ring[3][:, n * GW:(n + 1) * GW] for n in range(2)]
        dBu = [ring[3][:, (2 + n) * GW:(3 + n) * GW] for n in range(2)]
        hst = [ring[3][:, (4 + n) * GW:(5 + n) * GW] for n in range(2)]
        hC = [ring[3][:, (6 + n) * GW:(7 + n) * GW] for n in range(2)]
        hB = view(8256, 8256 + TT * D, "p (t d) -> p t d", t=TT)
        at = [(ring[0], 0), (ring[0], 2688), (ring[0], 5376), (ring[3], 4608)]
        f1s = [r[:, a:a + 1536].rearrange("p (k f) -> p k f", k=2) for r, a in at]
        f2s = [r[:, a + 1536:a + 2688].rearrange("p (k d) -> p k d", k=KF) for r, a in at]
        gT = [ring[3][:, n * KF * 128:(n + 1) * KF * 128].rearrange("p (f t) -> p f t", f=KF) for n in range(2)]
        tk = ring[2][:, 0:TT * D].rearrange("p (t d) -> p t d", t=TT)
        tkT = ring[2][:, 1000:1000 + 2 * TP].rearrange("p (k t) -> p k t", k=2)
        slx = [ring[2][:, 3000 + D * b:3000 + D * (b + 1)] for b in range(NB)]
        sly = [ring[2][:, 3800 + D * b:3800 + D * (b + 1)] for b in range(NB)]
        slT = [ring[2][:, 4600 + 256 * n:4600 + 256 * (n + 1)].rearrange("p (k t) -> p k t", k=2) for n in range(2)]
        yg = ring[2][:, 5120:5120 + TT * TOPK * D].rearrange("p (t k d) -> p t k d", t=TT, k=TOPK)
        rt = [ring[2][:, 2400 + 40 * n:2440 + 40 * n].rearrange("p (t e) -> p t e", t=TT) for n in range(8)]
        ridx = sb("ridx", [128, TT, 8], mybir.dt.uint32)
        tiles_of, tiles_to, first_tile = (ring[2][:, 2720 + NX * n:2720 + NX * (n + 1)] for n in range(3))
        place_f = [ring[2][:, 2744 + TT * n:2744 + TT * (n + 1)] for n in range(TOPK)]
        place = ring[2][:, 2760:2760 + TOPK * TT].bitcast(mybir.dt.uint32).rearrange("p (k t) -> p k t", k=TOPK)
        slot_cmp = ring[2][0:1, 2780:2780 + NSLOT * NX].rearrange("p (s e) -> p s e", s=NSLOT)
        slot_f = ring[2][0:1, 2910:2910 + NSLOT]
        slot_expert = ring[2][0:1, 2930:2930 + NSLOT].bitcast(mybir.dt.uint32)
        tri = ring[1][:, S_TRI:S_TRI + 128]
        slot_no = ring[1][0:1, S_SLOT:S_SLOT + NSLOT]
        thresholds = ring[1][:, S_THR:S_THR + TT]

        ps = [ctx.enter_context(nc.psum_tensor(f"ps{k}", [128, 512], fp32)) for k in range(8)]

        patch_loaded = [sem(f"patch_loaded{k}") for k in range(3)]
        cst_loaded, hw_loaded, row_loaded, col_loaded = map(sem, ("cst_loaded", "hw_loaded", "row_loaded", "col_loaded"))
        padded, xT_padded, tkT_padded, sel_ready = map(sem, ("padded", "xT_padded", "tkT_padded", "sel_ready"))
        bias_loaded, scan_w_loaded = sem("bias_loaded"), sem("scan_w_loaded")
        w1_loaded = [sem(f"w1_loaded{s}") for s in range(RING)]
        w2_loaded = [sem(f"w2_loaded{s}") for s in range(RING)]
        ys_stored = [sem(f"ys_stored{s}") for s in range(RING)]
        f1_loaded = [sem(f"f1_loaded{s}") for s in range(NB)]
        f2_loaded = [sem(f"f2_loaded{s}") for s in range(NB)]
        slx_loaded = [sem(f"slx_loaded{s}") for s in range(NB)]
        rows_gathered = [sem(f"rows_gathered{t}") for t in range(TT)]
        sly_stored = [sem(f"sly_stored{s}") for s in range(NB)]
        ys_moved, resid_moved, out_stored = map(sem, ("ys_moved", "resid_moved", "out_stored"))
        (dve_step, act_step, pool_step, embedded, xn_ready, x_turned, xT_ready) = map(sem, (
            "dve_step", "act_step", "pool_step", "embedded", "xn_ready", "x_turned", "xT_ready"))
        (qk_done, qk_saved, xR_ready, kbd_ready, v_done, vbd_ready, scores_done, shifted, exp_done, p_turned, pT_ready,
         av_done, o_ready, o_turned, oT_ready, y_done, an_ready, h1_ready) = map(sem, (
            "qk_done", "qk_saved", "xR_ready", "kbd_ready", "v_done", "vbd_ready", "scores_done", "shifted", "exp_done",
            "p_turned", "pT_ready", "av_done", "o_ready", "o_turned", "oT_ready", "y_done", "an_ready", "h1_ready"))
        (phi_sq, phi_sum, phi_ready, ld_done, lc_done, sm_shift, sm_exp, d_ready, d_turned, dbd_ready, c_ready,
         c_turned, cT_ready, xs_done, xs_zero, xs_ready) = map(sem, (
            "phi_sq", "phi_sum", "phi_ready", "ld_done", "lc_done", "sm_shift", "sm_exp", "d_ready", "d_turned",
            "dbd_ready", "c_ready", "c_turned", "cT_ready", "xs_done", "xs_zero", "xs_ready"))
        (xsq_ready, h_done, h_saved, h_turned, b1_added, gelu_done, ys_done, ys_ready, comb_done, hA_ready) = map(sem, (
            "xsq_ready", "h_done", "h_saved", "h_turned", "b1_added", "gelu_done", "ys_done", "ys_ready",
            "comb_done", "hA_ready"))
        (in_done, z_saved, conv_ready, zconv_ready, u_ready, xd_done, xd_saved, dt_done, sp_t, sp_act, bc_done,
         bc_saved, dA_zeroed, negA_ready, delta_ready, dA_ready, scan_done, h_used, hC_ready, z_ready, ybd_zero, yb_ready,
         so_done) = map(sem, (
            "in_done", "z_saved", "conv_ready", "zconv_ready", "u_ready", "xd_done", "xd_saved", "dt_done", "sp_t",
            "sp_act", "bc_done", "bc_saved", "dA_zeroed", "negA_ready", "delta_ready", "dA_ready", "scan_done", "h_used", "hC_ready",
            "z_ready", "ybd_zero", "yb_ready", "so_done"))
        (hB_pad, tk_ready, tk_turned, tkT_ready, logit_done, rt_shift, rt_exp, chosen, ranked, slots_known, places_ready,
         rows_filled, rows_scattered, slx_turned, slT_ready, up_done, silu_done, down_done, sly_ready,
         token_done, routed_padded) = map(sem, (
            "hB_pad", "tk_ready", "tk_turned", "tkT_ready", "logit_done", "rt_shift", "rt_exp", "chosen", "ranked", "slots_known",
            "places_ready", "rows_filled", "rows_scattered", "slx_turned", "slT_ready", "up_done", "silu_done", "down_done",
            "sly_ready", "token_done", "routed_padded"))

        ys_dram = nc.dram_tensor("ys_dram", (NE, B, D), fp32, kind="Internal").ap()
        slots_in = nc.dram_tensor("slots_in", (NSLOT * 128, D), fp32, kind="Internal").ap()
        slots_out = nc.dram_tensor("slots_out", (NSLOT * 128, D), fp32, kind="Internal").ap()
        NUNIT = (NS // NG) * CC
        PADS = 8
        COMB = (0, 1, 4, 5)
        SO = (0, 1, 2, 6, 7)
        XS_BANKS = ((4, 5, 6), (7, 0, 1))
        XS_PARTS = ((0, 0, 128, 0, 0), (1, 0, 64, 128, 0), (1, 64, 64, 0, 1), (2, 0, 128, 64, 1))

        def slot_inputs(half, n):
            c, p0, m, _, e = XS_PARTS[n]
            bs = slice(half * HALF, (half + 1) * HALF)
            return (XS[p0:p0 + m, :, c, e, bs].rearrange("p a b -> p b a"), ps[XS_BANKS[half][c]][p0:p0 + m, half * 4 * NE:(half + 1) * 4 * NE].rearrange("p (b a) -> p b a", b=HALF))

        block = ctx.enter_context(nc.Block())

        @block.sync
        def _(sp_):
            for k in range(3):
                sp_.dma_start(wpa[:, 2 * k:2 * k + 2, :], w_patch[:, 2 * k:2 * k + 2, :]).then_inc(patch_loaded[k], 16)
                sp_.dma_start(pat[:, 2 * k:2 * k + 2, :], patches[:, 2 * k:2 * k + 2, :]).then_inc(patch_loaded[k], 16)
            sp_.dma_start(row[:, :, :], rows).then_inc(row_loaded, 16)
            sp_.dma_start(hw[:, :, :], half_w).then_inc(hw_loaded, 16)
            sp_.dma_start(col[:, :], cols).then_inc(col_loaded, 16)
            sp_.dma_start(b1[:, :, :, :], b1t).then_inc(bias_loaded, 16)
            sp_.dma_start(b2[:, :], b2n).then_inc(bias_loaded, 16)

            def load_quad(s, quad):
                sp_.dma_start(ring[s][:, 0:W1N], w1q[quad, :, :]).then_inc(w1_loaded[s], 16)
                sp_.dma_start(ring[s][:, W1N:2 * W1N], w2q[quad, :, :]).then_inc(w2_loaded[s], 16)

            def store_ys(s, quad):
                sp_.wait_ge(ys_ready, quad + 1)
                for q in range(QUAD):
                    p0 = 32 * q + B * (q % 2)
                    sp_.dma_start(ys_dram[ds(QUAD * quad + q, 1), :, :].rearrange("a b d -> (a b) d"), ysb[p0:p0 + B, s, :]).then_inc(ys_stored[s], 16)

            def load_ys(n0, n1):
                for s in range(RING):
                    sp_.wait_ge(ys_stored[s], 16 * n1 // RING)
                for odd in range(2):
                    sp_.dma_start(ysn[64 * odd + n0:64 * odd + n1, :, :], ys_dram[n0:n1, odd:B:2, :]).then_inc(ys_moved, 16)

            for s in range(RING):
                if s == RING - 1:
                    sp_.wait_ge(embedded, NT)
                load_quad(s, s)
            sp_.wait_ge(padded, 1)
            sp_.dma_start(slots_in.rearrange("(p a) d -> p (a d)", p=128).rearrange("p (k n) -> p k n", n=128),
                          ones[:, :].rearrange("p (a n) -> p a n", a=1).to_broadcast([128, NSLOT * D // 128, 128])).then_inc(rows_filled, 16)
            with sp_.Fori(0, ROUNDS - 1) as r:
                for s in range(RING):
                    sp_.wait_ge(h_done, RING * r + s + 1)
                    sp_.dma_start(ring[s][:, 0:W1N], w1q[ds(RING * r + (RING + s), 1), :, :].rearrange("a p n -> (a p) n")).then_inc(w1_loaded[s], 16)
                    sp_.wait_ge(ys_done, RING * r + s + 1)
                    sp_.dma_start(ring[s][:, W1N:2 * W1N], w2q[ds(RING * r + (RING + s), 1), :, :].rearrange("a p n -> (a p) n")).then_inc(w2_loaded[s], 16)
                    store_ys(s, RING * r + s)
            sp_.wait_ge(ys_done, NQ - 2)
            sp_.dma_start(ring[1][:, 0:S_W], scan_w).then_inc(scan_w_loaded, 16)
            load_ys(0, NE - QUAD * RING)
            for s in range(RING):
                store_ys(s, NQ - RING + s)
            load_ys(NE - QUAD * RING, NE)
            sp_.wait_ge(hA_ready, 2)
            n = 0
            for t in range(NT):
                a, end = PAIR * t, PAIR * (t + 1)
                while a < end:
                    m = min(end, (a // 128 + 1) * 128) - a
                    sp_.dma_start(hB[a % 128:a % 128 + m, a // 128, :], hA[a - PAIR * t:a - PAIR * t + m, t, :]).then_inc(resid_moved, 16)
                    a += m
                    n += 1
            def load_weights(b, slot):
                e = sp_.value_load(slot_expert[0:1, ds(slot, 1)], min_val=0, max_val=NX - 1)
                yield sp_.dma_start(f1s[b][0:H], f1[ds(e, 1), :, :, :].rearrange("a p k n -> (a p) k n")).then_inc(f1_loaded[b], 16)
                yield sp_.dma_start(f2s[b], f2[ds(e, 1), :, :, :].rearrange("a p k n -> (a p) k n")).then_inc(f2_loaded[b], 16)

            def load_tokens(b, slot):
                sp_.dma_start(slx[b], slots_in[ds(128 * slot, 128), :]).then_inc(slx_loaded[b], 16)

            def store_outputs(b, slot):
                sp_.wait_ge(sly_ready, slot + 1)
                sp_.dma_start(slots_out[ds(128 * slot, 128), :], sly[b]).then_inc(sly_stored[b], 16)

            sp_.wait_ge(slots_known, 1)
            for b in range(NB):
                for _ in load_weights(b, b):
                    pass
            sp_.wait_ge(rows_scattered, 16 * TOPK * TT)
            for b in range(NB):
                load_tokens(b, b)
            with sp_.Fori(0, NSLOT // NB - 1) as r:
                for b in range(NB):
                    slot = NB * r + b
                    sp_.wait_ge(up_done, 2 * slot + 2)
                    load_tokens(b, slot + NB)
                    layers = load_weights(b, slot + NB)
                    next(layers)
                    sp_.wait_ge(down_done, slot + 1)
                    next(layers)
                    store_outputs(b, slot)
            for b in range(NB):
                store_outputs(b, NSLOT - NB + b)
            for t in range(TT):
                m = 128 if t < TT - 1 else LAST
                sp_.wait_ge(token_done, t + 1)
                sp_.dma_start(out[128 * t:128 * t + m, :], hB[0:m, t, :]).then_inc(out_stored, 16)
            sp_.wait_ge(out_stored, 16 * TT)

        NMOVE = 0
        for t in range(NT):
            a, end = PAIR * t, PAIR * (t + 1)
            while a < end:
                a += min(end, (a // 128 + 1) * 128) - a
                NMOVE += 1
        YMOVE = 4

        @block.gpsimd
        def _(gp):
            gp.memset(ones[:, :], 1.0).then_inc(padded, 1)
            gp.wait_ge(padded, 1)
            for first, end, value in ((1536, 3896, 1.0), (9112, 10264, 1.0), (5048, 5912, 0.0), (5912, 6776, 1.0), (7640, 8152, 1.0), (8152, 8920, 0.0)):
                gp.memset(ar[96:128, first:end], value).then_inc(padded, 1)
            gp.wait_ge(padded, PADS - 1)
            gp.memset(qT[0:H, :, T:TQ], 0.0).then_inc(padded, 1)
            gp.wait_ge(padded, PADS)
            gp.wait_ge(cst_loaded, 16)
            steps = 0

            def pool_link(ins):
                nonlocal steps
                ins.then_inc(pool_step, 1)
                steps += 1
                gp.wait_ge(pool_step, steps)

            def add_attention(g):
                two = slice(2 * g, 2 * g + 2)
                gp.wait_ge(an_ready, g + 1)
                pool_link(nc.gpsimd.tensor_tensor(xn[:, two, :], xn[:, two, :], row[0:PAIR, R_LG:R_LG + 1, :].to_broadcast([PAIR, 2, D]), MULT))
                pool_link(nc.gpsimd.tensor_tensor(xn[:, two, :], xn[:, two, :], row[0:PAIR, R_LB:R_LB + 1, :].to_broadcast([PAIR, 2, D]), ADD))
                nc.gpsimd.tensor_tensor(hA[:, two, :], hA[:, two, :], xn[:, two, :], ADD).then_inc(h1_ready, 1)

            gp.wait_ge(qk_saved, 8)
            for t in range(NT):
                if t == 6:
                    add_attention(0)
                if t >= 1:
                    gp.wait_ge(scores_done, t)
                for g in range(2):
                    ins = nc.gpsimd.tensor_tensor(
                        kbd[0:H, g, :, :],
                        kT[:, g:g + 1, PAIR * t:PAIR * (t + 1)].to_broadcast([H, 6, PAIR]),
                        cst[0:H, C_HEAD:C_HEAD + 6].rearrange("p (h a) -> p h a", a=1).to_broadcast([H, 6, PAIR]), MULT)
                ins.then_inc(kbd_ready, 1)
            for g in range(1, NT // 2 - 1):
                add_attention(g)
            gp.wait_ge(scores_done, NT)
            gp.wait_ge(h1_ready, 3)
            gp.memset(ar[:, 2688:4608], 0.0).then_inc(xs_zero, 1)
            gp.wait_ge(lc_done, 2)
            gp.memset(ar[:, 1536:2688], 0.0).then_inc(xs_zero, 1)
            gp.wait_ge(xs_ready, 8)
            gp.tensor_copy(XSq[0], XS[:, 0:2, :, :, :].rearrange("p a c e b -> p a c (e b)")).then_inc(xsq_ready, 1)
            gp.tensor_copy(XSq[1], XS[:, 2:4, :, :, :].rearrange("p a c e b -> p a c (e b)")).then_inc(xsq_ready, 1)
            with gp.Fori(0, (NQ - 2) // 2) as r:
                for s in range(2):
                    gp.wait_ge(h_done, 2 * r + s + 1)
                    gp.tensor_copy(XSq[s], XS[:, ds(4 * r + (4 + 2 * s), 2), :, :, :].rearrange("p a c e b -> p a c (e b)")).then_inc(xsq_ready, 1)
            gp.wait_ge(xsq_ready, NQ)
            gp.memset(ar[96:128, 1536:2688], 1.0).then_inc(xT_padded, 1)
            for n in range(2 * NS):
                if n in (0, 30):
                    gp.wait_ge(ys_done, NQ - 3 if n == 0 else NQ - 2)
                e = DTR + (n % 2) * NS + n // 2
                ins = nc.gpsimd.tensor_copy(sel[n].rearrange("p (b d) -> p b d", b=2), ident[0:2 * XD, e:XD + e + 1:XD].rearrange("p (b a) -> p b a", a=1).to_broadcast([2 * XD, 2, 64]))
            ins.then_inc(sel_ready, 1)
            gp.wait_ge(sel_ready, 1)
            gp.wait_ge(comb_done, 4)
            gp.memset(hB[LAST:128, TT - 1, :], 0.0).then_inc(hB_pad, 1)
            gp.wait_ge(hB_pad, 1)
            gp.memset(ybd[:, :, :], 0.0).then_inc(ybd_zero, 1)
            gp.wait_ge(ybd_zero, 1)
            for n in range(2):
                gp.memset(dA[n].rearrange("p (g l) -> p g l", l=L)[:, :, 0:1], 0.0).then_inc(dA_zeroed, 1)
            gp.wait_ge(z_saved, CC)
            for k in (1, 0, 2, 3):
                o = k - 1
                a, e = max(0, -o), L - max(0, o)
                dst = zc if k == 1 else ztmp
                for c in range(CC):
                    ins = nc.gpsimd.tensor_scalar(dst[:, c, :, a:e], zr[:, c, :, a + o:e + o], col[:, K_CZ + TAPS * c + k:K_CZ + TAPS * c + k + 1], None, MULT)
                pool_link(ins)
                if k != 1:
                    pool_link(nc.gpsimd.tensor_tensor(zc[:, :, :, a:e].rearrange("p c b l -> p (c b) l"), zc[:, :, :, a:e].rearrange("p c b l -> p (c b) l"), ztmp[:, :, :, a:e].rearrange("p c b l -> p (c b) l"), ADD))
            gp.memset(ztmp[0:1, 0, 0, 0:1], 0.0).then_inc(zconv_ready, 1)
            for b in range(NB - 1):
                gp.memset(f1s[b][96:128], 0.0).then_inc(routed_padded, 1)
            gp.wait_ge(yb_ready, CC)
            gp.memset(tkT[96:128, :, :], 1.0).then_inc(tkT_padded, 1)
            gp.memset(f1s[NB - 1][96:128], 0.0).then_inc(routed_padded, 1)
            for n in range(2):
                gp.memset(slT[n][96:128], 1.0).then_inc(routed_padded, 1)

            def each_choice():
                for t in range(TT):
                    m = 128 if t < TT - 1 else LAST
                    for k in range(TOPK):
                        yield t, k, m, bass.IndirectOffsetOnAxis(ap=place[0:m, k, t:t + 1], axis=0)

            gp.wait_ge(rows_filled, 16)
            gp.wait_ge(places_ready, 1)
            for t, k, m, where in each_choice():
                gp.indirect_dma_start(out=slots_in, out_offset=where, in_=tk[0:m, t, :], in_offset=None).then_inc(rows_scattered, 16)
            for b in range(NB):
                gp.wait_ge(sly_stored[b], 16 * NSLOT // NB)
            for t, k, m, where in each_choice():
                gp.indirect_dma_start(out=yg[0:m, t, k, :], out_offset=None, in_=slots_out, in_offset=where).then_inc(rows_gathered[t], 16)

        @block.scalar
        def _(act):
            A = nc.scalar.activation
            act.dma_start(cst[:, :], consts).then_inc(cst_loaded, 16)
            def save_turned(n0, tiles):
                for t in tiles:
                    act.wait_ge(x_turned, n0 + t + 1)
                    A(xT[0:H, :, PAIR * t:PAIR * (t + 1)], ps[t][0:H, 0:2 * PAIR].rearrange("p (k t) -> p k t", k=2), ACT.Copy).then_inc(xT_ready, 1)

            def triple(t):
                if t >= 2:
                    act.wait_ge(v_done, t - 1)
                for k in range(2):
                    ins = A(xR[t % 2][0:H, k, :, :, :], xT[0:H, k, PAIR * t:PAIR * (t + 1)].rearrange("p (b a l) -> p b a l", b=2, a=1).to_broadcast([H, 2, 3, L]), ACT.Copy)
                ins.then_inc(xR_ready, 1)

            act.wait_ge(padded, PADS)
            for half in range(2):
                save_turned(0, range(4 * half, 4 * half + 4))
                for c in (0, 2):
                    n = 4 * half + c
                    act.wait_ge(qk_done, n + 1)
                    A((qT if c < 2 else kT)[0:H, c % 2, half * TH:(half + 1) * TH], ps[n][0:H, 0:TH], ACT.Copy).then_inc(qk_saved, 1)
            act.wait_ge(xT_ready, NT)
            triple(0)
            for i in range(NT + 2):
                if 1 <= i <= NT:
                    t = i - 1
                    act.wait_ge(p_turned, t + 1)
                    if t >= 1:
                        act.wait_ge(av_done, t)
                    A(pT[0:3 * L], ps[2][0:3 * L, :].rearrange("p (g t) -> p g t", g=4), ACT.Copy).then_inc(pT_ready, 1)
                if i + 1 < NT:
                    triple(i + 1)
                if i < NT:
                    act.wait_ge(shifted, i + 1)
                    A(prob[i % 2], prob[i % 2], ACT.Exp, scale=HD ** -0.5).then_inc(exp_done, 1)
                if 2 <= i < NT + 2:
                    t = i - 2
                    act.wait_ge(o_turned, t + 1)
                    A(oT[0:H, :, PAIR * t:PAIR * (t + 1)].rearrange("p k (b l) -> p k b l", b=2),
                      ps[5][0:H, 0:256].rearrange("p (k b l) -> p k b l", k=2, b=2)[:, :, :, 0:L], ACT.Copy).then_inc(oT_ready, 1)
            save_turned(NT, range(NT))
            for half in range(2):
                act.wait_ge(sm_shift, half + 1)
                bs = slice(half * HALF, (half + 1) * HALF)
                A(Ld[:, bs, :], Ld[:, bs, :], ACT.Exp).then_inc(sm_exp, 1)
            act.wait_ge(xs_zero, 2)
            for half in range(2):
                for n in (0, 1):
                    act.wait_ge(xs_done, 4 * half + n + 1)
                    dst, src = slot_inputs(half, n)
                    A(dst, src, ACT.Copy).then_inc(xs_ready, 1)
            act.wait_ge(sm_shift, 3)
            A(Lc, Lc, ACT.Exp).then_inc(sm_exp, 1)

            def hidden(r):
                for s in range(RING):
                    act.wait_ge(h_done, RING * r + s + 1)
                    A(hs[s % 2], ps[s % 2][:, 0:NFT * 128], ACT.Copy).then_inc(h_saved, 1)
                    act.wait_ge(b1_added, RING * r + s + 1)
                    A(hg, hb, ACT.Gelu).then_inc(gelu_done, 1)

            hidden(0)
            for n in range(2):
                act.wait_ge(c_turned, n + 1)
                A(cT[:, 4 * n:4 * n + 4, :], ps[6 + n][:, 0:4 * PAIR].rearrange("p (t m) -> p t m", t=4), ACT.Copy).then_inc(cT_ready, 1)
            with act.Fori(1, ROUNDS) as r:
                hidden(r)
            save_turned(2 * NT, range(NT))
            A(negA, col[:, K_AL:K_AL + CC * NS], ACT.Exp).then_inc(act_step, 1)
            for c in range(CC):
                act.wait_ge(in_done, CC + c + 1)
                A(zr[:, c, :, :], ps[CC + c][:, 0:TH].rearrange("p (b l) -> p b l", b=HALF), ACT.Copy).then_inc(z_saved, 1)
            for c in range(CC):
                act.wait_ge(conv_ready, c + 1)
                A(u[:, c, :, :], u[:, c, :, :], ACT.Silu).then_inc(u_ready, 1)
            act.wait_ge(xd_done, 1)
            A(xd, ps[6][0:2 * XD, 0:TH], ACT.Copy).then_inc(xd_saved, 1)
            act.wait_ge(sp_t, 1)
            A(sp[1], sp[0], ACT.Abs).then_inc(sp_act, 1)
            act.wait_ge(sp_act, 1)
            A(sp[1], sp[1], ACT.Exp, scale=-1.0).then_inc(sp_act, 1)
            act.wait_ge(sp_act, 2)
            A(delta, sp[1], ACT.Ln, bias=1.0).then_inc(sp_act, 1)
            bc = [0]

            def save_bc(upto):
                while bc[0] < upto:
                    n = bc[0]
                    act.wait_ge(bc_done, n + 1)
                    A((Bb if n % 2 == 0 else Cb)[:, n // 2, :], ps[6 + n % 2][:, 0:TH], ACT.Copy).then_inc(bc_saved, 1)
                    bc[0] += 1

            act.wait_ge(dA_zeroed, 2)
            act.wait_ge(negA_ready, 1)
            save_bc(2 * NG)
            act.wait_ge(delta_ready, 1)
            for k in range(NUNIT):
                g, c = k // CC, k % CC
                if k >= 2:
                    act.wait_ge(scan_done, k - 1)
                for j in range(NG):
                    n = NG * g + j
                    dst = dA[k % 2][:, j * TH:(j + 1) * TH].rearrange("p (b l) -> p b l", b=HALF)[:, :, 1:L]
                    ins = A(dst, delta[:, c, :].rearrange("p (b l) -> p b l", b=HALF)[:, :, 1:L], ACT.Exp, scale=negA[:, CC * 0 + NS * c + n:NS * c + n + 1])
                ins.then_inc(dA_ready, 1)
                if g + 1 < NS // NG:
                    save_bc(min(2 * NG * (g + 2), 2 * NG * (g + 1) + (c + 1) * 3))
            act.wait_ge(zconv_ready, 1)
            act.wait_ge(ybd_zero, 1)
            for half in range(2):
                p0 = 64 * half
                A(ybd[p0:p0 + 64, CC:2 * CC, half * TH:(half + 1) * TH], zc[p0:p0 + 64, :, :, :].rearrange("p c b l -> p c (b l)"), ACT.Silu).then_inc(z_ready, 1)
            for t in range(TT):
                act.wait_ge(tk_turned, t + 1)
                A(tkT[0:H, :, 128 * t:128 * (t + 1)], ps[t][0:H, 0:256].rearrange("p (k t) -> p k t", k=2), ACT.Copy).then_inc(tkT_ready, 1)
            act.wait_ge(rt_shift, 1)
            A(rt[1], rt[0], ACT.Exp).then_inc(rt_exp, 1)

            def hidden_rows(slot, n):
                act.wait_ge(up_done, 2 * slot + 1)
                if not (isinstance(slot, int) and slot < 2):
                    act.wait_ge(down_done, slot - 1)
                A(gT[n][:, 0:4, :], ps[2 + 2 * n][:, :].rearrange("p (f t) -> p f t", f=4), ACT.Silu).then_inc(silu_done, 1)
                act.wait_ge(up_done, 2 * slot + 2)
                A(gT[n][:, 4:6, :], ps[3 + 2 * n][:, 0:256].rearrange("p (f t) -> p f t", f=2), ACT.Silu).then_inc(silu_done, 1)

            for n in range(2):
                hidden_rows(n, n)
            with act.Fori(1, NSLOT // 2) as r:
                for n in range(2):
                    hidden_rows(2 * r + n, n)

        @block.vector
        def _(dve):
            V = nc.vector
            chain = [0]

            def link(ins):
                ins.then_inc(dve_step, 1)
                chain[0] += 1
                dve.wait_ge(dve_step, chain[0])

            def rsqrt(p, n, first=0):
                z, t, y = (rs[k][0:p, first:first + n] for k in (0, 4, 3))
                link(V.tensor_scalar(y.bitcast(mybir.dt.int32), z.bitcast(mybir.dt.int32), -0.5, RSQRT_GUESS, MULT, ADD))
                for _ in range(3):
                    link(V.tensor_tensor(t, y, y, MULT))
                    link(V.scalar_tensor_tensor(out=t, in0=t, scalar=-0.5, in1=z, op0=MULT, op1=MULT))
                    link(V.scalar_tensor_tensor(out=y, in0=t, scalar=1.5, in1=y, op0=ADD, op1=MULT))

            def statistics(x, p, t0, n):
                for t in range(n):
                    ins = V.bn_stats(bn[0:p, t0 + t, :], x[:, t, :])
                link(ins)
                for t in range(n):
                    ins = V.bn_aggr(mv[0:p, t0 + t, :], bn[0:p, t0 + t, :])
                link(ins)

            def deviations(x, p, t0, n):
                statistics(x, p, t0, n)
                link(V.tensor_scalar(rs[0][0:p, t0:t0 + n], mv[0:p, t0:t0 + n, 1], LN_EPS, None, ADD))
                rsqrt(p, n, t0)

            def normalise(dst, x, p, t0, n):
                for t in range(n):
                    yield V.tensor_scalar(dst[:, t, :], x[:, t, :], mv[0:p, t0 + t, 0:1], rs[3][0:p, t0 + t:t0 + t + 1], SUB, MULT)

            def norm_in_halves(produce):
                n = NT // 2
                for half in range(2):
                    four = slice(half * n, (half + 1) * n)
                    produce(half)
                    deviations(hA[:, four, :], PAIR, half * n, n)
                    for ins in normalise(xn[:, four, :], hA[:, four, :], PAIR, half * n, n):
                        ins.then_inc(xn_ready, 1)

            def rowof(k, p, n):
                return row[0:p, k:k + 1, :].to_broadcast([p, n, D])

            dve.wait_ge(row_loaded, 16)

            def embedding(half):
                for t in range(4 * half, 4 * half + 4):
                    dve.wait_ge(embedded, t + 1)
                    ins = V.tensor_tensor(hA[:, t, :], ps[t][0:PAIR, 0:D], row[0:PAIR, R_BP, :], ADD)
                link(ins)

            norm_in_halves(embedding)
            dve.wait_ge(hw_loaded, 16)
            phi = hw[:, :, W_PHI:W_PHI + NE]
            V.tensor_tensor(phin[:, :, :], phi, phi, MULT).then_inc(phi_sq, 1)

            def unit_rows(t0, n):
                dve.wait_ge(h1_ready, min((t0 + n) // 2, 3))
                x = hA[:, t0:t0 + n, :]
                statistics(x, PAIR, t0, n)
                var, z = mv[0:PAIR, t0:t0 + n, 1], rs[0][0:PAIR, t0:t0 + n]
                link(V.tensor_scalar(z, var, LN_EPS, 1e-24, ADD, MULT))
                link(V.scalar_tensor_tensor(out=z, in0=var, scalar=float(D), in1=z, op0=MULT, op1=MAX))
                rsqrt(PAIR, n, t0)
                for ins in normalise(xn[:, t0:t0 + n, :], x, PAIR, t0, n):
                    ins.then_inc(xn_ready, 1)

            dve.wait_ge(padded, PADS)
            for half in range(2):
                for c in (1, 3):
                    n = 4 * half + c
                    dve.wait_ge(qk_done, n + 1)
                    V.tensor_copy((qT if c < 2 else kT)[0:H, c % 2, half * TH:(half + 1) * TH], ps[n][0:H, 0:TH]).then_inc(qk_saved, 1)
            for i in range(NT + 3):
                if i < NT:
                    dve.wait_ge(v_done, i + 1)
                    if i >= 2:
                        dve.wait_ge(av_done, i - 1)
                    V.tensor_tensor(vbd[i % 2][0:3 * L], ps[3][0:3 * L, 0:2 * D].rearrange("p (b d) -> p b d", b=2),
                                    cst[0:3 * L, C_VM:C_VM + D].rearrange("p (a d) -> p a d", a=1).to_broadcast([3 * L, 2, D]), MULT).then_inc(vbd_ready, 1)
                    dve.wait_ge(scores_done, i + 1)
                    s3 = ps[i % 2][:, 0:NH * L].rearrange("p (h k) -> p h k", h=NH)
                    link(V.tensor_reduce(mxs[:, 0, :], s3, AX, MAX))
                    if i >= 2:
                        dve.wait_ge(p_turned, i - 1)
                    V.tensor_tensor(prob[i % 2], s3, mxs[:, 0, :].rearrange("p (h a) -> p h a", a=1).to_broadcast([128, NH, L]), SUB).then_inc(shifted, 1)
                if i == 1:
                    dve.wait_ge(phi_sum, 1)
                    link(V.tensor_scalar(rs[0][:, 0:NE], ps[7][:, 0:NE], 1e-24, None, MAX))
                    rsqrt(128, NE)
                    dve.wait_ge(col_loaded, 16)
                    link(V.tensor_scalar(rs[3][:, 0:NE], rs[3][:, 0:NE], col[:, K_SC:K_SC + 1], None, MULT))
                    V.tensor_tensor(phin[:, :, :], phi, rs[3][:, 0:NE].rearrange("p (a n) -> p a n", a=1).to_broadcast([128, 2, NE]), MULT).then_inc(phi_ready, 1)
                g = (i - 4) // 2
                if 1 <= i <= NT:
                    t = i - 1
                    dve.wait_ge(av_done, t + 1)
                    if t >= 1:
                        dve.wait_ge(o_turned, t)
                    V.tensor_tensor(osb.rearrange("p (h d) -> p h d", h=NH), ps[4][:, 0:D].rearrange("p (h d) -> p h d", h=NH),
                                    mxs[:, 2 + t % 2, :].rearrange("p (h a) -> p h a", a=1).to_broadcast([128, NH, HD]), MULT).then_inc(o_ready, 1)
                if i >= 4 and i % 2 == 0:
                    dve.wait_ge(y_done, 2 * g + 2)
                    y2 = ps[6 + g % 2][0:PAIR, 0:2 * D].rearrange("p (t d) -> p t d", t=2)
                    deviations(y2, PAIR, 2 * g, 2)
                    for ins in normalise(xn[:, 2 * g:2 * g + 2, :], y2, PAIR, 2 * g, 2):
                        pass
                    ins.then_inc(an_ready, 1)
                if i < NT:
                    dve.wait_ge(exp_done, i + 1)
                    link(V.tensor_reduce(mxs[:, 1, :], prob[i % 2], AX, ADD))
                    link(V.reciprocal(mxs[:, 2 + i % 2, :], mxs[:, 1, :]))
                if i >= 7 and i % 2 == 1:
                    unit_rows(i - 7, 2)
            two = slice(NT - 2, NT)
            dve.wait_ge(an_ready, NT // 2)
            link(V.tensor_tensor(xn[:, two, :], xn[:, two, :], rowof(R_LG, PAIR, 2), MULT))
            link(V.tensor_tensor(xn[:, two, :], xn[:, two, :], rowof(R_LB, PAIR, 2), ADD))
            link(V.tensor_tensor(hA[:, two, :], hA[:, two, :], xn[:, two, :], ADD))
            unit_rows(NT // 2, NT // 2)
            mxd, smd = rs[0][0:NE, 0:B], rs[1][0:NE, 0:B]

            def dispatch_shift(half):
                dve.wait_ge(ld_done, half + 1)
                bs = slice(half * HALF, (half + 1) * HALF)
                l3 = ps[half][0:NE, 0:TH].rearrange("p (b m) -> p b m", b=HALF)
                link(V.tensor_reduce(mxd[:, bs], l3, AX, MAX))
                V.tensor_tensor(Ld[:, bs, :], l3, mxd[:, bs].rearrange("p (b a) -> p b a", a=1).to_broadcast([NE, HALF, L]), SUB).then_inc(sm_shift, 1)

            def dispatch_divide(half):
                dve.wait_ge(sm_exp, half + 1)
                bs = slice(half * HALF, (half + 1) * HALF)
                link(V.tensor_reduce(smd[:, bs], Ld[:, bs, :], AX, ADD))
                link(V.reciprocal(smd[:, bs], smd[:, bs]))
                V.tensor_tensor(Ld[:, bs, :], Ld[:, bs, :], smd[:, bs].rearrange("p (b a) -> p b a", a=1).to_broadcast([NE, HALF, L]), MULT).then_inc(d_ready, 1)

            def dispatch_save(half):
                dve.wait_ge(d_turned, half + 1)
                ts = slice(4 * half, 4 * half + 4)
                for b in range(2):
                    ins = V.tensor_scalar(dbd[:, ts, b, :], ps[3][0:PAIR, 4 * half * NE:4 * (half + 1) * NE].rearrange("p (t n) -> p t n", t=4), cst[0:PAIR, C_BM + b:C_BM + b + 1], None, MULT)
                ins.then_inc(dbd_ready, 1)

            dispatch_shift(0)
            dispatch_divide(0)
            dispatch_shift(1)
            dispatch_save(0)
            dispatch_divide(1)
            dispatch_save(1)
            mxc, smc = rs[2][0:PAIR, 0:NT], rs[3][0:PAIR, 0:NT]
            l3 = ps[2][0:PAIR, :].rearrange("p (t n) -> p t n", t=NT)
            dve.wait_ge(lc_done, 2)
            link(V.tensor_reduce(mxc, l3, AX, MAX))
            V.tensor_tensor(Lc, l3, mxc.rearrange("p (t a) -> p t a", a=1).to_broadcast([PAIR, NT, NE]), SUB).then_inc(sm_shift, 1)
            dve.wait_ge(xs_zero, 2)
            for half in range(2):
                for n in (2, 3):
                    dve.wait_ge(xs_done, 4 * half + n + 1)
                    dst, src = slot_inputs(half, n)
                    V.tensor_copy(dst, src).then_inc(xs_ready, 1)
            dve.wait_ge(sm_exp, 3)
            link(V.tensor_reduce(smc, Lc, AX, ADD))
            link(V.reciprocal(smc, smc))
            link(V.tensor_tensor(Lc, Lc, smc.rearrange("p (t a) -> p t a", a=1).to_broadcast([PAIR, NT, NE]), MULT))
            for b in range(2):
                ins = V.tensor_scalar(cbd[:, :, b, :], Lc, cst[0:PAIR, C_BM + b:C_BM + b + 1], None, MULT)
            ins.then_inc(c_ready, 1)
            dve.wait_ge(bias_loaded, 32)

            def quad_steps(r):
                for s in range(RING):
                    dve.wait_ge(h_turned, RING * r + s + 1)
                    V.tensor_tensor(hb.rearrange("p t g b -> p (t g) b"), ps[2 + s % 2][:, 0:NFT * 128].rearrange("p (g b) -> p g b", b=B),
                                    b1[:, ds(RING * r + s, 1), :, :].rearrange("p a t g -> p (a t g)").rearrange("p (g a) -> p g a", a=1).to_broadcast([128, NFT * 8, B]), ADD).then_inc(b1_added, 1)
                    dve.wait_ge(ys_done, RING * r + s + 1)
                    if not (isinstance(r, int) and r == 0):
                        dve.wait_ge(ys_stored[s], 16 * QUAD * r)
                    V.tensor_copy(ysb[:, s, :], ps[4 + s % 2][:, 0:D]).then_inc(ys_ready, 1)

            quad_steps(0)
            with dve.Fori(1, ROUNDS) as r:
                quad_steps(r)
            def combined(half):
                for k in range(2 * half, 2 * half + 2):
                    dve.wait_ge(comb_done, k + 1)
                    ins = V.tensor_tensor(hA[:, 2 * k:2 * k + 2, :], ps[COMB[k]][0:PAIR, 0:2 * D].rearrange("p (t d) -> p t d", t=2), hA[:, 2 * k:2 * k + 2, :], ADD)
                ins.then_inc(hA_ready, 1)
                dve.wait_ge(hA_ready, half + 1)

            norm_in_halves(combined)
            dve.wait_ge(act_step, 1)
            V.tensor_scalar(negA, negA, -1.0, None, MULT).then_inc(negA_ready, 1)
            for c in range(CC):
                dve.wait_ge(in_done, c + 1)
                src = ps[c][:, 0:TH].rearrange("p (b l) -> p b l", b=HALF)
                w = [col[:, K_CX + TAPS * c + k:K_CX + TAPS * c + k + 1] for k in range(TAPS)]
                link(V.tensor_scalar(u[:, c, :, :], src, w[1], None, MULT))
                link(V.scalar_tensor_tensor(out=u[:, c, :, 1:L], in0=src[:, :, 0:L - 1], scalar=w[0], in1=u[:, c, :, 1:L], op0=MULT, op1=ADD))
                link(V.scalar_tensor_tensor(out=u[:, c, :, 0:L - 1], in0=src[:, :, 1:L], scalar=w[2], in1=u[:, c, :, 0:L - 1], op0=MULT, op1=ADD))
                V.scalar_tensor_tensor(out=u[:, c, :, 0:L - 2], in0=src[:, :, 2:L], scalar=w[3], in1=u[:, c, :, 0:L - 2], op0=MULT, op1=ADD).then_inc(conv_ready, 1)
            for c in range(CC):
                dve.wait_ge(dt_done, c + 1)
                bias = col[:, K_DT + c:K_DT + c + 1]
                ins = V.tensor_scalar(sp[0][:, c, :], ps[c][:, 0:TH], bias, bias, ADD, ADD)
            ins.then_inc(sp_t, 1)
            dve.wait_ge(sp_act, 2)
            link(V.tensor_scalar(sp[2], sp[1], LOG1P[0], None, MULT))
            for k in LOG1P[1:]:
                link(V.scalar_tensor_tensor(out=sp[2], in0=sp[2], scalar=k, in1=sp[1], op0=ADD, op1=MULT))
            link(V.tensor_scalar(du, sp[1], LOG1P_MAX, None, ALU.is_lt))
            dve.wait_ge(sp_act, 3)
            link(V.copy_predicated(delta, du.bitcast(mybir.dt.uint32), sp[2]))
            V.scalar_tensor_tensor(out=delta, in0=sp[0], scalar=0.0, in1=delta, op0=MAX, op1=ADD).then_inc(delta_ready, 1)
            dve.wait_ge(delta_ready, 1)
            dve.wait_ge(u_ready, CC)
            link(V.tensor_tensor(du, delta, u.rearrange("p c b l -> p c (b l)"), MULT))
            for k in range(NUNIT):
                g, c = k // CC, k % CC
                dve.wait_ge(bc_saved, 2 * NG * (g + 1))
                link(V.tensor_tensor(dBu[k % 2].rearrange("p (n t) -> p n t", n=NG), Bb[:, NG * g:NG * (g + 1), :], du[:, c:c + 1, :].to_broadcast([128, NG, TH]), MULT))
                dve.wait_ge(dA_ready, k + 1)
                V.tensor_tensor_scan(hst[k % 2], dA[k % 2], dBu[k % 2], 0.0, MULT, ADD).then_inc(scan_done, 1)
                dve.wait_ge(scan_done, k + 1)
                if k >= 2:
                    dve.wait_ge(h_used, k - 1)
                V.tensor_tensor(hC[k % 2], hst[k % 2], Cb[:, NG * g:NG * (g + 1), :].rearrange("p n t -> p (n t)"), MULT).then_inc(hC_ready, 1)
            dve.wait_ge(ybd_zero, 1)
            for c in range(CC):
                dve.wait_ge(h_used, NUNIT - CC + c + 1)
                for half in range(2):
                    p0 = 64 * half
                    ins = V.scalar_tensor_tensor(out=ybd[p0:p0 + 64, c, half * TH:(half + 1) * TH], in0=u[p0:p0 + 64, c, :, :].rearrange("p b l -> p (b l)"),
                                                 scalar=col[p0:p0 + 64, K_D + c:K_D + c + 1], in1=ps[3 + c][p0:p0 + 64, 0:TH], op0=MULT, op1=ADD)
                ins.then_inc(yb_ready, 1)
            dve.wait_ge(resid_moved, 16 * NMOVE)
            dve.wait_ge(hB_pad, 1)
            for t in range(TT):
                dve.wait_ge(so_done, t + 1)
                ins = V.tensor_tensor(hB[:, t, :], ps[SO[t]][:, 0:D], hB[:, t, :], ADD)
            link(ins)

            statistics(hB, 128, 0, TT)
            var, z, r = mv[:, 0:TT, 1], rs[0][:, 0:TT], rs[4][:, 0:TT]
            link(V.tensor_scalar(z, var, LN_EPS, None, ADD))
            link(V.reciprocal(r, z))
            link(V.tensor_tensor(r, r, var, MULT))
            link(V.tensor_scalar(rs[0][:, TT:2 * TT], r, LN_EPS, None, ADD))
            rsqrt(128, 2 * TT)
            for ins in normalise(tk, hB, 128, 0, TT):
                pass
            link(ins)
            link(V.tensor_tensor(hB, hB, tk, ADD))
            for t in range(TT):
                ins = V.tensor_scalar(tk[:, t, :], tk[:, t, :], rs[3][:, TT + t:TT + t + 1], None, MULT)
            link(ins)
            link(V.tensor_tensor(tk, tk, rowof(R_FG, 128, TT), MULT))
            V.tensor_tensor(tk, tk, rowof(R_FB, 128, TT), ADD).then_inc(tk_ready, 1)
            dve.wait_ge(logit_done, 1)
            lg = ps[5][:, 0:TT * NX].rearrange("p (t e) -> p t e", t=TT)
            m5, s5 = mxs[:, 0, 0:TT], mxs[:, 1, 0:TT]

            def wide(x, n=NX):
                return x.rearrange("p (t a) -> p t a", a=1).to_broadcast([128, TT, n])

            link(V.tensor_reduce(m5, lg, AX, MAX))
            V.tensor_tensor(rt[0], lg, wide(m5), SUB).then_inc(rt_shift, 1)
            dve.wait_ge(rt_exp, 1)
            link(V.tensor_reduce(s5, rt[1], AX, ADD))
            link(V.reciprocal(s5, s5))
            link(V.tensor_tensor(rt[1], rt[1], wide(s5), MULT))
            for t in range(TT):
                ins = V.max(rt[2][:, t, :], rt[1][:, t, :])
            link(ins)
            for t in range(TT):
                ins = V.max_index(ridx[:, t, :], rt[2][:, t, :], rt[1][:, t, :])
            link(ins)
            link(V.tensor_copy(rt[3], ridx[:, :, :]))
            top = rt[2][:, :, 0:TOPK]
            link(V.tensor_reduce(s5, top, AX, ADD))
            link(V.reciprocal(s5, s5))
            link(V.tensor_tensor(top, top, wide(s5, TOPK), MULT))
            iota = cst[:, C_IOTA:C_IOTA + NX].rearrange("p (a e) -> p a e", a=1).to_broadcast([128, TT, NX])
            for k in range(TOPK):
                ins = V.tensor_tensor(rt[4 + k], iota, rt[3][:, :, k:k + 1].to_broadcast([128, TT, NX]), ALU.is_equal)
            link(ins)
            link(V.tensor_tensor(rt[6], rt[4], rt[5], ADD))
            V.memset(rt[6][LAST:128, TT - 1, :], 0.0).then_inc(chosen, 1)
            dve.wait_ge(ranked, 1)
            count = ps[7][:, 0:NX].rearrange("p (e a) -> p e a", a=1).to_broadcast([128, NX, TT])
            over = rt[7].rearrange("p t e -> p (t e)").rearrange("p (e k) -> p e k", e=NX)
            link(V.tensor_tensor(over, count, thresholds.rearrange("p (a k) -> p a k", a=1).to_broadcast([128, NX, TT]), ALU.is_gt))
            link(V.tensor_reduce(tiles_of, over, AX, ADD))
            link(V.tensor_tensor_scan(tiles_to, ones[:, 0:NX], tiles_of, 0.0, MULT, ADD))
            link(V.tensor_tensor(slot_cmp, tiles_to[0:1].rearrange("p (a e) -> p a e", a=1).to_broadcast([1, NSLOT, NX]), slot_no.rearrange("p (s a) -> p s a", a=1).to_broadcast([1, NSLOT, NX]), ALU.is_le))
            link(V.tensor_reduce(slot_f, slot_cmp, AX, ADD))
            V.tensor_scalar(slot_expert, slot_f, float(NX - 1), None, ALU.min).then_inc(slots_known, 1)
            link(V.tensor_tensor(first_tile, tiles_to, tiles_of, SUB))
            link(V.scalar_tensor_tensor(out=rt[7], in0=first_tile.rearrange("p (a e) -> p a e", a=1).to_broadcast([128, TT, NX]), scalar=128.0,
                                        in1=ps[6][:, 0:TT * NX].rearrange("p (t e) -> p t e", t=TT), op0=MULT, op1=ADD))
            for k in range(TOPK):
                ins = V.tensor_tensor(rt[4 + k], rt[4 + k], rt[7], MULT)
            link(ins)
            for k in range(TOPK):
                ins = V.tensor_reduce(place_f[k], rt[4 + k], AX, ADD)
            link(ins)
            for k in range(TOPK):
                ins = V.tensor_copy(place[:, k, :], place_f[k])
            ins.then_inc(places_ready, 1)

            def save_tokens(slot, n):
                dve.wait_ge(slx_turned, slot + 1)
                if not (isinstance(slot, int) and slot < 2):
                    dve.wait_ge(up_done, 2 * slot - 2)
                V.tensor_copy(slT[n][0:H], ps[n][0:H, 0:256].rearrange("p (k t) -> p k t", k=2)).then_inc(slT_ready, 1)

            def save_outputs(r, b, slot):
                dve.wait_ge(down_done, slot + 1)
                if not (isinstance(r, int) and r == 0):
                    dve.wait_ge(sly_stored[b], 16 * r)
                V.tensor_copy(sly[b], ps[6 + b % 2][:, 0:D]).then_inc(sly_ready, 1)

            def routed_steps(r):
                for b in range(NB):
                    slot = NB * r + b
                    if not (isinstance(r, int) and slot + 2 >= NSLOT):
                        save_tokens(slot + 2, b % 2)
                    save_outputs(r, b, slot)

            dve.wait_ge(routed_padded, NB + 2)
            save_tokens(0, 0)
            save_tokens(1, 1)
            routed_steps(0)
            with dve.Fori(1, NSLOT // NB - 1) as r:
                routed_steps(r)
            routed_steps(NSLOT // NB - 1)
            for t in range(TT):
                p = 128 if t < TT - 1 else LAST
                dve.wait_ge(rows_gathered[t], 16 * TOPK)
                link(V.scalar_tensor_tensor(out=hB[0:p, t, :], in0=yg[0:p, t, 0, :], scalar=rt[2][0:p, t, 0:1], in1=hB[0:p, t, :], op0=MULT, op1=ADD))
                V.scalar_tensor_tensor(out=hB[0:p, t, :], in0=yg[0:p, t, 1, :], scalar=rt[2][0:p, t, 1:2], in1=hB[0:p, t, :], op0=MULT, op1=ADD).then_inc(token_done, 1)

        
        @block.tensor
        def _(pe):
            mm, tr = nc.tensor.matmul, nc.tensor.transpose

            for k in range(KP):
                if k % 2 == 0:
                    pe.wait_ge(patch_loaded[k // 2], 32)
                for t in range(NT):
                    ins = mm(ps[t][0:PAIR, 0:D], pat[:, k, PAIR * t:PAIR * (t + 1)], wpa[:, k, :], start=(k == 0), stop=(k == KP - 1))
                    if k == KP - 1:
                        ins.then_inc(embedded, 1)

            def turn_tokens(n0, tiles=range(NT)):
                for t in tiles:
                    pe.wait_ge(xn_ready, n0 + t + 1)
                    for k in range(2):
                        ins = tr(ps[t][0:H, k * PAIR:(k + 1) * PAIR], xn[:, t, k * H:(k + 1) * H], ident[0:PAIR, 0:PAIR])
                    ins.then_inc(x_turned, 1)

            pe.wait_ge(cst_loaded, 16)
            pe.wait_ge(hw_loaded, 16)
            pe.wait_ge(padded, PADS)
            for half in range(2):
                turn_tokens(0, range(4 * half, 4 * half + 4))
                pe.wait_ge(xT_ready, 4 * half + 4)
                for c in range(4):
                    for k in range(2):
                        ins = mm(ps[4 * half + c][0:H, 0:TH], hw[:, k, W_QKV + c * H:W_QKV + (c + 1) * H], xT[:, k, half * TH:(half + 1) * TH], start=(k == 0), stop=(k == 1))
                    ins.then_inc(qk_done, 1)
            pe.wait_ge(qk_saved, 8)
            pe.wait_ge(phi_sq, 1)
            for k in range(2):
                ins = mm(ps[7][:, 0:NE], ones[:, :], phin[:, k, :], start=(k == 0), stop=(k == 1))
            ins.then_inc(phi_sum, 1)
            for i in range(NT + 3):
                if i >= 3:
                    t = i - 3
                    pe.wait_ge(oT_ready, t + 1)
                    if t == 2:
                        pe.wait_ge(phi_ready, 1)
                    if t >= 4 and t % 2 == 0:
                        pe.wait_ge(an_ready, t // 2 - 1)
                    for k in range(2):
                        ins = mm(ps[6 + t // 2 % 2][0:PAIR, t % 2 * D:(t % 2 + 1) * D], oT[:, k, PAIR * t:PAIR * (t + 1)], hw[:, k, W_OUT:W_OUT + D], start=(k == 0), stop=(k == 1))
                    ins.then_inc(y_done, 1)
                if i < NT:
                    if i >= 1:
                        pe.wait_ge(vbd_ready, i)
                    pe.wait_ge(xR_ready, i + 1)
                    for b in range(2):
                        for k in range(2):
                            ins = mm(ps[3][0:3 * L, b * D:(b + 1) * D], xR[i % 2][:, k, b, :, :].rearrange("p r l -> p (r l)"), hw[:, k, W_QKV + 2 * D:W_QKV + 3 * D], start=(k == 0), stop=(k == 1))
                    ins.then_inc(v_done, 1)
                if 1 <= i <= NT:
                    t = i - 1
                    pe.wait_ge(exp_done, t + 1)
                    if t >= 1:
                        pe.wait_ge(pT_ready, t)
                    for g in range(4):
                        ins = tr(ps[2][0:3 * L, g * 128:(g + 1) * 128], prob[t % 2][:, 3 * g:3 * g + 3, :].rearrange("p h k -> p (h k)"), ident)
                    ins.then_inc(p_turned, 1)
                if i < NT:
                    pe.wait_ge(kbd_ready, i + 1)
                    if i >= 2:
                        pe.wait_ge(shifted, i - 1)
                    for b in range(2):
                        t0 = PAIR * i + L * b
                        for g in range(2):
                            ins = mm(ps[i % 2][64 * b:64 * b + 64, g * 6 * L:(g + 1) * 6 * L], qT[:, g, t0:t0 + 64], kbd[:, g, :, b * L:(b + 1) * L], start=True, stop=True)
                    ins.then_inc(scores_done, 1)
                if 1 <= i <= NT:
                    t = i - 1
                    pe.wait_ge(pT_ready, t + 1)
                    pe.wait_ge(vbd_ready, t + 1)
                    if t >= 1:
                        pe.wait_ge(o_ready, t)
                    for b in range(2):
                        for g in range(4):
                            ins = mm(ps[4][64 * b:64 * b + 64, g * 3 * HD:(g + 1) * 3 * HD], pT[:, g, 64 * b:64 * b + 64], vbd[t % 2][:, b, g * 3 * HD:(g + 1) * 3 * HD], start=True, stop=True)
                    ins.then_inc(av_done, 1)
                if 2 <= i < NT + 2:
                    t = i - 2
                    pe.wait_ge(o_ready, t + 1)
                    if t >= 1:
                        pe.wait_ge(oT_ready, t)
                    for k in range(2):
                        ins = tr(ps[5][0:H, k * 128:(k + 1) * 128], osb[:, k * H:(k + 1) * H], ident)
                    ins.then_inc(o_turned, 1)

            def slot_logits(half):
                turn_tokens(NT, range(4 * half, 4 * half + 4))
                pe.wait_ge(xT_ready, NT + 4 * half + 4)
                for k in range(2):
                    ins = mm(ps[half][0:NE, 0:TH], phin[:, k, :], xT[:, k, half * TH:(half + 1) * TH], start=(k == 0), stop=(k == 1))
                ins.then_inc(ld_done, 1)

            def token_logits(half):
                for t in range(4 * half, 4 * half + 4):
                    for k in range(2):
                        ins = mm(ps[2][0:PAIR, t * NE:(t + 1) * NE], xT[:, k, PAIR * t:PAIR * (t + 1)], phin[:, k, :], start=(k == 0), stop=(k == 1))
                ins.then_inc(lc_done, 1)

            def turn_dispatch(half):
                pe.wait_ge(d_ready, half + 1)
                for t in range(4 * half, 4 * half + 4):
                    ins = tr(ps[3][0:PAIR, t * NE:(t + 1) * NE], Ld[:, 2 * t:2 * t + 2, :].rearrange("p b m -> p (b m)"), ident[0:NE, 0:NE])
                ins.then_inc(d_turned, 1)

            def dispatch(half):
                pe.wait_ge(dbd_ready, half + 1)
                for c, p0, m, d0, e in XS_PARTS:
                    for t in range(4 * half, 4 * half + 4):
                        ins = mm(ps[XS_BANKS[half][c]][p0:p0 + m, t * NE:(t + 1) * NE], xn[:, t, d0:d0 + m], dbd[:, t, :, e:NE:2], start=True, stop=True)
                    ins.then_inc(xs_done, 1)

            slot_logits(0)
            token_logits(0)
            slot_logits(1)
            turn_dispatch(0)
            token_logits(1)
            dispatch(0)
            turn_dispatch(1)
            dispatch(1)
            pe.wait_ge(sm_shift, 3)
            pe.wait_ge(xs_ready, 8)

            def experts(r):
                for s in range(RING):
                    pe.wait_ge(w1_loaded[s], 16 * r + 16)
                    pe.wait_ge(xsq_ready, RING * r + s + 1)
                    for c in range(3):
                        for j in range(4):
                            a, fh = j // 2, j % 2
                            ins = mm(ps[s % 2][32 * j:32 * j + 32, 0:NFT * 128], XSq[s % 2][:, a, c, :], w1s[s][:, a, c, fh * NFT * 128:(fh + 1) * NFT * 128], start=(c == 0), stop=(c == 2))
                    ins.then_inc(h_done, 1)
                    pe.wait_ge(h_saved, RING * r + s + 1)
                    for t in range(NFT):
                        ins = tr(ps[2 + s % 2][:, t * 128:(t + 1) * 128], hs[s % 2][:, t * 128:(t + 1) * 128], ident)
                    ins.then_inc(h_turned, 1)
                    pe.wait_ge(w2_loaded[s], 16 * r + 16)
                    pe.wait_ge(gelu_done, RING * r + s + 1)
                    for fh in range(2):
                        for t in range(NFT):
                            for q in range(QUAD):
                                a = q // 2
                                g0 = 4 * a + 2 * fh
                                ins = mm(ps[4 + s % 2][32 * q:32 * q + 32, 0:D], hg[:, t, g0:g0 + 2, :].rearrange("p g b -> p (g b)"), w2s[s][:, q, fh * NFT + t, :],
                                         start=(fh == 0 and t == 0), stop=(fh == 1 and t == NFT - 1))
                    ins.then_inc(ys_done, 1)

            experts(0)
            pe.wait_ge(c_ready, 1)
            for t in range(NT):
                ins = tr(ps[6 + t // 4][:, (t % 4) * PAIR:(t % 4 + 1) * PAIR], cbd[:, t, :, :].rearrange("p b n -> p (b n)"), ident[0:PAIR, 0:PAIR])
                if t % 4 == 3:
                    ins.then_inc(c_turned, 1)
            with pe.Fori(1, ROUNDS) as r:
                experts(r)
            pe.wait_ge(cT_ready, 2)
            pe.wait_ge(ys_moved, 16 * YMOVE)
            for t in range(NT):
                dst = ps[COMB[t // 2]][0:PAIR, (t % 2) * D:(t % 2 + 1) * D]
                mm(dst, cT[:, t, :], b2[:, :], start=True, stop=False)
                ins = mm(dst, cT[:, t, :], ysn[:, t, :], start=False, stop=True)
                if t % 2:
                    ins.then_inc(comb_done, 1)

            turn_tokens(2 * NT)
            pe.wait_ge(xT_padded, 1)
            pe.wait_ge(xT_ready, 3 * NT)
            pe.wait_ge(scan_w_loaded, 16)
            for c in range(2 * CC):
                for half in range(2):
                    for k in range(2):
                        ins = mm(ps[c][64 * half:64 * half + 64, 0:TH], w_in[:, k, c, :], xT[:, k, half * TH:(half + 1) * TH], start=(k == 0), stop=(k == 1))
                ins.then_inc(in_done, 1)
            for c in range(CC):
                pe.wait_ge(u_ready, c + 1)
                ins = mm(ps[6][0:2 * XD, 0:TH], w_xp[:, c, :], u[:, c, :, :].rearrange("p b l -> p (b l)"), start=(c == 0), stop=(c == CC - 1))
            ins.then_inc(xd_done, 1)
            pe.wait_ge(xd_saved, 1)
            for c in range(CC):
                mm(ps[c][:, 0:TH], w_dt[:, c, :], xd, start=True, stop=True).then_inc(dt_done, 1)

            def spread(n):
                if n == 0:
                    pe.wait_ge(sel_ready, 1)
                if n >= 2:
                    pe.wait_ge(bc_saved, n - 1)
                mm(ps[6 + n % 2][:, 0:TH], sel[n], xd, start=True, stop=True).then_inc(bc_done, 1)

            sent = 0
            for k in range(NUNIT + 1):
                if k < NUNIT:
                    g, c = k // CC, k % CC
                    upto = 2 * NG * (g + 1) if c == 0 else sent
                    if g + 1 < NS // NG:
                        upto = min(2 * NG * (g + 2), 2 * NG * (g + 1) + (c + 1) * 3)
                    while sent < upto:
                        spread(sent)
                        sent += 1
                if k >= 1:
                    g, c = (k - 1) // CC, (k - 1) % CC
                    pe.wait_ge(hC_ready, k)
                    for j in range(NG):
                        ins = mm(ps[3 + c][:, 0:TH], ident, hC[(k - 1) % 2][:, j * TH:(j + 1) * TH],
                                 start=(g == 0 and j == 0), stop=(g == NS // NG - 1 and j == NG - 1))
                    ins.then_inc(h_used, 1)
            pe.wait_ge(z_ready, 2)
            for half in range(2):
                for t in range(TT):
                    if half == 0 and t == 3:
                        pe.wait_ge(bc_saved, 2 * NS)
                    if half == 1:
                        pe.wait_ge(yb_ready, CC)
                    chunks = range(CC, 2 * CC) if half == 0 else range(CC)
                    for c in chunks:
                        ins = mm(ps[SO[t]][:, 0:D], ybd[:, c, 128 * t:128 * (t + 1)], w_so[:, c, :], start=(c == CC), stop=(c == CC - 1))
                    if half == 1:
                        ins.then_inc(so_done, 1)

            pe.wait_ge(tk_ready, 1)
            for t in range(TT):
                for k in range(2):
                    ins = tr(ps[t][0:H, k * 128:(k + 1) * 128], tk[:, t, k * H:(k + 1) * H], ident)
                ins.then_inc(tk_turned, 1)
            pe.wait_ge(tkT_ready, TT)
            pe.wait_ge(tkT_padded, 1)
            for t in range(TT):
                for k in range(2):
                    ins = mm(ps[5][:, t * NX:(t + 1) * NX], tkT[:, k, 128 * t:128 * (t + 1)], hw[:, k, W_RT:W_RT + NX], start=(k == 0), stop=(k == 1))
            ins.then_inc(logit_done, 1)

            pe.wait_ge(chosen, 1)
            for t in range(TT):
                for t1 in range(t + 1):
                    mm(ps[6][:, t * NX:(t + 1) * NX], tri if t1 == t else ones[:, :], rt[6][:, t1, :], start=(t1 == 0), stop=(t1 == t))
            for t in range(TT):
                ins = mm(ps[7][:, 0:NX], ones[:, :], rt[6][:, t, :], start=(t == 0), stop=(t == TT - 1))
            ins.then_inc(ranked, 1)

            def turn_slot(r, b, slot):
                pe.wait_ge(slx_loaded[b], 16 * r + 16)
                if not (isinstance(slot, int) and slot < 2):
                    pe.wait_ge(slT_ready, slot - 1)
                for k in range(2):
                    ins = tr(ps[b % 2][0:H, k * 128:(k + 1) * 128], slx[b][:, k * H:(k + 1) * H], ident)
                ins.then_inc(slx_turned, 1)

            def up(r, b, slot):
                pe.wait_ge(f1_loaded[b], 16 * r + 16)
                pe.wait_ge(slT_ready, slot + 1)
                for f in range(KF):
                    bank, c = (2, f) if f < 4 else (3, f - 4)
                    for k in range(2):
                        ins = mm(ps[bank + 2 * (b % 2)][:, c * 128:(c + 1) * 128], f1s[b][:, k, f * 128:(f + 1) * 128], slT[b % 2][:, k, :], start=(k == 0), stop=(k == 1))
                    if f in (3, KF - 1):
                        ins.then_inc(up_done, 1)

            def down(r, b, slot):
                pe.wait_ge(f2_loaded[b], 16 * r + 16)
                if not (isinstance(slot, int) and slot < 2):
                    pe.wait_ge(sly_ready, slot - 1)
                for f in range(KF):
                    if f in (0, 4):
                        pe.wait_ge(silu_done, 2 * slot + 1 + f // 4)
                    ins = mm(ps[6 + b % 2][:, 0:D], gT[b % 2][:, f, :], f2s[b][:, f, :], start=(f == 0), stop=(f == KF - 1))
                ins.then_inc(down_done, 1)

            def slot_steps(r):
                for b in range(NB):
                    slot = NB * r + b
                    last = isinstance(r, int) and r == NSLOT // NB - 1
                    for stage, ahead in ((turn_slot, 2), (up, 1)):
                        if not (last and b + ahead >= NB):
                            stage(r + (b + ahead) // NB, (b + ahead) % NB, slot + ahead)
                    down(r, b, slot)

            pe.wait_ge(places_ready, 1)
            pe.wait_ge(routed_padded, NB + 2)
            turn_slot(0, 0, 0)
            turn_slot(0, 1, 1)
            up(0, 0, 0)
            slot_steps(0)
            with pe.Fori(1, NSLOT // NB - 1) as r:
                slot_steps(r)
            slot_steps(NSLOT // NB - 1)


def layouts(x, L0_tok_W_proj, L0_tok_b_proj, L0_attn_w_qkv, L0_attn_w_out, L0_attn_b_out, L0_attn_ln_g, L0_attn_ln_b,
            L0_ffn_phi, L0_ffn_scale, L0_ffn_w1, L0_ffn_b1, L0_ffn_w2, L0_ffn_b2, L1_attn_in_proj_w, L1_attn_x_proj_w,
            L1_attn_dt_proj_w, L1_attn_dt_proj_b, L1_attn_A_log, L1_attn_D_param, L1_attn_out_proj_w, L1_attn_conv_x_w,
            L1_attn_conv_z_w, L1_ffn_ln_gamma, L1_ffn_ln_beta, L1_ffn_router_w, L1_ffn_w1, L1_ffn_w2):
    f4 = np.float32
    C = np.ascontiguousarray

    def halves(w, row=None):
        out = np.zeros((128, 2, w.shape[1]), f4)
        out[0:H] = w.reshape(2, H, -1).transpose(1, 0, 2)
        if row is not None:
            out[H, 1] = row
        return out

    patches = x.reshape(B, 3, 6, 16, 6, 16).transpose(1, 3, 5, 0, 2, 4).reshape(KP, 128, T).transpose(1, 0, 2)
    w_patch = L0_tok_W_proj.T.reshape(KP, 128, D).transpose(1, 0, 2)
    consts = np.zeros((128, C_W), f4)
    p = np.arange(128)
    consts[:, C_ID:C_ID + 128] = np.eye(128)
    consts[:, C_HEAD:C_HEAD + 6] = p[:, None] // HD == np.arange(6)
    consts[:, C_VM:C_VM + D] = p[:, None] // L == np.arange(D) // HD % 3
    consts[:, C_BM:C_BM + 2] = p[:, None] // L == np.arange(2)
    consts[:, C_IOTA:C_IOTA + NX] = np.arange(NX)
    half_w = np.concatenate([halves(L0_attn_w_qkv), halves(L0_attn_w_out, L0_attn_b_out), halves(L0_ffn_phi.reshape(D, NE)), halves(L1_ffn_router_w)], 2)
    rows = np.broadcast_to(np.stack([L0_tok_b_proj, L0_attn_ln_g, L0_attn_ln_b, L1_ffn_ln_gamma, L1_ffn_ln_beta]), (128, 5, D))

    def by_channel(w):
        w = w.reshape(CC, 64, -1).transpose(1, 0, 2).reshape(64, -1)
        return np.concatenate([w, w])

    cols = np.concatenate([by_channel(L1_attn_conv_x_w), by_channel(L1_attn_conv_z_w), by_channel(L1_attn_D_param), by_channel(L1_attn_dt_proj_b),
                           by_channel(L1_attn_A_log), np.broadcast_to(L0_ffn_scale, (128, 1))], 1)
    b1t = L0_ffn_b1.reshape(NQ, 2, 2, 2, NFT, 128).transpose(5, 0, 4, 1, 3, 2).reshape(128, NQ, NFT, 8)
    b2n = np.concatenate([L0_ffn_b2, L0_ffn_b2])
    scan_w = np.zeros((128, S_W), f4)
    scan_w[:, S_IN:S_IN + 768] = halves(L1_attn_in_proj_w.T).reshape(128, -1)
    xp = np.zeros((2, 64, CC, 2, XD), f4)
    dt = np.zeros((2, XD, CC, 2, 64), f4)
    for half in range(2):
        xp[half, :, :, half, :] = L1_attn_x_proj_w.reshape(XD, CC, 64).transpose(2, 1, 0)
        dt[half, 0:DTR, :, half, :] = L1_attn_dt_proj_w.reshape(CC, 64, DTR).transpose(2, 0, 1)
    scan_w[:, S_XP:S_XP + 264] = xp.reshape(128, -1)
    scan_w[0:2 * XD, S_DT:S_DT + 384] = dt.reshape(2 * XD, -1)
    scan_w[:, S_OUT:S_TRI] = np.concatenate(
        [by_channel(L1_attn_out_proj_w.T[0:D]), by_channel(L1_attn_out_proj_w.T[D:2 * D])], 1)
    w1q = L0_ffn_w1.reshape(NQ, 2, 3, 128, FF).transpose(0, 3, 1, 2, 4).reshape(NQ, 128, -1)
    w2q = L0_ffn_w2.reshape(NQ, QUAD, KF, 128, D).transpose(0, 3, 1, 2, 4).reshape(NQ, 128, -1)
    scan_w[:, S_TRI:S_TRI + 128] = np.triu(np.ones((128, 128)), 1)
    scan_w[:, S_SLOT:S_SLOT + NSLOT] = np.arange(NSLOT)
    scan_w[:, S_THR:S_THR + TT] = 128 * np.arange(TT)
    f1 = L1_ffn_w1.reshape(NX, 2, H, FF).transpose(0, 2, 1, 3)
    f2 = L1_ffn_w2.reshape(NX, KF, 128, D).transpose(0, 2, 1, 3)
    return dict(patches=C(patches), w_patch=C(w_patch), consts=consts, half_w=C(half_w), rows=C(rows), cols=C(cols), b1t=C(b1t), b2n=C(b2n),
                scan_w=scan_w, w1q=C(w1q), w2q=C(w2q), f1=C(f1), f2=C(f2))


def kernel(**inputs):
    import concourse.bacc as bacc
    from concourse.bass_utils import run_bass_kernel_spmd

    nc = bacc.Bacc("TRN2", target_bir_lowering=False, num_devices=1)
    arrays = layouts(**{k: np.asarray(v) for k, v in inputs.items()})
    names = {k: f"in_{k}_dram" for k in arrays}
    args = {k: nc.dram_tensor(names[k], a.shape, mybir.dt.from_np(a.dtype), kind="ExternalInput").ap() for k, a in arrays.items()}
    out = nc.dram_tensor("out_dram", (T, D), mybir.dt.float32, kind="ExternalOutput").ap()
    build_tower(nc, out=out, **args)
    r = run_bass_kernel_spmd(nc, [{names[k]: a for k, a in arrays.items()}], core_ids=[0])
    return r.results[0]["out_dram"].reshape(B, L, D)
```

```python
import numpy as np
import concourse.bass as bass
from concourse import mybir
from contextlib import ExitStack

B, L, D = 16, 36, 192
T = B * L
PD = 768
H = D // 2
NH, HD = 12, 16
NE, FF = 64, 768
NS, DTR, TAPS = 16, 12, 4
NX, TOPK = 8, 2
LN_EPS = 1e-5

LOG1P_MAX = 0.0625
LOG1P = (-0.2267529733215877, 0.33244881243292695, -0.49998911196695306, 0.9999999790041106)

RSQRT_GUESS = float(0x5F3759DF)

PAIR = 2 * L
NT = T // PAIR
KP = PD // 128
QUAD = 4
NQ = NE // QUAD
RING = 4
ROUNDS = NQ // RING
NFT = 3
KF = FF // 128
HALF = B // 2
TH = HALF * L
CC = D // 64
XD = DTR + 2 * NS
NG = 4
TT = 5
NSLOT = (T * TOPK + NX * 127) // 128
NB = 4
TP = TT * 128
LAST = T - (TT - 1) * 128

C_ID, C_HEAD, C_VM, C_BM, C_IOTA = 0, 128, 134, 326, 328
C_W = 336
W_QKV, W_OUT, W_PHI, W_RT = 0, 3 * D, 4 * D, 4 * D + NE
W_W = 4 * D + NE + NX
R_BP, R_LG, R_LB, R_FG, R_FB = range(5)
K_CX, K_CZ, K_D, K_DT, K_AL, K_SC, K_FG, K_FB = 0, 12, 24, 27, 30, 78, 79, 81
K_W = 83
S_IN, S_XP, S_DT, S_OUT = 0, 768, 1032, 1416
S_TRI = S_OUT + 2 * CC * D
S_SLOT, S_THR = S_TRI + 128, S_TRI + 128 + NSLOT
S_W = S_THR + TT


def build_tower(nc, patches, w_patch, consts, half_w, rows, cols, b1t, b2n, scan_w, w1q, w2q, f1, f2, out):
    fp32 = mybir.dt.float32
    ALU = mybir.AluOpType
    ACT = mybir.ActivationFunctionType
    AX = mybir.AxisListType.X
    ds = bass.ds
    MULT, ADD, SUB, MAX = ALU.mult, ALU.add, ALU.subtract, ALU.max

    ctx = ExitStack()
    with ctx:
        def sb(name, shape, dt=fp32):
            return ctx.enter_context(nc.sbuf_tensor(name, shape, dt))

        def sem(name):
            return ctx.enter_context(nc.semaphore(name))

        ring = [sb(f"ring{s}", [128, 2 * QUAD * KF * D]) for s in range(RING)]
        W1N = QUAD * KF * D
        w1s = [r[:, 0:W1N].rearrange("p (a c f) -> p a c f", a=2, c=3) for r in ring]
        w2s = [r[:, W1N:2 * W1N].rearrange("p (q k d) -> p q k d", q=QUAD, k=KF) for r in ring]
        cst = sb("cst", [128, C_W])
        ident = cst[:, C_ID:C_ID + 128]
        hw = sb("hw", [128, 2, W_W])
        row = sb("row", [128, 5, D])
        col = sb("col", [128, K_W])
        b1 = sb("b1", [128, NQ, NFT, 8])
        b2 = sb("b2", [128, D])
        hA = sb("hA", [PAIR, NT, D])
        ones = sb("ones", [128, 128])
        phin = sb("phin", [128, 2, NE])
        bn = sb("bn", [128, NT, 6])
        mv = sb("mv", [128, NT, 2])
        rs = [sb(f"rs{k}", [128, 64]) for k in range(5)]
        mxs = sb("mxs", [128, 4, NH])
        ar = sb("ar", [128, 10264])

        pat = ring[3][:, 0:KP * T].rearrange("p (k t) -> p k t", k=KP)
        wpa = ring[3][:, KP * T:KP * (T + D)].rearrange("p (k d) -> p k d", k=KP)

        squares = ar[:, 0:2 * NE].rearrange("p (k n) -> p k n", k=2)

        def view(first, end, pattern=None, rows_=128, **kw):
            v = ar[0:rows_, first:end]
            return v.rearrange(pattern, **kw) if pattern else v

        zdiag = [ring[0][:, 128 * n:128 * (n + 1)] for n in range(CC * TAPS)]
        xn = view(0, 1536, "p (t d) -> p t d", rows_=PAIR, t=NT)
        ysn = view(0, 1536, "p (t d) -> p t d", t=NT)
        xT = view(1536, 2688, "p (k t) -> p k t", k=2)
        TQ = T + 28
        qT = view(2688, 2688 + 2 * TQ, "p (k t) -> p k t", k=2)
        kT = view(3896, 5048, "p (k t) -> p k t", rows_=H, k=2)
        kbd = view(5048, 5912, "p (g h t) -> p g h t", g=2, h=6)
        xR = [view(5912 + 432 * n, 6344 + 432 * n, "p (k b r l) -> p k b r l", k=2, b=2, r=3) for n in range(2)]
        prob = [view(6776 + 432 * n, 7208 + 432 * n, "p (h k) -> p h k", h=NH) for n in range(2)]
        pT = view(7640, 8152, "p (g t) -> p g t", g=4)
        vbd = [view(8152 + 384 * n, 8536 + 384 * n, "p (b d) -> p b d", b=2) for n in range(2)]
        osb = view(8920, 9112)
        oT = view(9112, 10264, "p (k t) -> p k t", k=2)
        XS = view(1536, 4608, "p (a c e b) -> p a c e b", a=NE // 2, c=3, e=2)
        Lc = view(4608, 5120, "p (t n) -> p t n", rows_=PAIR, t=NT)
        Ld = view(5120, 5696, "p (b m) -> p b m", rows_=NE, b=B)
        cbd = view(6464, 7488, "p (t b n) -> p t b n", rows_=PAIR, t=NT, b=2)
        dbd = view(8192, 9216, "p (t b n) -> p t b n", rows_=PAIR, t=NT, b=2)
        cT = view(9216, 9792, "p (t m) -> p t m", t=NT)
        XSq = [view(9792 + 192 * n, 9984 + 192 * n, "p (a c m) -> p a c m", a=2, c=3) for n in range(2)]
        hs = [view(7680 + 384 * n, 8064 + 384 * n) for n in range(2)]
        hb = view(8448, 8832, "p (t g b) -> p t g b", t=NFT, g=8)
        hg = view(8832, 9216, "p (t g b) -> p t g b", t=NFT, g=8)
        ysb = view(5696, 5696 + RING * D, "p (s d) -> p s d", s=RING)
        sw = ring[1][:, 0:S_W]
        w_in = sw[:, S_IN:S_IN + 768].rearrange("p (k c d) -> p k c d", k=2, c=2 * CC)
        w_xp = sw[:, S_XP:S_XP + 264].rearrange("p (c e) -> p c e", c=CC)
        w_dt = sw[:, S_DT:S_DT + 384].rearrange("p (c d) -> p c d", c=CC)
        w_so = sw[:, S_OUT:S_OUT + 2 * CC * D].rearrange("p (c d) -> p c d", c=2 * CC)
        o1 = [S_W]

        def slot1(n, p=128):
            o1[0] += n
            return ring[1][0:p, o1[0] - n:o1[0]]

        u = slot1(CC * TH).rearrange("p (c b l) -> p c b l", c=CC, b=HALF)
        du = slot1(CC * TH).rearrange("p (c t) -> p c t", c=CC)
        delta = slot1(CC * TH).rearrange("p (c t) -> p c t", c=CC)
        sp = [slot1(CC * TH).rearrange("p (c t) -> p c t", c=CC) for _ in range(3)]
        xd = slot1(TH)
        negA = slot1(CC * NS)
        assert o1[0] <= 2 * W1N
        zr = view(9216, 9216 + CC * TH, "p (c b l) -> p c b l", c=CC, b=HALF)
        ybd = view(2688, 2688 + 2 * CC * TP, "p (c t) -> p c t", c=2 * CC)
        zc = view(6528, 6528 + CC * TH, "p (c b l) -> p c b l", c=CC, b=HALF)
        sel = [ring[s][:, a + 128 * n:a + 128 * (n + 1)] for s, a, m in ((0, 5376, 30), (1, o1[0], 2)) for n in range(m)]
        Bb = ring[2][:, 0:NS * TH].rearrange("p (n t) -> p n t", n=NS)
        first_norm = ring[2][:, 5120:5120 + TT * D].rearrange("p (t d) -> p t d", t=TT)
        Cb = ring[2][:, NS * TH:2 * NS * TH].rearrange("p (n t) -> p n t", n=NS)
        GW = NG * TH
        dA = [ring[3][:, n * GW:(n + 1) * GW] for n in range(2)]
        dBu = [ring[3][:, (2 + n) * GW:(3 + n) * GW] for n in range(2)]
        hst = [ring[3][:, (4 + n) * GW:(5 + n) * GW] for n in range(2)]
        hC = [ring[3][:, (6 + n) * GW:(7 + n) * GW] for n in range(2)]
        hB = view(8256, 8256 + TT * D, "p (t d) -> p t d", t=TT)
        at = [(ring[0], 0), (ring[0], 2688), (ring[0], 5376), (ring[3], 4608)]
        f1s = [r[:, a:a + 1536].rearrange("p (k f) -> p k f", k=2) for r, a in at]
        f2s = [r[:, a + 1536:a + 2688].rearrange("p (k d) -> p k d", k=KF) for r, a in at]
        gT = [ring[3][:, n * KF * 128:(n + 1) * KF * 128].rearrange("p (f t) -> p f t", f=KF) for n in range(2)]
        tk = ring[2][:, 0:TT * D].rearrange("p (t d) -> p t d", t=TT)
        tkT = ring[2][:, 1000:1000 + 2 * TP].rearrange("p (k t) -> p k t", k=2)
        slx = [ring[2][:, 3000 + D * b:3000 + D * (b + 1)] for b in range(NB)]
        sly = [ring[2][:, 3800 + D * b:3800 + D * (b + 1)] for b in range(NB)]
        slT = [ring[2][:, 4600 + 256 * n:4600 + 256 * (n + 1)].rearrange("p (k t) -> p k t", k=2) for n in range(2)]
        yg = ring[2][:, 5120:5120 + TT * TOPK * D].rearrange("p (t k d) -> p t k d", t=TT, k=TOPK)
        rt = [ring[2][:, 2400 + 40 * n:2440 + 40 * n].rearrange("p (t e) -> p t e", t=TT) for n in range(8)]
        ridx = sb("ridx", [128, TT, 8], mybir.dt.uint32)
        chosen_sum = ring[2][:, 2950:2950 + NX]
        tiles_of, tiles_to, first_tile = (ring[2][:, 2720 + NX * n:2720 + NX * (n + 1)] for n in range(3))
        place_f = [ring[2][:, 2744 + TT * n:2744 + TT * (n + 1)] for n in range(TOPK)]
        place = ring[2][:, 2760:2760 + TOPK * TT].bitcast(mybir.dt.uint32).rearrange("p (k t) -> p k t", k=TOPK)
        slot_cmp = ring[2][0:1, 2780:2780 + NSLOT * NX].rearrange("p (s e) -> p s e", s=NSLOT)
        slot_f = ring[2][0:1, 2910:2910 + NSLOT]
        slot_expert = ring[2][0:1, 2930:2930 + NSLOT].bitcast(mybir.dt.uint32)
        tri = ring[1][:, S_TRI:S_TRI + 128]
        slot_no = ring[1][0:1, S_SLOT:S_SLOT + NSLOT]
        thresholds = ring[1][:, S_THR:S_THR + TT]

        ps = [ctx.enter_context(nc.psum_tensor(f"ps{k}", [128, 512], fp32)) for k in range(8)]

        patch_loaded = [sem(f"patch_loaded{k}") for k in range(3)]
        cst_loaded, hw_loaded, row_loaded, col_loaded = map(sem, ("cst_loaded", "hw_loaded", "row_loaded", "col_loaded"))
        padded, xT_padded, xd_padded, tkT_padded, sel_ready = map(sem, ("padded", "xT_padded", "xd_padded", "tkT_padded", "sel_ready"))
        bias_loaded, scan_w_loaded = sem("bias_loaded"), sem("scan_w_loaded")
        w1_loaded = [sem(f"w1_loaded{s}") for s in range(RING)]
        w2_loaded = [sem(f"w2_loaded{s}") for s in range(RING)]
        ys_stored = [sem(f"ys_stored{s}") for s in range(RING)]
        f1_loaded = [sem(f"f1_loaded{s}") for s in range(NB)]
        f2_loaded = [sem(f"f2_loaded{s}") for s in range(NB)]
        slx_loaded = [sem(f"slx_loaded{s}") for s in range(NB)]
        rows_gathered = [sem(f"rows_gathered{t}") for t in range(TT)]
        sly_stored = [sem(f"sly_stored{s}") for s in range(NB)]
        ys_moved, resid_moved, out_stored = map(sem, ("ys_moved", "resid_moved", "out_stored"))
        (dve_step, act_step, pool_step, embedded, xn_ready, x_turned, xT_ready) = map(sem, (
            "dve_step", "act_step", "pool_step", "embedded", "xn_ready", "x_turned", "xT_ready"))
        (qk_done, qk_saved, xR_ready, kbd_ready, v_done, vbd_ready, scores_done, shifted, exp_done, p_turned, pT_ready,
         av_done, o_ready, o_turned, oT_ready, y_done, an_ready, h1_ready) = map(sem, (
            "qk_done", "qk_saved", "xR_ready", "kbd_ready", "v_done", "vbd_ready", "scores_done", "shifted", "exp_done",
            "p_turned", "pT_ready", "av_done", "o_ready", "o_turned", "oT_ready", "y_done", "an_ready", "h1_ready"))
        (phi_loaded, tokens_added, phi_sq, phi_sum, phi_sum_read, phi_ready, ld_done, lc_done, sm_shift, sm_exp, d_ready, d_turned, dbd_ready, c_ready,
         c_turned, cT_ready, xs_done, xs_zero, xs_ready) = map(sem, (
            "phi_loaded", "tokens_added", "phi_sq", "phi_sum", "phi_sum_read", "phi_ready", "ld_done", "lc_done", "sm_shift", "sm_exp", "d_ready", "d_turned",
            "dbd_ready", "c_ready", "c_turned", "cT_ready", "xs_done", "xs_zero", "xs_ready"))
        (xsq_ready, h_done, h_saved, h_turned, b1_added, gelu_done, ys_done, ys_ready, comb_done, hA_ready) = map(sem, (
            "xsq_ready", "h_done", "h_saved", "h_turned", "b1_added", "gelu_done", "ys_done", "ys_ready",
            "comb_done", "hA_ready"))
        (in_done, z_saved, conv_ready, diag_ready, zconv_done, zc_saved, u_ready, xd_done, xd_saved, dt_done, sp_t, sp_act, e_ready, ln_ready, bc_done,
         bc_saved, dA_zeroed, negA_ready, delta_ready, dA_ready, dBu_ready, scan_done, h_used, hC_ready, z_ready, ybd_zero, yb_ready,
         so_done) = map(sem, (
            "in_done", "z_saved", "conv_ready", "diag_ready", "zconv_done", "zc_saved", "u_ready", "xd_done", "xd_saved", "dt_done", "sp_t",
            "sp_act", "e_ready", "ln_ready", "bc_done", "bc_saved", "dA_zeroed", "negA_ready", "delta_ready", "dA_ready", "dBu_ready", "scan_done", "h_used", "hC_ready",
            "z_ready", "ybd_zero", "yb_ready", "so_done"))
        (hB_pad, h3_added, tk0_ready, tk_turned, tkT_ready, logit_done, rt_shift, rt_exp, chosen, ranked, slots_known, places_ready,
         rows_filled, rows_scattered, slx_turned, slT_ready, up_done, silu_done, down_done, sly_ready,
         token_done, routed_padded) = map(sem, (
            "hB_pad", "h3_added", "tk0_ready", "tk_turned", "tkT_ready", "logit_done", "rt_shift", "rt_exp", "chosen", "ranked", "slots_known",
            "places_ready", "rows_filled", "rows_scattered", "slx_turned", "slT_ready", "up_done", "silu_done", "down_done",
            "sly_ready", "token_done", "routed_padded"))

        ys_dram = nc.dram_tensor("ys_dram", (NE, B, D), fp32, kind="Internal").ap()
        slots_in = nc.dram_tensor("slots_in", (NSLOT * 128, D), fp32, kind="Internal").ap()
        slots_out = nc.dram_tensor("slots_out", (NSLOT * 128, D), fp32, kind="Internal").ap()
        NUNIT = (NS // NG) * CC
        PADS = 8
        SO = (0, 1, 2, 6, 7)
        def y_tile(t):
            return ps[(6, 7, 0, 1)[t // 2]][0:PAIR, t % 2 * D:(t % 2 + 1) * D]

        XS_PARTS = ((0, 0, 128, 0, 0), (1, 0, 64, 128, 0), (2, 0, 128, 0, 1), (1, 64, 64, 128, 1))
        XS_BANKS = ((4, 5), (6, 7))

        def slot_inputs(half, n):
            c, p0, m, _, e = XS_PARTS[n]
            bs = slice(half * HALF, (half + 1) * HALF)
            if c == 1:
                src = ps[XS_BANKS[half][1]][p0:p0 + m, 0:4 * NE].rearrange("p (b a) -> p b a", b=HALF)
            else:
                src = ps[XS_BANKS[half][0]][:, e:8 * NE:2].rearrange("p (b a) -> p b a", b=HALF)
            return XS[p0:p0 + m, :, c, e, bs].rearrange("p a b -> p b a"), src

        block = ctx.enter_context(nc.Block())

        @block.sync
        def _(sp_):
            for k in range(3):
                sp_.dma_start(wpa[:, 2 * k:2 * k + 2, :], w_patch[:, 2 * k:2 * k + 2, :]).then_inc(patch_loaded[k], 16)
                sp_.dma_start(pat[:, 2 * k:2 * k + 2, :], patches[:, 2 * k:2 * k + 2, :]).then_inc(patch_loaded[k], 16)
            sp_.dma_start(row[:, :, :], rows).then_inc(row_loaded, 16)
            sp_.dma_start(hw[:, :, :], half_w).then_inc(hw_loaded, 16)
            sp_.dma_start(b1[:, :, :, :], b1t).then_inc(bias_loaded, 16)
            sp_.dma_start(b2[:, :], b2n).then_inc(bias_loaded, 16)

            def load_quad(s, quad):
                sp_.dma_start(ring[s][:, 0:W1N], w1q[quad, :, :]).then_inc(w1_loaded[s], 16)
                sp_.dma_start(ring[s][:, W1N:2 * W1N], w2q[quad, :, :]).then_inc(w2_loaded[s], 16)

            def store_ys(s, quad):
                sp_.wait_ge(ys_ready, quad + 1)
                for q in range(QUAD):
                    p0 = 32 * q + B * (q % 2)
                    sp_.dma_start(ys_dram[ds(QUAD * quad + q, 1), :, :].rearrange("a b d -> (a b) d"), ysb[p0:p0 + B, s, :]).then_inc(ys_stored[s], 16)

            def load_ys(n0, n1):
                for s in range(RING):
                    sp_.wait_ge(ys_stored[s], 16 * n1 // RING)
                for odd in range(2):
                    sp_.dma_start(ysn[64 * odd + n0:64 * odd + n1, :, :], ys_dram[n0:n1, odd:B:2, :]).then_inc(ys_moved, 16)

            for s in range(RING):
                if s == RING - 1:
                    sp_.wait_ge(embedded, NT)
                load_quad(s, s)
            sp_.wait_ge(padded, 1)
            sp_.dma_start(slots_in.rearrange("(p a) d -> p (a d)", p=128).rearrange("p (k n) -> p k n", n=128),
                          ones[:, :].rearrange("p (a n) -> p a n", a=1).to_broadcast([128, NSLOT * D // 128, 128])).then_inc(rows_filled, 16)
            with sp_.Fori(0, ROUNDS - 1) as r:
                for s in range(RING):
                    sp_.wait_ge(h_done, RING * r + s + 1)
                    sp_.dma_start(ring[s][:, 0:W1N], w1q[ds(RING * r + (RING + s), 1), :, :].rearrange("a p n -> (a p) n")).then_inc(w1_loaded[s], 16)
                    sp_.wait_ge(ys_done, RING * r + s + 1)
                    sp_.dma_start(ring[s][:, W1N:2 * W1N], w2q[ds(RING * r + (RING + s), 1), :, :].rearrange("a p n -> (a p) n")).then_inc(w2_loaded[s], 16)
                    store_ys(s, RING * r + s)
            store_ys(0, NQ - 4)
            store_ys(1, NQ - 3)
            sp_.wait_ge(ys_done, NQ - 2)
            sp_.dma_start(ring[1][:, 0:S_W], scan_w).then_inc(scan_w_loaded, 16)
            load_ys(0, NE - QUAD * RING)
            store_ys(2, NQ - 2)
            store_ys(3, NQ - 1)
            load_ys(NE - QUAD * RING, NE)
            sp_.wait_ge(hA_ready, 2)
            n = 0
            for t in range(NT):
                a, end = PAIR * t, PAIR * (t + 1)
                while a < end:
                    m = min(end, (a // 128 + 1) * 128) - a
                    sp_.dma_start(hB[a % 128:a % 128 + m, a // 128, :], hA[a - PAIR * t:a - PAIR * t + m, t, :]).then_inc(resid_moved, 16)
                    a += m
                    n += 1
            def load_weights(b, slot):
                e = sp_.value_load(slot_expert[0:1, ds(slot, 1)], min_val=0, max_val=NX - 1)
                yield sp_.dma_start(f1s[b][0:H], f1[ds(e, 1), :, :, :].rearrange("a p k n -> (a p) k n")).then_inc(f1_loaded[b], 16)
                yield sp_.dma_start(f2s[b], f2[ds(e, 1), :, :, :].rearrange("a p k n -> (a p) k n")).then_inc(f2_loaded[b], 16)

            def load_tokens(b, slot):
                sp_.dma_start(slx[b], slots_in[ds(128 * slot, 128), :]).then_inc(slx_loaded[b], 16)

            def store_outputs(b, slot):
                sp_.wait_ge(sly_ready, slot + 1)
                sp_.dma_start(slots_out[ds(128 * slot, 128), :], sly[b]).then_inc(sly_stored[b], 16)

            sp_.wait_ge(slots_known, 1)
            for b in range(2):
                for _ in load_weights(b, b):
                    pass
            sp_.wait_ge(rows_scattered, 16 * TOPK * TT)
            for b in range(NB):
                load_tokens(b, b)
            for b in range(2, NB):
                for _ in load_weights(b, b):
                    pass
            with sp_.Fori(0, NSLOT // NB - 1) as r:
                for b in range(NB):
                    slot = NB * r + b
                    sp_.wait_ge(up_done, 2 * slot + 2)
                    load_tokens(b, slot + NB)
                    layers = load_weights(b, slot + NB)
                    next(layers)
                    sp_.wait_ge(down_done, slot + 1)
                    next(layers)
                    store_outputs(b, slot)
            for b in range(NB):
                store_outputs(b, NSLOT - NB + b)
            for t in range(TT):
                m = 128 if t < TT - 1 else LAST
                sp_.wait_ge(token_done, t + 1)
                sp_.dma_start(out[128 * t:128 * t + m, :], hB[0:m, t, :]).then_inc(out_stored, 16)
            sp_.wait_ge(out_stored, 16 * TT)

        NMOVE = 0
        for t in range(NT):
            a, end = PAIR * t, PAIR * (t + 1)
            while a < end:
                a += min(end, (a // 128 + 1) * 128) - a
                NMOVE += 1
        YMOVE = 4

        @block.gpsimd
        def _(gp):
            gp.memset(ones[:, :], 1.0).then_inc(padded, 1)
            gp.wait_ge(padded, 1)
            for first, end, value in ((1536, 3896, 1.0), (9112, 10264, 1.0), (5048, 5912, 0.0), (5912, 6776, 1.0), (7640, 8152, 1.0), (8152, 8920, 0.0)):
                gp.memset(ar[96:128, first:end], value).then_inc(padded, 1)
            gp.wait_ge(padded, PADS - 1)
            gp.memset(qT[0:H, :, T:TQ], 0.0).then_inc(padded, 1)
            gp.wait_ge(padded, PADS)
            gp.wait_ge(cst_loaded, 16)
            steps = 0

            def pool_link(ins):
                nonlocal steps
                ins.then_inc(pool_step, 1)
                steps += 1
                gp.wait_ge(pool_step, steps)

            def add_attention(g):
                two = slice(2 * g, 2 * g + 2)
                gp.wait_ge(an_ready, g // 2 + 1)
                pool_link(nc.gpsimd.tensor_tensor(xn[:, two, :], xn[:, two, :], row[0:PAIR, R_LG:R_LG + 1, :].to_broadcast([PAIR, 2, D]), MULT))
                pool_link(nc.gpsimd.tensor_tensor(xn[:, two, :], xn[:, two, :], row[0:PAIR, R_LB:R_LB + 1, :].to_broadcast([PAIR, 2, D]), ADD))
                nc.gpsimd.tensor_tensor(hA[:, two, :], hA[:, two, :], xn[:, two, :], ADD).then_inc(h1_ready, 1)

            gp.wait_ge(qk_saved, 8)
            for t in range(NT):
                if t >= 1:
                    gp.wait_ge(scores_done, t)
                for g in range(2):
                    ins = nc.gpsimd.tensor_tensor(
                        kbd[0:H, g, :, :],
                        kT[:, g:g + 1, PAIR * t:PAIR * (t + 1)].to_broadcast([H, 6, PAIR]),
                        cst[0:H, C_HEAD:C_HEAD + 6].rearrange("p (h a) -> p h a", a=1).to_broadcast([H, 6, PAIR]), MULT)
                ins.then_inc(kbd_ready, 1)
            for g in range(NT // 2):
                add_attention(g)
            gp.wait_ge(scores_done, NT)
            gp.wait_ge(h1_ready, NT // 2)
            gp.memset(ar[:, 2688:4608], 0.0).then_inc(xs_zero, 1)
            gp.wait_ge(lc_done, 2)
            gp.memset(ar[:, 1536:2688], 0.0).then_inc(xs_zero, 1)
            gp.wait_ge(xs_ready, 8)
            gp.tensor_copy(XSq[0], XS[:, 0:2, :, :, :].rearrange("p a c e b -> p a c (e b)")).then_inc(xsq_ready, 1)
            gp.tensor_copy(XSq[1], XS[:, 2:4, :, :, :].rearrange("p a c e b -> p a c (e b)")).then_inc(xsq_ready, 1)
            with gp.Fori(0, (NQ - 2) // 2) as r:
                for s in range(2):
                    gp.wait_ge(h_done, 2 * r + s + 1)
                    gp.tensor_copy(XSq[s], XS[:, ds(4 * r + (4 + 2 * s), 2), :, :, :].rearrange("p a c e b -> p a c (e b)")).then_inc(xsq_ready, 1)
            gp.wait_ge(xsq_ready, NQ)
            gp.memset(ar[96:128, 1536:2688], 1.0).then_inc(xT_padded, 1)
            gp.wait_ge(xT_padded, 1)
            for n in range(2 * NS):
                if n in (0, 30):
                    gp.wait_ge(ys_done, NQ - 3 if n == 0 else NQ - 2)
                e = DTR + (n % 2) * NS + n // 2
                ins = nc.gpsimd.tensor_copy(sel[n].rearrange("p (b d) -> p b d", b=2), ident[:, e:XD + e + 1:XD].rearrange("p (b a) -> p b a", a=1).to_broadcast([128, 2, 64]))
            ins.then_inc(sel_ready, 1)
            gp.wait_ge(sel_ready, 1)
            gp.memset(xd[64:128], 1.0).then_inc(xd_padded, 1)
            gp.wait_ge(xd_padded, 1)
            gp.wait_ge(comb_done, NT)
            gp.memset(hB[LAST:128, TT - 1, :], 0.0).then_inc(hB_pad, 1)
            gp.wait_ge(hB_pad, 1)
            gp.memset(ybd[:, :, :], 0.0).then_inc(ybd_zero, 1)
            gp.wait_ge(ybd_zero, 1)
            for n in range(2):
                gp.memset(dA[n].rearrange("p (g l) -> p g l", l=L)[:, :, 0:1], 0.0).then_inc(dA_zeroed, 1)
            gp.wait_ge(yb_ready, CC)
            for b in range(NB - 1):
                gp.memset(f1s[b][96:128], 0.0).then_inc(routed_padded, 1)
            gp.memset(tkT[96:128, :, :], 1.0).then_inc(tkT_padded, 1)
            gp.memset(f1s[NB - 1][96:128], 0.0).then_inc(routed_padded, 1)
            for n in range(2):
                gp.memset(slT[n][96:128], 1.0).then_inc(routed_padded, 1)

            def each_choice():
                for t in range(TT):
                    m = 128 if t < TT - 1 else LAST
                    for k in range(TOPK):
                        yield t, k, m, bass.IndirectOffsetOnAxis(ap=place[0:m, k, t:t + 1], axis=0)

            gp.wait_ge(rows_filled, 16)
            gp.wait_ge(places_ready, 1)
            for t, k, m, where in each_choice():
                gp.indirect_dma_start(out=slots_in, out_offset=where, in_=tk[0:m, t, :], in_offset=None).then_inc(rows_scattered, 16)
            for b in range(NB):
                gp.wait_ge(sly_stored[b], 16 * NSLOT // NB)
            for t, k, m, where in each_choice():
                gp.indirect_dma_start(out=yg[0:m, t, k, :], out_offset=None, in_=slots_out, in_offset=where).then_inc(rows_gathered[t], 16)

        @block.scalar
        def _(act):
            A = nc.scalar.activation
            phis = slice(W_PHI, W_PHI + NE)
            act.dma_start(phin[:, :, :], half_w[:, :, phis]).then_inc(phi_loaded, 16)
            act.dma_start(col[:, :], cols).then_inc(col_loaded, 16)
            act.dma_start(cst[:, :], consts).then_inc(cst_loaded, 16)
            act.wait_ge(padded, 1)
            A(rs[1][:, 0:1], ones[:, 0:1], ACT.Exp)
            def save_turned(n0, tiles):
                for t in tiles:
                    act.wait_ge(x_turned, n0 + t + 1)
                    A(xT[0:H, :, PAIR * t:PAIR * (t + 1)], ps[t][0:H, 0:2 * PAIR].rearrange("p (k t) -> p k t", k=2), ACT.Copy).then_inc(xT_ready, 1)

            def triple(t):
                if t >= 2:
                    act.wait_ge(v_done, t - 1)
                for k in range(2):
                    ins = A(xR[t % 2][0:H, k, :, :, :], xT[0:H, k, PAIR * t:PAIR * (t + 1)].rearrange("p (b a l) -> p b a l", b=2, a=1).to_broadcast([H, 2, 3, L]), ACT.Copy)
                ins.then_inc(xR_ready, 1)

            act.wait_ge(padded, PADS)
            for half in range(2):
                save_turned(0, range(4 * half, 4 * half + 4))
                for c in (0, 2):
                    n = 4 * half + c
                    act.wait_ge(qk_done, n + 1)
                    A((qT if c < 2 else kT)[0:H, c % 2, half * TH:(half + 1) * TH], ps[n][0:H, 0:TH], ACT.Copy).then_inc(qk_saved, 1)
            act.wait_ge(xT_ready, NT)
            triple(0)
            for i in range(NT + 2):
                if 1 <= i <= NT:
                    t = i - 1
                    act.wait_ge(p_turned, t + 1)
                    if t >= 1:
                        act.wait_ge(av_done, t)
                    A(pT[0:3 * L], ps[2][0:3 * L, :].rearrange("p (g t) -> p g t", g=4), ACT.Copy).then_inc(pT_ready, 1)
                if i + 1 < NT:
                    triple(i + 1)
                if 2 <= i < NT + 2:
                    t = i - 2
                    act.wait_ge(o_turned, t + 1)
                    A(oT[0:H, :, PAIR * t:PAIR * (t + 1)].rearrange("p k (b l) -> p k b l", b=2),
                      ps[5][0:H, 0:256].rearrange("p (k b l) -> p k b l", k=2, b=2)[:, :, :, 0:L], ACT.Copy).then_inc(oT_ready, 1)
                if i < NT:
                    act.wait_ge(shifted, i + 1)
                    A(prob[i % 2], prob[i % 2], ACT.Exp, scale=HD ** -0.5).then_inc(exp_done, 1)
            save_turned(NT, range(NT))
            for half in range(2):
                act.wait_ge(sm_shift, half + 1)
                bs = slice(half * HALF, (half + 1) * HALF)
                A(Ld[:, bs, :], Ld[:, bs, :], ACT.Exp).then_inc(sm_exp, 1)
            act.wait_ge(xs_zero, 2)
            for half in range(2):
                act.wait_ge(xs_done, 2 * half + 1)
                for n in (0, 2):
                    dst, src = slot_inputs(half, n)
                    A(dst, src, ACT.Copy).then_inc(xs_ready, 1)
            act.wait_ge(sm_shift, 3)
            A(Lc, Lc, ACT.Exp).then_inc(sm_exp, 1)

            def hidden(r):
                for s in range(RING):
                    act.wait_ge(h_done, RING * r + s + 1)
                    A(hs[s % 2], ps[s % 2][:, 0:NFT * 128], ACT.Copy).then_inc(h_saved, 1)
                    act.wait_ge(b1_added, RING * r + s + 1)
                    A(hg, hb, ACT.Gelu).then_inc(gelu_done, 1)

            hidden(0)
            for n in range(2):
                act.wait_ge(c_turned, n + 1)
                A(cT[:, 4 * n:4 * n + 4, :], ps[6 + n][:, 0:4 * PAIR].rearrange("p (t m) -> p t m", t=4), ACT.Copy).then_inc(cT_ready, 1)
            with act.Fori(1, ROUNDS) as r:
                hidden(r)
            act.wait_ge(scan_w_loaded, 16)
            A(negA, col[:, K_AL:K_AL + CC * NS], ACT.Exp).then_inc(act_step, 1)
            save_turned(2 * NT, range(NT))

            def save_z(c):
                act.wait_ge(in_done, CC + c + 1)
                A(zr[:, c, :, :], ps[CC + c][:, 0:TH].rearrange("p (b l) -> p b l", b=HALF), ACT.Copy).then_inc(z_saved, 1)

            for c in range(CC):
                act.wait_ge(conv_ready, c + 1)
                A(u[:, c, :, :], u[:, c, :, :], ACT.Silu).then_inc(u_ready, 1)
                if c >= 1:
                    save_z(c - 1)
            act.wait_ge(xd_done, 1)
            act.wait_ge(xd_padded, 1)
            A(xd[0:2 * XD], ps[6][0:2 * XD, 0:TH], ACT.Copy).then_inc(xd_saved, 1)
            save_z(CC - 1)
            A(rs[1][:, 0:1], ones[:, 0:1], ACT.Exp)
            for c in range(CC):
                act.wait_ge(sp_t, c + 1)
                A(sp[1][:, c, :], sp[0][:, c, :], ACT.Abs).then_inc(sp_act, 1)
            act.wait_ge(sp_act, CC)
            for cs in (slice(0, 1), slice(1, CC)):
                A(sp[1][:, cs, :], sp[1][:, cs, :], ACT.Exp, scale=-1.0).then_inc(e_ready, 1)
            for n, cs in enumerate((slice(0, 1), slice(1, CC))):
                act.wait_ge(e_ready, n + 1)
                A(delta[:, cs, :], sp[1][:, cs, :], ACT.Ln, bias=1.0).then_inc(ln_ready, 1)
            bc = [0]

            def save_bc(upto):
                while bc[0] < upto:
                    n = bc[0]
                    act.wait_ge(bc_done, n + 1)
                    A((Bb if n % 2 == 0 else Cb)[:, n // 2, :], ps[6 + n % 2][:, 0:TH], ACT.Copy).then_inc(bc_saved, 1)
                    bc[0] += 1

            act.wait_ge(dA_zeroed, 2)
            act.wait_ge(negA_ready, 1)
            save_bc(2 * NG)
            act.wait_ge(delta_ready, 1)
            for k in range(NUNIT):
                g, c = k // CC, k % CC
                if k == 1:
                    for n in range(CC):
                        act.wait_ge(zconv_done, n + 1)
                        A(zc[:, n, :, :], ps[CC + n][:, 0:TH].rearrange("p (b l) -> p b l", b=HALF), ACT.Copy).then_inc(zc_saved, 1)
                    act.wait_ge(delta_ready, 2)
                if k >= 2:
                    act.wait_ge(scan_done, k - 1)
                for j in range(NG):
                    n = NG * g + j
                    dst = dA[k % 2][:, j * TH:(j + 1) * TH].rearrange("p (b l) -> p b l", b=HALF)[:, :, 1:L]
                    ins = A(dst, delta[:, c, :].rearrange("p (b l) -> p b l", b=HALF)[:, :, 1:L], ACT.Exp, scale=negA[:, CC * 0 + NS * c + n:NS * c + n + 1])
                ins.then_inc(dA_ready, 1)
                if k == NUNIT - CC:
                    act.wait_ge(ybd_zero, 1)
                    act.wait_ge(zc_saved, CC)
                    for half in range(2):
                        p0 = 64 * half
                        A(ybd[p0:p0 + 64, CC:2 * CC, half * TH:(half + 1) * TH], zc[p0:p0 + 64, :, :, :].rearrange("p c b l -> p c (b l)"), ACT.Silu).then_inc(z_ready, 1)
                if g + 1 < NS // NG:
                    save_bc(min(2 * NG * (g + 2), 2 * NG * (g + 1) + (c + 1) * 3))
            for t in range(TT):
                act.wait_ge(tk_turned, t + 1)
                for k in range(2):
                    ins = A(tkT[0:H, k, 128 * t:128 * (t + 1)], ps[t][0:H, k * 128:(k + 1) * 128], ACT.Identity, scale=col[0:H, K_FG + k:K_FG + k + 1], bias=col[0:H, K_FB + k:K_FB + k + 1])
                ins.then_inc(tkT_ready, 1)
            act.wait_ge(rt_shift, 1)
            A(rt[1], rt[0], ACT.Exp).then_inc(rt_exp, 1)

            def hidden_rows(slot, n):
                act.wait_ge(up_done, 2 * slot + 1)
                if not (isinstance(slot, int) and slot < 2):
                    act.wait_ge(down_done, slot - 1)
                A(gT[n][:, 0:4, :], ps[2 + 2 * n][:, :].rearrange("p (f t) -> p f t", f=4), ACT.Silu).then_inc(silu_done, 1)
                act.wait_ge(up_done, 2 * slot + 2)
                A(gT[n][:, 4:6, :], ps[3 + 2 * n][:, 0:256].rearrange("p (f t) -> p f t", f=2), ACT.Silu).then_inc(silu_done, 1)

            for n in range(2):
                hidden_rows(n, n)
            with act.Fori(1, NSLOT // 2) as r:
                for n in range(2):
                    hidden_rows(2 * r + n, n)

        @block.vector
        def _(dve):
            V = nc.vector
            chain = [0]

            def link(ins):
                ins.then_inc(dve_step, 1)
                chain[0] += 1
                dve.wait_ge(dve_step, chain[0])

            def rsqrt(p, n, first=0):
                z, t, y = (rs[k][0:p, first:first + n] for k in (0, 4, 3))
                link(V.tensor_scalar(y.bitcast(mybir.dt.int32), z.bitcast(mybir.dt.int32), -0.5, RSQRT_GUESS, MULT, ADD))
                for _ in range(3):
                    link(V.tensor_tensor(t, y, y, MULT))
                    link(V.scalar_tensor_tensor(out=t, in0=t, scalar=-0.5, in1=z, op0=MULT, op1=MULT))
                    link(V.scalar_tensor_tensor(out=y, in0=t, scalar=1.5, in1=y, op0=ADD, op1=MULT))

            def statistics(x, p, t0, n):
                for t in range(n):
                    ins = V.bn_stats(bn[0:p, t0 + t, :], x[t])
                link(ins)
                for t in range(n):
                    ins = V.bn_aggr(mv[0:p, t0 + t, :], bn[0:p, t0 + t, :])
                link(ins)

            def deviations(x, p, t0, n):
                statistics(x, p, t0, n)
                link(V.tensor_scalar(rs[0][0:p, t0:t0 + n], mv[0:p, t0:t0 + n, 1], LN_EPS, None, ADD))
                rsqrt(p, n, t0)

            def normalise(dst, x, p, t0, n):
                for t in range(n):
                    yield V.tensor_scalar(dst[:, t, :], x[t], mv[0:p, t0 + t, 0:1], rs[3][0:p, t0 + t:t0 + t + 1], SUB, MULT)

            def norm_in_halves(produce):
                n = NT // 2
                for half in range(2):
                    four = slice(half * n, (half + 1) * n)
                    produce(half)
                    x = [hA[:, t, :] for t in range(half * n, (half + 1) * n)]
                    deviations(x, PAIR, half * n, n)
                    for ins in normalise(xn[:, four, :], x, PAIR, half * n, n):
                        ins.then_inc(xn_ready, 1)

            def rowof(k, p=PAIR, n=NT // 2):
                return row[0:p, k:k + 1, :].to_broadcast([p, n, D])

            dve.wait_ge(phi_loaded, 16)
            V.tensor_tensor(squares, phin[:, :, :], phin[:, :, :], MULT).then_inc(phi_sq, 1)
            dve.wait_ge(phi_sum, 1)
            V.tensor_scalar(rs[0][:, 0:NE], ps[7][:, 0:NE], 1e-24, None, MAX).then_inc(phi_sum_read, 1)
            dve.wait_ge(phi_sum_read, 1)
            rsqrt(128, NE)
            dve.wait_ge(col_loaded, 16)
            link(V.tensor_scalar(rs[3][:, 0:NE], rs[3][:, 0:NE], col[:, K_SC:K_SC + 1], None, MULT))
            V.tensor_tensor(phin[:, :, :], phin[:, :, :], rs[3][:, 0:NE].rearrange("p (a n) -> p a n", a=1).to_broadcast([128, 2, NE]), MULT).then_inc(phi_ready, 1)

            dve.wait_ge(row_loaded, 16)

            def embedding(half):
                for t in range(4 * half, 4 * half + 4):
                    dve.wait_ge(embedded, t + 1)
                    ins = V.tensor_tensor(hA[:, t, :], ps[t][0:PAIR, 0:D], row[0:PAIR, R_BP, :], ADD)
                ins.then_inc(tokens_added, 1)
                dve.wait_ge(tokens_added, half + 1)

            norm_in_halves(embedding)

            def unit_rows(t0, n):
                x = [hA[:, t, :] for t in range(t0, t0 + n)]
                statistics(x, PAIR, t0, n)
                var, z = mv[0:PAIR, t0:t0 + n, 1], rs[0][0:PAIR, t0:t0 + n]
                link(V.tensor_scalar(z, var, LN_EPS, 1e-24, ADD, MULT))
                link(V.scalar_tensor_tensor(out=z, in0=var, scalar=float(D), in1=z, op0=MULT, op1=MAX))
                rsqrt(PAIR, n, t0)
                for ins in normalise(xn[:, t0:t0 + n, :], x, PAIR, t0, n):
                    ins.then_inc(xn_ready, 1)

            dve.wait_ge(padded, PADS)
            for half in range(2):
                for c in (1, 3):
                    n = 4 * half + c
                    dve.wait_ge(qk_done, n + 1)
                    V.tensor_copy((qT if c < 2 else kT)[0:H, c % 2, half * TH:(half + 1) * TH], ps[n][0:H, 0:TH]).then_inc(qk_saved, 1)
            for i in range(NT + 3):
                if i < NT:
                    dve.wait_ge(v_done, i + 1)
                    if i >= 2:
                        dve.wait_ge(av_done, i - 1)
                    V.tensor_tensor(vbd[i % 2][0:3 * L], ps[3][0:3 * L, 0:2 * D].rearrange("p (b d) -> p b d", b=2),
                                    cst[0:3 * L, C_VM:C_VM + D].rearrange("p (a d) -> p a d", a=1).to_broadcast([3 * L, 2, D]), MULT).then_inc(vbd_ready, 1)
                    dve.wait_ge(scores_done, i + 1)
                    s3 = ps[i % 2][:, 0:NH * L].rearrange("p (h k) -> p h k", h=NH)
                    link(V.tensor_reduce(mxs[:, 0, :], s3, AX, MAX))
                    if i >= 2:
                        dve.wait_ge(p_turned, i - 1)
                    V.tensor_tensor(prob[i % 2], s3, mxs[:, 0, :].rearrange("p (h a) -> p h a", a=1).to_broadcast([128, NH, L]), SUB).then_inc(shifted, 1)
                if 1 <= i <= NT:
                    t = i - 1
                    dve.wait_ge(av_done, t + 1)
                    if t >= 1:
                        dve.wait_ge(o_turned, t)
                    V.tensor_tensor(osb.rearrange("p (h d) -> p h d", h=NH), ps[4][:, 0:D].rearrange("p (h d) -> p h d", h=NH),
                                    mxs[:, 2 + t % 2, :].rearrange("p (h a) -> p h a", a=1).to_broadcast([128, NH, HD]), MULT).then_inc(o_ready, 1)
                if i < NT:
                    dve.wait_ge(exp_done, i + 1)
                    link(V.tensor_reduce(mxs[:, 1, :], prob[i % 2], AX, ADD))
                    link(V.reciprocal(mxs[:, 2 + i % 2, :], mxs[:, 1, :]))
                if i in (NT, NT + 2):
                    t0 = 2 * (i - NT)
                    dve.wait_ge(y_done, t0 + 4)
                    y4 = [y_tile(t) for t in range(t0, t0 + 4)]
                    deviations(y4, PAIR, t0, 4)
                    for ins in normalise(xn[:, t0:t0 + 4, :], y4, PAIR, t0, 4):
                        pass
                    ins.then_inc(an_ready, 1)
            for half in range(2):
                dve.wait_ge(h1_ready, 2 * half + 2)
                unit_rows(4 * half, NT // 2)

            mxd, smd = rs[0][0:NE, 0:B], rs[1][0:NE, 0:B]

            def dispatch_shift(half):
                dve.wait_ge(ld_done, half + 1)
                bs = slice(half * HALF, (half + 1) * HALF)
                l3 = ps[half][0:NE, 0:TH].rearrange("p (b m) -> p b m", b=HALF)
                link(V.tensor_reduce(mxd[:, bs], l3, AX, MAX))
                V.tensor_tensor(Ld[:, bs, :], l3, mxd[:, bs].rearrange("p (b a) -> p b a", a=1).to_broadcast([NE, HALF, L]), SUB).then_inc(sm_shift, 1)

            def dispatch_divide(half):
                dve.wait_ge(sm_exp, half + 1)
                bs = slice(half * HALF, (half + 1) * HALF)
                link(V.tensor_reduce(smd[:, bs], Ld[:, bs, :], AX, ADD))
                link(V.reciprocal(smd[:, bs], smd[:, bs]))
                V.tensor_tensor(Ld[:, bs, :], Ld[:, bs, :], smd[:, bs].rearrange("p (b a) -> p b a", a=1).to_broadcast([NE, HALF, L]), MULT).then_inc(d_ready, 1)

            def dispatch_save(half):
                dve.wait_ge(d_turned, half + 1)
                ts = slice(4 * half, 4 * half + 4)
                for b in range(2):
                    ins = V.tensor_scalar(dbd[:, ts, b, :], ps[3][0:PAIR, 4 * half * NE:4 * (half + 1) * NE].rearrange("p (t n) -> p t n", t=4), cst[0:PAIR, C_BM + b:C_BM + b + 1], None, MULT)
                ins.then_inc(dbd_ready, 1)

            dispatch_shift(0)
            dispatch_divide(0)
            dispatch_shift(1)
            dispatch_save(0)
            dispatch_divide(1)
            dispatch_save(1)
            mxc, smc = rs[2][0:PAIR, 0:NT], rs[3][0:PAIR, 0:NT]
            l3 = ps[2][0:PAIR, :].rearrange("p (t n) -> p t n", t=NT)
            dve.wait_ge(lc_done, 2)
            link(V.tensor_reduce(mxc, l3, AX, MAX))
            V.tensor_tensor(Lc, l3, mxc.rearrange("p (t a) -> p t a", a=1).to_broadcast([PAIR, NT, NE]), SUB).then_inc(sm_shift, 1)
            dve.wait_ge(xs_zero, 2)
            for half in range(2):
                dve.wait_ge(xs_done, 2 * half + 2)
                for n in (1, 3):
                    dst, src = slot_inputs(half, n)
                    V.tensor_copy(dst, src).then_inc(xs_ready, 1)
            dve.wait_ge(sm_exp, 3)
            link(V.tensor_reduce(smc, Lc, AX, ADD))
            link(V.reciprocal(smc, smc))
            link(V.tensor_tensor(Lc, Lc, smc.rearrange("p (t a) -> p t a", a=1).to_broadcast([PAIR, NT, NE]), MULT))
            for b in range(2):
                ins = V.tensor_scalar(cbd[:, :, b, :], Lc, cst[0:PAIR, C_BM + b:C_BM + b + 1], None, MULT)
            ins.then_inc(c_ready, 1)
            dve.wait_ge(bias_loaded, 32)

            def quad_steps(r):
                for s in range(RING):
                    dve.wait_ge(h_turned, RING * r + s + 1)
                    V.tensor_tensor(hb.rearrange("p t g b -> p (t g) b"), ps[2 + s % 2][:, 0:NFT * 128].rearrange("p (g b) -> p g b", b=B),
                                    b1[:, ds(RING * r + s, 1), :, :].rearrange("p a t g -> p (a t g)").rearrange("p (g a) -> p g a", a=1).to_broadcast([128, NFT * 8, B]), ADD).then_inc(b1_added, 1)
                    dve.wait_ge(ys_done, RING * r + s + 1)
                    if not (isinstance(r, int) and r == 0):
                        dve.wait_ge(ys_stored[s], 16 * QUAD * r)
                    V.tensor_copy(ysb[:, s, :], ps[4 + s % 2][:, 0:D]).then_inc(ys_ready, 1)

            quad_steps(0)
            with dve.Fori(1, ROUNDS) as r:
                quad_steps(r)
            for n in range(CC * TAPS):
                ins = V.tensor_scalar(zdiag[n], ident, col[:, K_CZ + n:K_CZ + n + 1], None, MULT)
            ins.then_inc(diag_ready, 1)

            def combined(half):
                for t in range(4 * half, 4 * half + 4):
                    dve.wait_ge(comb_done, t + 1)
                    ins = V.tensor_tensor(hA[:, t, :], ps[t][0:PAIR, 0:D], hA[:, t, :], ADD)
                ins.then_inc(hA_ready, 1)
                dve.wait_ge(hA_ready, half + 1)

            norm_in_halves(combined)
            dve.wait_ge(act_step, 1)
            V.tensor_scalar(negA, negA, -1.0, None, MULT).then_inc(negA_ready, 1)
            for c in range(CC):
                dve.wait_ge(in_done, c + 1)
                src = ps[c][:, 0:TH].rearrange("p (b l) -> p b l", b=HALF)
                w = [col[:, K_CX + TAPS * c + k:K_CX + TAPS * c + k + 1] for k in range(TAPS)]
                link(V.tensor_scalar(u[:, c, :, :], src, w[1], None, MULT))
                link(V.scalar_tensor_tensor(out=u[:, c, :, 1:L], in0=src[:, :, 0:L - 1], scalar=w[0], in1=u[:, c, :, 1:L], op0=MULT, op1=ADD))
                link(V.scalar_tensor_tensor(out=u[:, c, :, 0:L - 1], in0=src[:, :, 1:L], scalar=w[2], in1=u[:, c, :, 0:L - 1], op0=MULT, op1=ADD))
                V.scalar_tensor_tensor(out=u[:, c, :, 0:L - 2], in0=src[:, :, 2:L], scalar=w[3], in1=u[:, c, :, 0:L - 2], op0=MULT, op1=ADD).then_inc(conv_ready, 1)
            for c in range(CC):
                dve.wait_ge(dt_done, c + 1)
                bias = col[:, K_DT + c:K_DT + c + 1]
                V.tensor_scalar(sp[0][:, c, :], ps[c][:, 0:TH], bias, bias, ADD, ADD).then_inc(sp_t, 1)

            def softplus(n, cs):
                t, e, p, small, d = sp[0][:, cs, :], sp[1][:, cs, :], sp[2][:, cs, :], du[:, cs, :], delta[:, cs, :]
                dve.wait_ge(e_ready, n + 1)
                link(V.tensor_scalar(p, e, LOG1P[0], None, MULT))
                for k in LOG1P[1:]:
                    link(V.scalar_tensor_tensor(out=p, in0=p, scalar=k, in1=e, op0=ADD, op1=MULT))
                link(V.tensor_scalar(small, e, LOG1P_MAX, None, ALU.is_lt))
                dve.wait_ge(ln_ready, n + 1)
                link(V.copy_predicated(d, small.bitcast(mybir.dt.uint32), p))
                V.scalar_tensor_tensor(out=d, in0=t, scalar=0.0, in1=d, op0=MAX, op1=ADD).then_inc(delta_ready, 1)
                dve.wait_ge(delta_ready, n + 1)
                dve.wait_ge(u_ready, CC)
                link(V.tensor_tensor(small, d, u[:, cs, :, :].rearrange("p c b l -> p c (b l)"), MULT))

            softplus(0, slice(0, 1))
            softplus(1, slice(1, CC))
            def weigh_input(k):
                g, c = k // CC, k % CC
                dve.wait_ge(bc_saved, 2 * NG * (g + 1))
                V.tensor_tensor(dBu[k % 2].rearrange("p (n t) -> p n t", n=NG), Bb[:, NG * g:NG * (g + 1), :], du[:, c:c + 1, :].to_broadcast([128, NG, TH]), MULT).then_inc(dBu_ready, 1)

            weigh_input(0)
            for k in range(NUNIT):
                g = k // CC
                dve.wait_ge(dA_ready, k + 1)
                dve.wait_ge(dBu_ready, k + 1)
                V.tensor_tensor_scan(hst[k % 2], dA[k % 2], dBu[k % 2], 0.0, MULT, ADD).then_inc(scan_done, 1)
                if k + 1 < NUNIT:
                    weigh_input(k + 1)
                dve.wait_ge(scan_done, k + 1)
                if k >= 2:
                    dve.wait_ge(h_used, k - 1)
                V.tensor_tensor(hC[k % 2], hst[k % 2], Cb[:, NG * g:NG * (g + 1), :].rearrange("p n t -> p (n t)"), MULT).then_inc(hC_ready, 1)
            dve.wait_ge(ybd_zero, 1)
            for c in range(CC):
                dve.wait_ge(h_used, NUNIT - CC + c + 1)
                for half in range(2):
                    p0 = 64 * half
                    ins = V.scalar_tensor_tensor(out=ybd[p0:p0 + 64, c, half * TH:(half + 1) * TH], in0=u[p0:p0 + 64, c, :, :].rearrange("p b l -> p (b l)"),
                                                 scalar=col[p0:p0 + 64, K_D + c:K_D + c + 1], in1=ps[3 + c][p0:p0 + 64, 0:TH], op0=MULT, op1=ADD)
                ins.then_inc(yb_ready, 1)
            dve.wait_ge(resid_moved, 16 * NMOVE)
            dve.wait_ge(hB_pad, 1)
            for t in range(TT + 1):
                if t < TT:
                    dve.wait_ge(so_done, t + 1)
                    V.tensor_tensor(hB[:, t, :], ps[SO[t]][:, 0:D], hB[:, t, :], ADD).then_inc(h3_added, 1)
                if t >= 1:
                    dve.wait_ge(h3_added, t)
                    ins = V.bn_stats(bn[:, t - 1, :], hB[:, t - 1, :])
            link(ins)

            for t in range(TT):
                ins = V.bn_aggr(mv[:, t, :], bn[:, t, :])
            link(ins)
            var, z, r = mv[:, 0:TT, 1], rs[0][:, 0:TT], rs[4][:, 0:TT]
            link(V.tensor_scalar(z, var, LN_EPS, None, ADD))
            link(V.reciprocal(r, z))
            link(V.tensor_tensor(r, r, var, MULT))
            link(V.tensor_scalar(rs[0][:, TT:2 * TT], r, LN_EPS, None, ADD))
            rsqrt(128, 2 * TT)
            rs1, rs2 = rs[3][:, 0:TT], rs[3][:, TT:2 * TT]
            link(V.tensor_tensor(rs2, rs1, rs2, MULT))
            for t in range(TT):
                V.tensor_scalar(tk[:, t, :], hB[:, t, :], mv[:, t, 0:1], rs2[:, t:t + 1], SUB, MULT).then_inc(tk0_ready, 1)
            for ins in normalise(first_norm, [hB[:, t, :] for t in range(TT)], 128, 0, TT):
                pass
            link(ins)
            link(V.tensor_tensor(hB, hB, first_norm, ADD))
            dve.wait_ge(tk_turned, TT)
            for k, op in ((R_FG, MULT), (R_FB, ADD)):
                link(V.tensor_tensor(tk, tk, rowof(k, 128, TT), op))
            dve.wait_ge(logit_done, 1)
            lg = ps[5][:, 0:TT * NX].rearrange("p (t e) -> p t e", t=TT)
            m5, s5 = mxs[:, 0, 0:TT], mxs[:, 1, 0:TT]

            def wide(x, n=NX):
                return x.rearrange("p (t a) -> p t a", a=1).to_broadcast([128, TT, n])

            link(V.tensor_reduce(m5, lg, AX, MAX))
            V.tensor_tensor(rt[0], lg, wide(m5), SUB).then_inc(rt_shift, 1)
            dve.wait_ge(rt_exp, 1)
            link(V.tensor_reduce(s5, rt[1], AX, ADD))
            link(V.reciprocal(s5, s5))
            link(V.tensor_tensor(rt[1], rt[1], wide(s5), MULT))
            for t in range(TT):
                ins = V.max(rt[2][:, t, :], rt[1][:, t, :])
            link(ins)
            for t in range(TT):
                ins = V.max_index(ridx[:, t, :], rt[2][:, t, :], rt[1][:, t, :])
            link(ins)
            link(V.tensor_copy(rt[3], ridx[:, :, :]))
            top = rt[2][:, :, 0:TOPK]
            link(V.tensor_reduce(s5, top, AX, ADD))
            link(V.reciprocal(s5, s5))
            link(V.tensor_tensor(top, top, wide(s5, TOPK), MULT))
            iota = cst[:, C_IOTA:C_IOTA + NX].rearrange("p (a e) -> p a e", a=1).to_broadcast([128, TT, NX])
            for k in range(TOPK):
                ins = V.tensor_tensor(rt[4 + k], iota, rt[3][:, :, k:k + 1].to_broadcast([128, TT, NX]), ALU.is_equal)
            link(ins)
            link(V.tensor_tensor(rt[6], rt[4], rt[5], ADD))
            link(V.memset(rt[6][LAST:128, TT - 1, :], 0.0))
            V.tensor_reduce(chosen_sum, rt[6].rearrange("p t e -> p e t"), AX, ADD).then_inc(chosen, 1)
            dve.wait_ge(ranked, 1)
            count = ps[7][:, 0:NX].rearrange("p (e a) -> p e a", a=1).to_broadcast([128, NX, TT])
            over = rt[7].rearrange("p t e -> p (t e)").rearrange("p (e k) -> p e k", e=NX)
            link(V.tensor_tensor(over, count, thresholds.rearrange("p (a k) -> p a k", a=1).to_broadcast([128, NX, TT]), ALU.is_gt))
            link(V.tensor_reduce(tiles_of, over, AX, ADD))
            link(V.tensor_tensor_scan(tiles_to, ones[:, 0:NX], tiles_of, 0.0, MULT, ADD))
            link(V.tensor_tensor(slot_cmp, tiles_to[0:1].rearrange("p (a e) -> p a e", a=1).to_broadcast([1, NSLOT, NX]), slot_no.rearrange("p (s a) -> p s a", a=1).to_broadcast([1, NSLOT, NX]), ALU.is_le))
            link(V.tensor_reduce(slot_f, slot_cmp, AX, ADD))
            V.tensor_scalar(slot_expert, slot_f, float(NX - 1), None, ALU.min).then_inc(slots_known, 1)
            link(V.tensor_tensor(first_tile, tiles_to, tiles_of, SUB))
            link(V.scalar_tensor_tensor(out=rt[7], in0=first_tile.rearrange("p (a e) -> p a e", a=1).to_broadcast([128, TT, NX]), scalar=128.0,
                                        in1=ps[6][:, 0:TT * NX].rearrange("p (t e) -> p t e", t=TT), op0=MULT, op1=ADD))
            for k in range(TOPK):
                ins = V.tensor_tensor(rt[4 + k], rt[4 + k], rt[7], MULT)
            link(ins)
            for k in range(TOPK):
                ins = V.tensor_reduce(place_f[k], rt[4 + k], AX, ADD)
            link(ins)
            for k in range(TOPK):
                ins = V.tensor_copy(place[:, k, :], place_f[k])
            ins.then_inc(places_ready, 1)

            def save_tokens(slot, n):
                dve.wait_ge(slx_turned, slot + 1)
                if not (isinstance(slot, int) and slot < 2):
                    dve.wait_ge(up_done, 2 * slot - 2)
                V.tensor_copy(slT[n][0:H], ps[n][0:H, 0:256].rearrange("p (k t) -> p k t", k=2)).then_inc(slT_ready, 1)

            def save_outputs(r, b, slot):
                dve.wait_ge(down_done, slot + 1)
                if not (isinstance(r, int) and r == 0):
                    dve.wait_ge(sly_stored[b], 16 * r)
                V.tensor_copy(sly[b], ps[6 + b % 2][:, 0:D]).then_inc(sly_ready, 1)

            def routed_steps(r):
                for b in range(NB):
                    slot = NB * r + b
                    if not (isinstance(r, int) and slot + 2 >= NSLOT):
                        save_tokens(slot + 2, b % 2)
                    save_outputs(r, b, slot)

            dve.wait_ge(routed_padded, NB + 2)
            save_tokens(0, 0)
            save_tokens(1, 1)
            routed_steps(0)
            with dve.Fori(1, NSLOT // NB - 1) as r:
                routed_steps(r)
            routed_steps(NSLOT // NB - 1)
            for t in range(TT):
                p = 128 if t < TT - 1 else LAST
                dve.wait_ge(rows_gathered[t], 16 * TOPK)
                link(V.scalar_tensor_tensor(out=hB[0:p, t, :], in0=yg[0:p, t, 0, :], scalar=rt[2][0:p, t, 0:1], in1=hB[0:p, t, :], op0=MULT, op1=ADD))
                V.scalar_tensor_tensor(out=hB[0:p, t, :], in0=yg[0:p, t, 1, :], scalar=rt[2][0:p, t, 1:2], in1=hB[0:p, t, :], op0=MULT, op1=ADD).then_inc(token_done, 1)

        
        @block.tensor
        def _(pe):
            mm, tr = nc.tensor.matmul, nc.tensor.transpose

            def keep_clock(n, bank):
                for _ in range(n):
                    mm(ps[bank][:, :], ones[:, :], hw[:, 0, 0:512], start=True, stop=True)

            pe.wait_ge(padded, 1)
            pe.wait_ge(phi_sq, 1)
            for k in range(2):
                ins = mm(ps[7][:, 0:NE], ones[:, :], squares[:, k, :], start=(k == 0), stop=(k == 1))
            ins.then_inc(phi_sum, 1)
            pe.wait_ge(phi_sum_read, 1)
            for k in range(KP):
                if k % 2 == 0:
                    pe.wait_ge(patch_loaded[k // 2], 32)
                for t in range(NT):
                    ins = mm(ps[t][0:PAIR, 0:D], pat[:, k, PAIR * t:PAIR * (t + 1)], wpa[:, k, :], start=(k == 0), stop=(k == KP - 1))
                    if k == KP - 1:
                        ins.then_inc(embedded, 1)

            def turn_tokens(n0, tiles=range(NT)):
                for t in tiles:
                    pe.wait_ge(xn_ready, n0 + t + 1)
                    for k in range(2):
                        ins = tr(ps[t][0:H, k * PAIR:(k + 1) * PAIR], xn[:, t, k * H:(k + 1) * H], ident[0:PAIR, 0:PAIR])
                    ins.then_inc(x_turned, 1)

            pe.wait_ge(cst_loaded, 16)
            pe.wait_ge(hw_loaded, 16)
            pe.wait_ge(padded, PADS)
            pe.wait_ge(tokens_added, 2)
            for half in range(2):
                turn_tokens(0, range(4 * half, 4 * half + 4))
                pe.wait_ge(xT_ready, 4 * half + 4)
                for c in range(4):
                    for k in range(2):
                        ins = mm(ps[4 * half + c][0:H, 0:TH], hw[:, k, W_QKV + c * H:W_QKV + (c + 1) * H], xT[:, k, half * TH:(half + 1) * TH], start=(k == 0), stop=(k == 1))
                    ins.then_inc(qk_done, 1)
            pe.wait_ge(qk_saved, 8)
            for i in range(NT + 3):
                for t in {NT: (4, 5), NT + 1: (6,), NT + 2: (7,)}.get(i, range(i - 3, i - 2) if 3 <= i < 7 else ()):
                    pe.wait_ge(oT_ready, t + 1)
                    if t >= 4:
                        pe.wait_ge(shifted, NT - 1 + t % 4 // 2)
                    for k in range(2):
                        ins = mm(y_tile(t), oT[:, k, PAIR * t:PAIR * (t + 1)], hw[:, k, W_OUT:W_OUT + D], start=(k == 0), stop=(k == 1))
                    ins.then_inc(y_done, 1)
                if i < NT:
                    if i >= 1:
                        pe.wait_ge(vbd_ready, i)
                    pe.wait_ge(xR_ready, i + 1)
                    for b in range(2):
                        for k in range(2):
                            ins = mm(ps[3][0:3 * L, b * D:(b + 1) * D], xR[i % 2][:, k, b, :, :].rearrange("p r l -> p (r l)"), hw[:, k, W_QKV + 2 * D:W_QKV + 3 * D], start=(k == 0), stop=(k == 1))
                    ins.then_inc(v_done, 1)
                if 1 <= i <= NT:
                    t = i - 1
                    pe.wait_ge(exp_done, t + 1)
                    if t >= 1:
                        pe.wait_ge(pT_ready, t)
                    for g in range(4):
                        ins = tr(ps[2][0:3 * L, g * 128:(g + 1) * 128], prob[t % 2][:, 3 * g:3 * g + 3, :].rearrange("p h k -> p (h k)"), ident)
                    ins.then_inc(p_turned, 1)
                if i < NT:
                    pe.wait_ge(kbd_ready, i + 1)
                    if i >= 2:
                        pe.wait_ge(shifted, i - 1)
                    for b in range(2):
                        t0 = PAIR * i + L * b
                        for g in range(2):
                            ins = mm(ps[i % 2][64 * b:64 * b + 64, g * 6 * L:(g + 1) * 6 * L], qT[:, g, t0:t0 + 64], kbd[:, g, :, b * L:(b + 1) * L], start=True, stop=True)
                    ins.then_inc(scores_done, 1)
                if 1 <= i <= NT:
                    t = i - 1
                    pe.wait_ge(pT_ready, t + 1)
                    pe.wait_ge(vbd_ready, t + 1)
                    if t >= 1:
                        pe.wait_ge(o_ready, t)
                    for b in range(2):
                        for g in range(4):
                            ins = mm(ps[4][64 * b:64 * b + 64, g * 3 * HD:(g + 1) * 3 * HD], pT[:, g, 64 * b:64 * b + 64], vbd[t % 2][:, b, g * 3 * HD:(g + 1) * 3 * HD], start=True, stop=True)
                    ins.then_inc(av_done, 1)
                if 2 <= i < NT + 2:
                    t = i - 2
                    pe.wait_ge(o_ready, t + 1)
                    if t >= 1:
                        pe.wait_ge(oT_ready, t)
                    for k in range(2):
                        ins = tr(ps[5][0:H, k * 128:(k + 1) * 128], osb[:, k * H:(k + 1) * H], ident)
                    ins.then_inc(o_turned, 1)

            def slot_logits(half):
                turn_tokens(NT, range(4 * half, 4 * half + 4))
                pe.wait_ge(xT_ready, NT + 4 * half + 4)
                for k in range(2):
                    ins = mm(ps[half][0:NE, 0:TH], phin[:, k, :], xT[:, k, half * TH:(half + 1) * TH], start=(k == 0), stop=(k == 1))
                ins.then_inc(ld_done, 1)

            def token_logits(half):
                for t in range(4 * half, 4 * half + 4):
                    for k in range(2):
                        ins = mm(ps[2][0:PAIR, t * NE:(t + 1) * NE], xT[:, k, PAIR * t:PAIR * (t + 1)], phin[:, k, :], start=(k == 0), stop=(k == 1))
                ins.then_inc(lc_done, 1)

            def turn_dispatch(half):
                pe.wait_ge(d_ready, half + 1)
                for t in range(4 * half, 4 * half + 4):
                    ins = tr(ps[3][0:PAIR, t * NE:(t + 1) * NE], Ld[:, 2 * t:2 * t + 2, :].rearrange("p b m -> p (b m)"), ident[0:NE, 0:NE])
                ins.then_inc(d_turned, 1)

            def dispatch(half):
                pe.wait_ge(dbd_ready, half + 1)
                both, last = (ps[b] for b in XS_BANKS[half])
                for t in range(4 * half, 4 * half + 4):
                    ins = mm(both[:, (t % 4) * 2 * NE:(t % 4 + 1) * 2 * NE], xn[:, t, 0:128], dbd[:, t, :, :].rearrange("p b n -> p (b n)"), start=True, stop=True)
                ins.then_inc(xs_done, 1)
                for e in range(2):
                    for t in range(4 * half, 4 * half + 4):
                        ins = mm(last[64 * e:64 * e + 64, (t % 4) * NE:(t % 4 + 1) * NE], xn[:, t, 128:D], dbd[:, t, :, e:NE:2], start=True, stop=True)
                ins.then_inc(xs_done, 1)

            slot_logits(0)
            token_logits(0)
            keep_clock(1, 7)
            slot_logits(1)
            turn_dispatch(0)
            token_logits(1)
            dispatch(0)
            turn_dispatch(1)
            dispatch(1)
            pe.wait_ge(sm_shift, 3)
            pe.wait_ge(xs_ready, 8)

            def experts(r):
                for s in range(RING):
                    pe.wait_ge(w1_loaded[s], 16 * r + 16)
                    pe.wait_ge(xsq_ready, RING * r + s + 1)
                    for c in range(3):
                        for j in range(4):
                            a, fh = j // 2, j % 2
                            ins = mm(ps[s % 2][32 * j:32 * j + 32, 0:NFT * 128], XSq[s % 2][:, a, c, :], w1s[s][:, a, c, fh * NFT * 128:(fh + 1) * NFT * 128], start=(c == 0), stop=(c == 2))
                    ins.then_inc(h_done, 1)
                    pe.wait_ge(h_saved, RING * r + s + 1)
                    for t in range(NFT):
                        ins = tr(ps[2 + s % 2][:, t * 128:(t + 1) * 128], hs[s % 2][:, t * 128:(t + 1) * 128], ident)
                    ins.then_inc(h_turned, 1)
                    pe.wait_ge(w2_loaded[s], 16 * r + 16)
                    pe.wait_ge(gelu_done, RING * r + s + 1)
                    for fh in range(2):
                        for t in range(NFT):
                            for q in range(QUAD):
                                a = q // 2
                                g0 = 4 * a + 2 * fh
                                ins = mm(ps[4 + s % 2][32 * q:32 * q + 32, 0:D], hg[:, t, g0:g0 + 2, :].rearrange("p g b -> p (g b)"), w2s[s][:, q, fh * NFT + t, :],
                                         start=(fh == 0 and t == 0), stop=(fh == 1 and t == NFT - 1))
                    ins.then_inc(ys_done, 1)

            experts(0)
            pe.wait_ge(c_ready, 1)
            for t in range(NT):
                ins = tr(ps[6 + t // 4][:, (t % 4) * PAIR:(t % 4 + 1) * PAIR], cbd[:, t, :, :].rearrange("p b n -> p (b n)"), ident[0:PAIR, 0:PAIR])
                if t % 4 == 3:
                    ins.then_inc(c_turned, 1)
            with pe.Fori(1, ROUNDS) as r:
                experts(r)
            pe.wait_ge(ys_ready, NQ)
            pe.wait_ge(cT_ready, 2)
            for t in range(NT):
                mm(ps[t][0:PAIR, 0:D], cT[:, t, :], b2[:, :], start=True, stop=False)
            pe.wait_ge(ys_moved, 16 * YMOVE)
            for t in range(NT):
                mm(ps[t][0:PAIR, 0:D], cT[:, t, :], ysn[:, t, :], start=False, stop=True).then_inc(comb_done, 1)

            def project(c, half):
                for k in range(2):
                    ins = mm(ps[c][64 * half:64 * half + 64, 0:TH], w_in[:, k, c, :], xT[:, k, half * TH:(half + 1) * TH], start=(k == 0), stop=(k == 1))
                if half == 1:
                    ins.then_inc(in_done, 1)

            pe.wait_ge(hA_ready, 1)
            turn_tokens(2 * NT, range(4))
            pe.wait_ge(xT_padded, 1)
            pe.wait_ge(scan_w_loaded, 16)
            pe.wait_ge(xT_ready, 2 * NT + 4)
            for c in range(4):
                project(c, 0)
            pe.wait_ge(hA_ready, 2)
            turn_tokens(2 * NT, range(4, NT))
            pe.wait_ge(xT_ready, 3 * NT)
            for c in range(4):
                project(c, 1)
            for c in range(4, 2 * CC):
                for half in range(2):
                    project(c, half)
            for c in range(CC):
                keep_clock(1, 7)
                pe.wait_ge(u_ready, c + 1)
                ins = mm(ps[6][0:2 * XD, 0:TH], w_xp[:, c, :], u[:, c, :, :].rearrange("p b l -> p (b l)"), start=(c == 0), stop=(c == CC - 1))
            ins.then_inc(xd_done, 1)
            pe.wait_ge(xd_saved, 1)
            for c in range(CC):
                mm(ps[c][:, 0:TH], w_dt[:, c, :], xd, start=True, stop=True).then_inc(dt_done, 1)

            def spread(n):
                if n == 0:
                    pe.wait_ge(sel_ready, 1)
                if n >= 2:
                    pe.wait_ge(bc_saved, n - 1)
                mm(ps[6 + n % 2][:, 0:TH], sel[n], xd, start=True, stop=True).then_inc(bc_done, 1)

            for n in range(2 * NG):
                spread(n)
            sent = 2 * NG
            pe.wait_ge(diag_ready, 1)
            for c in range(CC):
                pe.wait_ge(z_saved, c + 1)
                dst = ps[CC + c][:, 0:TH].rearrange("p (b l) -> p b l", b=HALF)
                for k in (1, 0, 2, 3):
                    o = k - 1
                    a, e = max(0, -o), L - max(0, o)
                    ins = mm(dst[:, :, a:e], zdiag[TAPS * c + k], zr[:, c, :, a + o:e + o], start=(k == 1), stop=(k == TAPS - 1))
                ins.then_inc(zconv_done, 1)
            for k in range(NUNIT + 1):
                if k < NUNIT:
                    g, c = k // CC, k % CC
                    while sent < min(2 * NS, 2 * NG * (g + 1) + (c + 1) * 3):
                        spread(sent)
                        sent += 1
                if k >= 1:
                    g, c = (k - 1) // CC, (k - 1) % CC
                    if k == 1:
                        pe.wait_ge(zc_saved, CC)
                    pe.wait_ge(hC_ready, k)
                    for j in range(NG):
                        ins = mm(ps[3 + c][:, 0:TH], ident, hC[(k - 1) % 2][:, j * TH:(j + 1) * TH],
                                 start=(g == 0 and j == 0), stop=(g == NS // NG - 1 and j == NG - 1))
                    ins.then_inc(h_used, 1)
                if k == NUNIT - CC:
                    pe.wait_ge(z_ready, 2)
                    pe.wait_ge(bc_saved, 2 * NS)
                    for t in range(TT):
                        for c in range(CC, 2 * CC):
                            mm(ps[SO[t]][:, 0:D], ybd[:, c, 128 * t:128 * (t + 1)], w_so[:, c, :], start=(c == CC), stop=False)
            for c in range(CC):
                pe.wait_ge(yb_ready, c + 1)
                for t in range(TT):
                    ins = mm(ps[SO[t]][:, 0:D], ybd[:, c, 128 * t:128 * (t + 1)], w_so[:, c, :], start=False, stop=(c == CC - 1))
                    if c == CC - 1:
                        ins.then_inc(so_done, 1)

            for t in range(TT):
                pe.wait_ge(tk0_ready, t + 1)
                for k in range(2):
                    ins = tr(ps[t][0:H, k * 128:(k + 1) * 128], tk[:, t, k * H:(k + 1) * H], ident)
                ins.then_inc(tk_turned, 1)
            pe.wait_ge(tkT_ready, TT)
            pe.wait_ge(tkT_padded, 1)
            for t in range(TT):
                for k in range(2):
                    ins = mm(ps[5][:, t * NX:(t + 1) * NX], tkT[:, k, 128 * t:128 * (t + 1)], hw[:, k, W_RT:W_RT + NX], start=(k == 0), stop=(k == 1))
            ins.then_inc(logit_done, 1)

            pe.wait_ge(chosen, 1)
            all_chosen = rt[6].rearrange("p t e -> p (t e)")
            mm(ps[6][:, 0:TT * NX], tri, all_chosen, start=True, stop=False)
            for n in range(1, TT):
                mm(ps[6][:, n * NX:TT * NX], ones[:, :], all_chosen[:, 0:(TT - n) * NX], start=False, stop=(n == TT - 1))
            ins = mm(ps[7][:, 0:NX], ones[:, :], chosen_sum, start=True, stop=True)
            ins.then_inc(ranked, 1)

            def turn_slot(r, b, slot):
                pe.wait_ge(slx_loaded[b], 16 * r + 16)
                if not (isinstance(slot, int) and slot < 2):
                    pe.wait_ge(slT_ready, slot - 1)
                for k in range(2):
                    ins = tr(ps[b % 2][0:H, k * 128:(k + 1) * 128], slx[b][:, k * H:(k + 1) * H], ident)
                ins.then_inc(slx_turned, 1)

            def up(r, b, slot):
                pe.wait_ge(f1_loaded[b], 16 * r + 16)
                pe.wait_ge(slT_ready, slot + 1)
                for f in range(KF):
                    bank, c = (2, f) if f < 4 else (3, f - 4)
                    for k in range(2):
                        ins = mm(ps[bank + 2 * (b % 2)][:, c * 128:(c + 1) * 128], f1s[b][:, k, f * 128:(f + 1) * 128], slT[b % 2][:, k, :], start=(k == 0), stop=(k == 1))
                    if f in (3, KF - 1):
                        ins.then_inc(up_done, 1)

            def down(r, b, slot):
                pe.wait_ge(f2_loaded[b], 16 * r + 16)
                if not (isinstance(slot, int) and slot < 2):
                    pe.wait_ge(sly_ready, slot - 1)
                for f in range(KF):
                    if f in (0, 4):
                        pe.wait_ge(silu_done, 2 * slot + 1 + f // 4)
                    ins = mm(ps[6 + b % 2][:, 0:D], gT[b % 2][:, f, :], f2s[b][:, f, :], start=(f == 0), stop=(f == KF - 1))
                ins.then_inc(down_done, 1)

            def slot_steps(r):
                for b in range(NB):
                    slot = NB * r + b
                    last = isinstance(r, int) and r == NSLOT // NB - 1
                    for stage, ahead in ((turn_slot, 2), (up, 1)):
                        if not (last and b + ahead >= NB):
                            stage(r + (b + ahead) // NB, (b + ahead) % NB, slot + ahead)
                    down(r, b, slot)

            pe.wait_ge(places_ready, 1)
            pe.wait_ge(routed_padded, NB + 2)
            turn_slot(0, 0, 0)
            turn_slot(0, 1, 1)
            up(0, 0, 0)
            slot_steps(0)
            with pe.Fori(1, NSLOT // NB - 1) as r:
                slot_steps(r)
            slot_steps(NSLOT // NB - 1)


def layouts(x, L0_tok_W_proj, L0_tok_b_proj, L0_attn_w_qkv, L0_attn_w_out, L0_attn_b_out, L0_attn_ln_g, L0_attn_ln_b,
            L0_ffn_phi, L0_ffn_scale, L0_ffn_w1, L0_ffn_b1, L0_ffn_w2, L0_ffn_b2, L1_attn_in_proj_w, L1_attn_x_proj_w,
            L1_attn_dt_proj_w, L1_attn_dt_proj_b, L1_attn_A_log, L1_attn_D_param, L1_attn_out_proj_w, L1_attn_conv_x_w,
            L1_attn_conv_z_w, L1_ffn_ln_gamma, L1_ffn_ln_beta, L1_ffn_router_w, L1_ffn_w1, L1_ffn_w2):
    f4 = np.float32
    C = np.ascontiguousarray

    def halves(w, row=None):
        out = np.zeros((128, 2, w.shape[1]), f4)
        out[0:H] = w.reshape(2, H, -1).transpose(1, 0, 2)
        if row is not None:
            out[H, 1] = row
        return out

    patches = x.reshape(B, 3, 6, 16, 6, 16).transpose(1, 3, 5, 0, 2, 4).reshape(KP, 128, T).transpose(1, 0, 2)
    w_patch = L0_tok_W_proj.T.reshape(KP, 128, D).transpose(1, 0, 2)
    consts = np.zeros((128, C_W), f4)
    p = np.arange(128)
    consts[:, C_ID:C_ID + 128] = np.eye(128)
    consts[:, C_HEAD:C_HEAD + 6] = p[:, None] // HD == np.arange(6)
    consts[:, C_VM:C_VM + D] = p[:, None] // L == np.arange(D) // HD % 3
    consts[:, C_BM:C_BM + 2] = p[:, None] // L == np.arange(2)
    consts[:, C_IOTA:C_IOTA + NX] = np.arange(NX)
    half_w = np.concatenate([halves(L0_attn_w_qkv), halves(L0_attn_w_out, L0_attn_b_out), halves(L0_ffn_phi.reshape(D, NE)), halves(L1_ffn_router_w)], 2)
    rows = np.broadcast_to(np.stack([L0_tok_b_proj, L0_attn_ln_g, L0_attn_ln_b, L1_ffn_ln_gamma, L1_ffn_ln_beta]), (128, 5, D))

    def by_channel(w):
        w = w.reshape(CC, 64, -1).transpose(1, 0, 2).reshape(64, -1)
        return np.concatenate([w, w])

    def by_half(v):
        return halves(v[:, None])[:, :, 0]

    cols = np.concatenate([by_channel(L1_attn_conv_x_w), by_channel(L1_attn_conv_z_w), by_channel(L1_attn_D_param), by_channel(L1_attn_dt_proj_b),
                           by_channel(L1_attn_A_log), np.broadcast_to(L0_ffn_scale, (128, 1)), by_half(L1_ffn_ln_gamma), by_half(L1_ffn_ln_beta)], 1)
    b1t = L0_ffn_b1.reshape(NQ, 2, 2, 2, NFT, 128).transpose(5, 0, 4, 1, 3, 2).reshape(128, NQ, NFT, 8)
    b2n = np.concatenate([L0_ffn_b2, L0_ffn_b2])
    scan_w = np.zeros((128, S_W), f4)
    scan_w[:, S_IN:S_IN + 768] = halves(L1_attn_in_proj_w.T).reshape(128, -1)
    xp = np.zeros((2, 64, CC, 2, XD), f4)
    dt = np.zeros((2, XD, CC, 2, 64), f4)
    for half in range(2):
        xp[half, :, :, half, :] = L1_attn_x_proj_w.reshape(XD, CC, 64).transpose(2, 1, 0)
        dt[half, 0:DTR, :, half, :] = L1_attn_dt_proj_w.reshape(CC, 64, DTR).transpose(2, 0, 1)
    scan_w[:, S_XP:S_XP + 264] = xp.reshape(128, -1)
    scan_w[0:2 * XD, S_DT:S_DT + 384] = dt.reshape(2 * XD, -1)
    scan_w[:, S_OUT:S_TRI] = np.concatenate(
        [by_channel(L1_attn_out_proj_w.T[0:D]), by_channel(L1_attn_out_proj_w.T[D:2 * D])], 1)
    w1 = L0_ffn_w1.reshape(NE // 2, 2, D, FF)
    w1 = np.concatenate([w1[:, 0], w1[:, 1, 128:], w1[:, 1, :128]], 1)
    w1q = w1.reshape(NQ, 2, 3, 128, FF).transpose(0, 3, 1, 2, 4).reshape(NQ, 128, -1)
    w2q = L0_ffn_w2.reshape(NQ, QUAD, KF, 128, D).transpose(0, 3, 1, 2, 4).reshape(NQ, 128, -1)
    scan_w[:, S_TRI:S_TRI + 128] = np.triu(np.ones((128, 128)), 1)
    scan_w[:, S_SLOT:S_SLOT + NSLOT] = np.arange(NSLOT)
    scan_w[:, S_THR:S_THR + TT] = 128 * np.arange(TT)
    f1 = L1_ffn_w1.reshape(NX, 2, H, FF).transpose(0, 2, 1, 3)
    f2 = L1_ffn_w2.reshape(NX, KF, 128, D).transpose(0, 2, 1, 3)
    return dict(patches=C(patches), w_patch=C(w_patch), consts=consts, half_w=C(half_w), rows=C(rows), cols=C(cols), b1t=C(b1t), b2n=C(b2n),
                scan_w=scan_w, w1q=C(w1q), w2q=C(w2q), f1=C(f1), f2=C(f2))


def kernel(**inputs):
    import concourse.bacc as bacc
    from concourse.bass_utils import run_bass_kernel_spmd

    nc = bacc.Bacc("TRN2", target_bir_lowering=False, num_devices=1)
    arrays = layouts(**{k: np.asarray(v) for k, v in inputs.items()})
    names = {k: f"in_{k}_dram" for k in arrays}
    args = {k: nc.dram_tensor(names[k], a.shape, mybir.dt.from_np(a.dtype), kind="ExternalInput").ap() for k, a in arrays.items()}
    out = nc.dram_tensor("out_dram", (T, D), mybir.dt.float32, kind="ExternalOutput").ap()
    build_tower(nc, out=out, **args)
    r = run_bass_kernel_spmd(nc, [{names[k]: a for k, a in arrays.items()}], core_ids=[0])
    return r.results[0]["out_dram"].reshape(B, L, D)
```
